# Optimizing a Trainium2 kernel written in Bass

```python
import numpy as np
import jax
import jax.numpy as jnp

def _softmax(x, axis=-1):
    return jax.nn.softmax(x, axis=axis)

def _gelu(x):
    return jax.nn.gelu(x, approximate=True)

def _silu(x):
    return jax.nn.silu(x)

def _sigmoid(x):
    return jax.nn.sigmoid(x)

def _layernorm(x, axis=-1, eps=1e-05):
    m = jnp.mean(x, axis=axis, keepdims=True)
    v = jnp.var(x, axis=axis, keepdims=True)
    return (x - m) / jnp.sqrt(v + eps)

def _scatter_add(tgt, idx, src, axis=0):
    return tgt.at[idx].add(src)

def _segment_sum(src, seg, n):
    return jax.ops.segment_sum(src, seg, n)
kernel_name = 'mk_vit_tower_d4_tok_img1024_r4_58a3f1'

def setup_inputs(seed: int=0):
    np.random.seed(seed)
    _w = jnp.asarray

    def _rec_inputs():
        import jax
        import jax.numpy as jnp
        _rk = jax.random.key(seed)
        x = -0.000356955 + 1 * jax.random.normal(jax.random.fold_in(_rk, 1), (16, 3, 96, 96), jnp.float32)
        return x
    x = _rec_inputs()

    def _L0_tok_setup():
        import jax, jax.numpy as jnp
        import numpy as np
        PATCH = 16
        EMBED = 256
        key = jax.random.key(seed)
        kx, kw = jax.random.split(key, 2)
        x = jax.random.normal(kx, (128, 3, 224, 224), dtype=jnp.float32)
        in_feat = PATCH * PATCH * 3
        W = jax.random.normal(kw, (EMBED, in_feat), dtype=jnp.float32) * 0.02
        b = jnp.zeros((EMBED,), dtype=jnp.float32)
        return {'x': x, 'W': W, 'b': b}
    _L0_tok_all = _L0_tok_setup()
    _L0_tok_in = {k: v for k, v in _L0_tok_all.items() if k in ('W', 'b')}
    del _L0_tok_all

    def _L0_attn_setup():
        import jax, jax.numpy as jnp
        import numpy as np
        LN_EPS = 1e-05
        key = jax.random.key(seed)
        ks = jax.random.split(key, 4)
        B_, S, D = (32, 256, 256)
        return {'x': jax.random.normal(ks[0], (B_, S, D), dtype=jnp.float32), 'A': jax.random.normal(ks[1], (D, D), dtype=jnp.float32) * 0.01, 'B': jax.random.normal(ks[2], (D, D), dtype=jnp.float32) * 0.01, 'C': jax.random.normal(ks[3], (D, D), dtype=jnp.float32) * 0.01, 'gamma': jnp.ones((D,), dtype=jnp.float32), 'beta': jnp.zeros((D,), dtype=jnp.float32)}
    _L0_attn_all = _L0_attn_setup()
    _L0_attn_in = {k: v for k, v in _L0_attn_all.items() if k in ('A', 'B', 'C', 'gamma', 'beta')}
    del _L0_attn_all

    def _L0_ffn_setup():
        import jax, jax.numpy as jnp
        import numpy as np
        B, T, D, F, E = (2, 256, 256, 1024, 8)
        EPS = 1e-06
        key = jax.random.key(seed)
        k = jax.random.split(key, 5)
        scale = 0.02
        return {'x': jax.random.normal(k[0], (B, T, D), dtype=jnp.float32), 'rms_w': jnp.ones((D,), dtype=jnp.float32), 'gate_w': jax.random.normal(k[1], (E, D), dtype=jnp.float32) * scale, 'W1': jax.random.normal(k[2], (E, D, F), dtype=jnp.float32) * scale, 'b1': jnp.zeros((E, F), dtype=jnp.float32), 'W2': jax.random.normal(k[3], (E, F, D), dtype=jnp.float32) * scale, 'b2': jnp.zeros((E, D), dtype=jnp.float32)}
    _L0_ffn_all = _L0_ffn_setup()
    _L0_ffn_in = {k: v for k, v in _L0_ffn_all.items() if k in ('rms_w', 'gate_w', 'W1', 'b1', 'W2', 'b2')}
    del _L0_ffn_all

    def _L1_attn_setup():
        import jax, jax.numpy as jnp
        import numpy as np
        D_MODEL = 256
        D_STATE = 16
        LN_EPS = 1e-05
        key = jax.random.key(seed)
        ks = jax.random.split(key, 10)
        B, L, D, N = (4, 256, D_MODEL, D_STATE)
        s = lambda fan_in: 1.0 / np.sqrt(fan_in)
        x_in = jax.random.normal(ks[0], (B, L, D), dtype=jnp.float32)
        W_in = jax.random.uniform(ks[1], (D, 2 * D), jnp.float32, -s(D), s(D))
        W_x = jax.random.uniform(ks[2], (D, D + 2 * N), jnp.float32, -s(D), s(D))
        W_dt = jax.random.uniform(ks[3], (D, D), jnp.float32, -s(D), s(D))
        b_dt = jax.random.uniform(ks[4], (D,), jnp.float32, -4.0, -1.0)
        A_log = jnp.tile(jnp.log(jnp.arange(1, N + 1, dtype=jnp.float32))[None, :], (D, 1))
        D_param = jnp.ones((D,), dtype=jnp.float32)
        W_out = jax.random.uniform(ks[5], (D, D), jnp.float32, -s(D), s(D))
        ln_g = jnp.ones((D,), dtype=jnp.float32)
        ln_b = jnp.zeros((D,), dtype=jnp.float32)
        return {'x_in': x_in, 'W_in': W_in, 'W_x': W_x, 'W_dt': W_dt, 'b_dt': b_dt, 'A_log': A_log, 'D_param': D_param, 'W_out': W_out, 'ln_g': ln_g, 'ln_b': ln_b}
    _L1_attn_all = _L1_attn_setup()
    _L1_attn_in = {k: v for k, v in _L1_attn_all.items() if k in ('W_in', 'W_x', 'W_dt', 'b_dt', 'A_log', 'D_param', 'W_out', 'ln_g', 'ln_b')}
    del _L1_attn_all

    def _L1_ffn_setup():
        import jax, jax.numpy as jnp
        import numpy as np
        LN_EPS = 1e-05

        def _layernorm(x, g, b):
            m = jnp.mean(x, axis=-1, keepdims=True)
            v = jnp.mean(jnp.square(x - m), axis=-1, keepdims=True)
            return (x - m) * jax.lax.rsqrt(v + LN_EPS) * g + b
        K_TOP = 2
        key = jax.random.key(seed)
        ks = jax.random.split(key, 4)
        B, N, D, E = (8, 512, 256, 4)
        s = 0.02
        return {'x': jax.random.normal(ks[0], (B, N, D), dtype=jnp.float32), 'gate_W': jax.random.normal(ks[1], (D, E), dtype=jnp.float32) * s, 'gate_b': jnp.zeros((E,), jnp.float32), 'W1': jax.random.normal(ks[2], (E, D, D), dtype=jnp.float32) * s, 'b1': jnp.zeros((E, D), jnp.float32), 'g1': jnp.ones((E, D), jnp.float32), 'be1': jnp.zeros((E, D), jnp.float32), 'W2': jax.random.normal(ks[3], (E, D, D), dtype=jnp.float32) * s, 'b2': jnp.zeros((E, D), jnp.float32), 'g2': jnp.ones((E, D), jnp.float32), 'be2': jnp.zeros((E, D), jnp.float32)}
    _L1_ffn_all = _L1_ffn_setup()
    _L1_ffn_in = {k: v for k, v in _L1_ffn_all.items() if k in ('gate_W', 'gate_b', 'W1', 'b1', 'g1', 'be1', 'W2', 'b2', 'g2', 'be2')}
    del _L1_ffn_all

    def _L2_attn_setup():
        import jax, jax.numpy as jnp
        import numpy as np
        from jax import lax
        DIM = 256
        INNER = 512
        GROUPS = 128
        GSZ = INNER // GROUPS
        KSZ = 4
        EPS = 1e-08

        def log_g(x):
            return jnp.where(x >= 0, jnp.log(jax.nn.relu(x) + 0.5 + EPS), -jax.nn.softplus(-x) + EPS)
        key = jax.random.key(seed)
        ks = jax.random.split(key, 10)
        B, S = (4, 1024)
        std_up = float(np.sqrt(2.0 / (5 * DIM)))
        std_down = float(2.0 / 1 / np.sqrt(DIM))
        return {'x': jax.random.normal(ks[0], (B, S, DIM), jnp.float32), 'w_up': jax.random.normal(ks[1], (2 * INNER, DIM), jnp.float32) * std_up, 'b_up': jnp.zeros((2 * INNER,), jnp.float32), 'conv_w': jax.random.normal(ks[2], (INNER, 1, KSZ), jnp.float32) * 0.25, 'conv_b': jnp.zeros((INNER,), jnp.float32), 'skip': jnp.ones((INNER,), jnp.float32), 'w_f': jax.random.normal(ks[3], (GROUPS, GSZ, GSZ), jnp.float32) * 0.1, 'w_i': jax.random.normal(ks[4], (GROUPS, GSZ, GSZ), jnp.float32) * 0.1, 'w_h': jax.random.normal(ks[5], (GROUPS, GSZ, GSZ), jnp.float32) * 0.1, 'w_down': jax.random.normal(ks[6], (DIM, INNER), jnp.float32) * std_down, 'b_down': jnp.zeros((DIM,), jnp.float32)}
    _L2_attn_all = _L2_attn_setup()
    _L2_attn_in = {k: v for k, v in _L2_attn_all.items() if k in ('w_up', 'b_up', 'conv_w', 'conv_b', 'skip', 'w_f', 'w_i', 'w_h', 'w_down', 'b_down')}
    del _L2_attn_all

    def _L2_ffn_setup():
        import jax, jax.numpy as jnp
        import numpy as np
        DIM = 256
        HIDDEN = 1024
        E = 8
        K = 2

        def _ffn_hidden(h, multiple_of=64):
            h = int(2 * h / 3)
            return multiple_of * ((h + multiple_of - 1) // multiple_of)
        EXP_HID = _ffn_hidden(HIDDEN)
        SH_HID = _ffn_hidden(HIDDEN // 2)

        def _swiglu(t, a, b, c):
            return jax.nn.silu(t @ a) * (t @ c) @ b
        key = jax.random.key(seed)
        ks = jax.random.split(key, 8)

        def xavier(k, shape, fan_in, fan_out):
            lim = np.sqrt(6.0 / (fan_in + fan_out)).astype(np.float32)
            return jax.random.uniform(k, shape, jnp.float32, -lim, lim)
        return {'x': jax.random.normal(ks[0], (2, 512, DIM), jnp.float32), 'gate_w': xavier(ks[1], (E, DIM), DIM, E), 'w1': xavier(ks[2], (E, DIM, EXP_HID), DIM, EXP_HID), 'w2': xavier(ks[3], (E, EXP_HID, DIM), EXP_HID, DIM), 'w3': xavier(ks[4], (E, DIM, EXP_HID), DIM, EXP_HID), 'sw1': xavier(ks[5], (DIM, SH_HID), DIM, SH_HID), 'sw2': xavier(ks[6], (SH_HID, DIM), SH_HID, DIM), 'sw3': xavier(ks[7], (DIM, SH_HID), DIM, SH_HID)}
    _L2_ffn_all = _L2_ffn_setup()
    _L2_ffn_in = {k: v for k, v in _L2_ffn_all.items() if k in ('gate_w', 'w1', 'w2', 'w3', 'sw1', 'sw2', 'sw3')}
    del _L2_ffn_all

    def _L3_attn_setup():
        import jax, jax.numpy as jnp
        import numpy as np
        import math
        B_SZ, T, D_IN, D_OUT, N = (8, 1024, 256, 256, 128)
        RMIN, RMAX, MAX_PHASE = (0.9, 1.0, 6.283)
        key = jax.random.key(seed)
        ks = jax.random.split(key, 9)
        x = jax.random.normal(ks[0], (B_SZ, T, D_IN), dtype=jnp.float32)
        u1 = jax.random.uniform(ks[1], (N,), dtype=jnp.float32)
        u2 = jax.random.uniform(ks[2], (N,), dtype=jnp.float32)
        nu_log = jnp.log(-0.5 * jnp.log(u1 * (RMAX + RMIN) * (RMAX - RMIN) + RMIN ** 2))
        theta_log = jnp.log(MAX_PHASE * u2)
        lam_mod = jnp.exp(-jnp.exp(nu_log))
        gamma_log = jnp.log(jnp.sqrt(1.0 - jnp.square(lam_mod)))
        B_re = jax.random.normal(ks[3], (N, D_IN), dtype=jnp.float32) / math.sqrt(2 * D_IN)
        B_im = jax.random.normal(ks[4], (N, D_IN), dtype=jnp.float32) / math.sqrt(2 * D_IN)
        C_re = jax.random.normal(ks[5], (D_OUT, N), dtype=jnp.float32) / math.sqrt(N)
        C_im = jax.random.normal(ks[6], (D_OUT, N), dtype=jnp.float32) / math.sqrt(N)
        D = jax.random.normal(ks[7], (D_OUT, D_IN), dtype=jnp.float32) / math.sqrt(D_IN)
        return {'x': x, 'nu_log': nu_log, 'theta_log': theta_log, 'gamma_log': gamma_log, 'B_re': B_re, 'B_im': B_im, 'C_re': C_re, 'C_im': C_im, 'D': D}
    _L3_attn_all = _L3_attn_setup()
    _L3_attn_in = {k: v for k, v in _L3_attn_all.items() if k in ('nu_log', 'theta_log', 'gamma_log', 'B_re', 'B_im', 'C_re', 'C_im', 'D')}
    del _L3_attn_all

    def _L3_ffn_setup():
        import jax, jax.numpy as jnp
        import numpy as np
        H, I, E_ROUTED, TOP_K = (256, 704, 7, 2)
        B, S = (4, 512)

        def _expert(h, g, u, d):
            return jnp.einsum('...i,hi->...h', jax.nn.silu(h @ g.T) * (h @ u.T), d)
        key = jax.random.key(seed)
        ks = jax.random.split(key, 10)
        sc = 0.02
        return {'x': jax.random.normal(ks[0], (B, S, H), dtype=jnp.float32), 'sg': jax.random.normal(ks[1], (I, H), dtype=jnp.float32) * sc, 'su': jax.random.normal(ks[2], (I, H), dtype=jnp.float32) * sc, 'sd': jax.random.normal(ks[3], (H, I), dtype=jnp.float32) * sc, 'rg': jax.random.normal(ks[4], (E_ROUTED, I, H), dtype=jnp.float32) * sc, 'ru': jax.random.normal(ks[5], (E_ROUTED, I, H), dtype=jnp.float32) * sc, 'rd': jax.random.normal(ks[6], (E_ROUTED, H, I), dtype=jnp.float32) * sc, 'wr': jax.random.normal(ks[7], (E_ROUTED, H), dtype=jnp.float32) * sc, 'rb': jnp.zeros((E_ROUTED,), dtype=jnp.float32)}
    _L3_ffn_all = _L3_ffn_setup()
    _L3_ffn_in = {k: v for k, v in _L3_ffn_all.items() if k in ('sg', 'su', 'sd', 'rg', 'ru', 'rd', 'wr', 'rb')}
    del _L3_ffn_all
    return {'x': x, 'L0_tok_W': _L0_tok_in['W'], 'L0_tok_b': _L0_tok_in['b'], 'L0_attn_A': _L0_attn_in['A'], 'L0_attn_B': _L0_attn_in['B'], 'L0_attn_C': _L0_attn_in['C'], 'L0_attn_gamma': _L0_attn_in['gamma'], 'L0_attn_beta': _L0_attn_in['beta'], 'L0_ffn_rms_w': _L0_ffn_in['rms_w'], 'L0_ffn_gate_w': _L0_ffn_in['gate_w'], 'L0_ffn_W1': _L0_ffn_in['W1'], 'L0_ffn_b1': _L0_ffn_in['b1'], 'L0_ffn_W2': _L0_ffn_in['W2'], 'L0_ffn_b2': _L0_ffn_in['b2'], 'L1_attn_W_in': _L1_attn_in['W_in'], 'L1_attn_W_x': _L1_attn_in['W_x'], 'L1_attn_W_dt': _L1_attn_in['W_dt'], 'L1_attn_b_dt': _L1_attn_in['b_dt'], 'L1_attn_A_log': _L1_attn_in['A_log'], 'L1_attn_D_param': _L1_attn_in['D_param'], 'L1_attn_W_out': _L1_attn_in['W_out'], 'L1_attn_ln_g': _L1_attn_in['ln_g'], 'L1_attn_ln_b': _L1_attn_in['ln_b'], 'L1_ffn_gate_W': _L1_ffn_in['gate_W'], 'L1_ffn_gate_b': _L1_ffn_in['gate_b'], 'L1_ffn_W1': _L1_ffn_in['W1'], 'L1_ffn_b1': _L1_ffn_in['b1'], 'L1_ffn_g1': _L1_ffn_in['g1'], 'L1_ffn_be1': _L1_ffn_in['be1'], 'L1_ffn_W2': _L1_ffn_in['W2'], 'L1_ffn_b2': _L1_ffn_in['b2'], 'L1_ffn_g2': _L1_ffn_in['g2'], 'L1_ffn_be2': _L1_ffn_in['be2'], 'L2_attn_w_up': _L2_attn_in['w_up'], 'L2_attn_b_up': _L2_attn_in['b_up'], 'L2_attn_conv_w': _L2_attn_in['conv_w'], 'L2_attn_conv_b': _L2_attn_in['conv_b'], 'L2_attn_skip': _L2_attn_in['skip'], 'L2_attn_w_f': _L2_attn_in['w_f'], 'L2_attn_w_i': _L2_attn_in['w_i'], 'L2_attn_w_h': _L2_attn_in['w_h'], 'L2_attn_w_down': _L2_attn_in['w_down'], 'L2_attn_b_down': _L2_attn_in['b_down'], 'L2_ffn_gate_w': _L2_ffn_in['gate_w'], 'L2_ffn_w1': _L2_ffn_in['w1'], 'L2_ffn_w2': _L2_ffn_in['w2'], 'L2_ffn_w3': _L2_ffn_in['w3'], 'L2_ffn_sw1': _L2_ffn_in['sw1'], 'L2_ffn_sw2': _L2_ffn_in['sw2'], 'L2_ffn_sw3': _L2_ffn_in['sw3'], 'L3_attn_nu_log': _L3_attn_in['nu_log'], 'L3_attn_theta_log': _L3_attn_in['theta_log'], 'L3_attn_gamma_log': _L3_attn_in['gamma_log'], 'L3_attn_B_re': _L3_attn_in['B_re'], 'L3_attn_B_im': _L3_attn_in['B_im'], 'L3_attn_C_re': _L3_attn_in['C_re'], 'L3_attn_C_im': _L3_attn_in['C_im'], 'L3_attn_D': _L3_attn_in['D'], 'L3_ffn_sg': _L3_ffn_in['sg'], 'L3_ffn_su': _L3_ffn_in['su'], 'L3_ffn_sd': _L3_ffn_in['sd'], 'L3_ffn_rg': _L3_ffn_in['rg'], 'L3_ffn_ru': _L3_ffn_in['ru'], 'L3_ffn_rd': _L3_ffn_in['rd'], 'L3_ffn_wr': _L3_ffn_in['wr'], 'L3_ffn_rb': _L3_ffn_in['rb']}

def reference(x, L0_tok_W, L0_tok_b, L0_attn_A, L0_attn_B, L0_attn_C, L0_attn_gamma, L0_attn_beta, L0_ffn_rms_w, L0_ffn_gate_w, L0_ffn_W1, L0_ffn_b1, L0_ffn_W2, L0_ffn_b2, L1_attn_W_in, L1_attn_W_x, L1_attn_W_dt, L1_attn_b_dt, L1_attn_A_log, L1_attn_D_param, L1_attn_W_out, L1_attn_ln_g, L1_attn_ln_b, L1_ffn_gate_W, L1_ffn_gate_b, L1_ffn_W1, L1_ffn_b1, L1_ffn_g1, L1_ffn_be1, L1_ffn_W2, L1_ffn_b2, L1_ffn_g2, L1_ffn_be2, L2_attn_w_up, L2_attn_b_up, L2_attn_conv_w, L2_attn_conv_b, L2_attn_skip, L2_attn_w_f, L2_attn_w_i, L2_attn_w_h, L2_attn_w_down, L2_attn_b_down, L2_ffn_gate_w, L2_ffn_w1, L2_ffn_w2, L2_ffn_w3, L2_ffn_sw1, L2_ffn_sw2, L2_ffn_sw3, L3_attn_nu_log, L3_attn_theta_log, L3_attn_gamma_log, L3_attn_B_re, L3_attn_B_im, L3_attn_C_re, L3_attn_C_im, L3_attn_D, L3_ffn_sg, L3_ffn_su, L3_ffn_sd, L3_ffn_rg, L3_ffn_ru, L3_ffn_rd, L3_ffn_wr, L3_ffn_rb):
    import jax
    import jax.numpy as jnp

    def _L0_tok_ref(x, W, b):
        import jax, jax.numpy as jnp
        import numpy as np
        PATCH = 16
        EMBED = 256
        p = PATCH
        B, C, H, Wd = x.shape
        gh, gw = (H // p, Wd // p)
        patches = x.reshape(B, C, gh, p, gw, p).transpose(0, 1, 2, 4, 3, 5)
        patches = patches.reshape(B, gh * gw, p * p * C)
        return jnp.einsum('bnk,ek->bne', patches, W) + b

    def _L0_attn_ref(x, A, B, C, gamma, beta):
        import jax, jax.numpy as jnp
        import numpy as np
        LN_EPS = 1e-05
        batch, seq_len, d = x.shape
        xb = jnp.einsum('bsd,ed->sbe', x, B)

        def step(h, xb_t):
            h = jnp.tanh(h @ A.T + xb_t)
            y = h @ C.T
            return (h, y)
        h0 = jnp.zeros((batch, d), dtype=x.dtype)
        _, ys = jax.lax.scan(step, h0, xb)
        out = jnp.transpose(ys, (1, 0, 2)) + x
        mu = jnp.mean(out, axis=-1, keepdims=True)
        var = jnp.mean(jnp.square(out - mu), axis=-1, keepdims=True)
        return (out - mu) * jax.lax.rsqrt(var + LN_EPS) * gamma + beta

    def _L0_ffn_ref(x, rms_w, gate_w, W1, b1, W2, b2):
        import jax, jax.numpy as jnp
        import numpy as np
        B, T, D, F, E = (2, 256, 256, 1024, 8)
        EPS = 1e-06
        ms = jnp.mean(x * x, axis=-1, keepdims=True)
        xn = x * jax.lax.rsqrt(ms + EPS) * rms_w
        logits = jnp.einsum('btd,ed->bte', xn, gate_w)
        scores = jax.nn.softmax(logits, axis=-1)
        top1_idx = jnp.argmax(scores, axis=-1)
        top1_score = jnp.max(scores, axis=-1)
        out = jnp.zeros_like(xn)
        for e in range(E):
            h = jax.nn.silu(jnp.einsum('btd,df->btf', xn, W1[e]) + b1[e])
            ye = jnp.einsum('btf,fd->btd', h, W2[e]) + b2[e]
            out = jnp.where((top1_idx == e)[..., None], ye, out)
        return out * top1_score[..., None]

    def _L1_attn_ref(x_in, W_in, W_x, W_dt, b_dt, A_log, D_param, W_out, ln_g, ln_b):
        import jax, jax.numpy as jnp
        import numpy as np
        D_MODEL = 256
        D_STATE = 16
        LN_EPS = 1e-05
        B, L, D = x_in.shape
        N = A_log.shape[1]
        xz = x_in @ W_in
        x, z = (xz[..., :D], xz[..., D:])
        proj = x @ W_x
        delta_raw = proj[..., :D]
        B_ssm = proj[..., D:D + N]
        C_ssm = proj[..., D + N:]
        delta = jax.nn.softplus(delta_raw @ W_dt + b_dt)
        A = -jnp.exp(A_log)
        dA = jnp.exp(jnp.einsum('bld,dn->bldn', delta, A))
        dBx = jnp.einsum('bld,bln->bldn', delta * x, B_ssm)

        def step(h, inp):
            dA_t, dBx_t, C_t = inp
            h = dA_t * h + dBx_t
            y_t = jnp.einsum('bdn,bn->bd', h, C_t)
            return (h, y_t)
        h0 = jnp.zeros((B, D, N), dtype=x.dtype)
        xs = (jnp.moveaxis(dA, 1, 0), jnp.moveaxis(dBx, 1, 0), jnp.moveaxis(C_ssm, 1, 0))
        _, ys = jax.lax.scan(step, h0, xs)
        y = jnp.moveaxis(ys, 0, 1) + x * D_param
        y = y * jax.nn.silu(z) @ W_out
        res = y + x_in
        mu = jnp.mean(res, axis=-1, keepdims=True)
        var = jnp.var(res, axis=-1, keepdims=True)
        return (res - mu) * jax.lax.rsqrt(var + LN_EPS) * ln_g + ln_b

    def _L1_ffn_ref(x, gate_W, gate_b, W1, b1, g1, be1, W2, b2, g2, be2):
        import jax, jax.numpy as jnp
        import numpy as np
        LN_EPS = 1e-05

        def _layernorm(x, g, b):
            m = jnp.mean(x, axis=-1, keepdims=True)
            v = jnp.mean(jnp.square(x - m), axis=-1, keepdims=True)
            return (x - m) * jax.lax.rsqrt(v + LN_EPS) * g + b
        K_TOP = 2
        B, N, D = x.shape
        BN = B * N
        xf = x.reshape(BN, D)
        gate_scores = xf @ gate_W + gate_b
        topk_scores, topk_idx = jax.lax.top_k(gate_scores, K_TOP)
        weights = jax.nn.softmax(topk_scores, axis=-1)

        def expert(w1, bb1, gg1, bbe1, w2, bb2, gg2, bbe2):
            h = jax.nn.relu(_layernorm(xf @ w1 + bb1, gg1, bbe1))
            return _layernorm(h @ w2 + bb2, gg2, bbe2)
        all_out = jax.vmap(expert)(W1, b1, g1, be1, W2, b2, g2, be2)
        exp_out = all_out[topk_idx, jnp.arange(BN)[:, None]]
        out = jnp.sum(weights[..., None] * exp_out, axis=1)
        return (out + xf).reshape(B, N, D)

    def _L2_attn_ref(x, w_up, b_up, conv_w, conv_b, skip, w_f, w_i, w_h, w_down, b_down):
        import jax, jax.numpy as jnp
        import numpy as np
        from jax import lax
        DIM = 256
        INNER = 512
        GROUPS = 128
        GSZ = INNER // GROUPS
        KSZ = 4
        EPS = 1e-08

        def log_g(x):
            return jnp.where(x >= 0, jnp.log(jax.nn.relu(x) + 0.5 + EPS), -jax.nn.softplus(-x) + EPS)
        B, S, _ = x.shape
        x_inner = jnp.einsum('bsd,ed->bse', x, w_up) + b_up
        x_min, z = jnp.split(x_inner, 2, axis=-1)
        xc = lax.conv_general_dilated(x_min.transpose(0, 2, 1), conv_w, window_strides=(1,), padding=[(KSZ - 1, 0)], feature_group_count=INNER, dimension_numbers=('NCH', 'OIH', 'NCH'))
        xc = (xc + conv_b[None, :, None]).transpose(0, 2, 1)
        act = jax.nn.silu(xc)
        ag = act.reshape(B, S, GROUPS, GSZ)
        f_gate = jnp.einsum('bsgi,goi->bsgo', ag, w_f).reshape(B, S, INNER)
        i_gate = jnp.einsum('bsgi,goi->bsgo', ag, w_i).reshape(B, S, INNER)
        hidden = jnp.einsum('bsgi,goi->bsgo', ag, w_h).reshape(B, S, INNER)
        diff = jax.nn.softplus(-f_gate) - jax.nn.softplus(-i_gate)
        log_f = -jax.nn.softplus(diff)
        log_i = -jax.nn.softplus(-diff)
        log_tilde_h = log_g(hidden)
        a_star = jnp.cumsum(log_f + EPS, axis=1)
        log_h0_b = lax.cumlogsumexp(log_i + log_tilde_h - a_star, axis=1)
        h_t = jnp.exp(a_star + log_h0_b)
        h = h_t[:, -1:, :] + skip * act
        h = h * jax.nn.silu(z)
        out = jnp.einsum('bse,de->bsd', h, w_down) + b_down
        return out

    def _L2_ffn_ref(x, gate_w, w1, w2, w3, sw1, sw2, sw3):
        import jax, jax.numpy as jnp
        import numpy as np
        DIM = 256
        HIDDEN = 1024
        E = 8
        K = 2

        def _ffn_hidden(h, multiple_of=64):
            h = int(2 * h / 3)
            return multiple_of * ((h + multiple_of - 1) // multiple_of)
        EXP_HID = _ffn_hidden(HIDDEN)
        SH_HID = _ffn_hidden(HIDDEN // 2)

        def _swiglu(t, a, b, c):
            return jax.nn.silu(t @ a) * (t @ c) @ b
        B, S, D = x.shape
        xt = x.reshape(-1, D)
        T = xt.shape[0]
        logits = xt @ gate_w.T
        scores = jax.nn.softmax(logits, axis=-1)
        topk_w, topk_i = jax.lax.top_k(scores, K)
        comb = jnp.zeros((T, E), x.dtype).at[jnp.arange(T)[:, None], topk_i].add(topk_w)
        y = jnp.zeros_like(xt)
        for e in range(E):
            y = y + comb[:, e:e + 1] * _swiglu(xt, w1[e], w2[e], w3[e])
        y = y.reshape(B, S, D)
        return y + _swiglu(x, sw1, sw2, sw3)

    def _L3_attn_ref(x, nu_log, theta_log, gamma_log, B_re, B_im, C_re, C_im, D):
        import jax, jax.numpy as jnp
        import numpy as np
        import math
        B_SZ, T, D_IN, D_OUT, N = (8, 1024, 256, 256, 128)
        RMIN, RMAX, MAX_PHASE = (0.9, 1.0, 6.283)
        lam = jnp.exp(-jnp.exp(nu_log) + 1j * jnp.exp(theta_log))
        gamma = jnp.exp(gamma_log)
        Bmat = B_re + 1j * B_im
        Bu = jnp.einsum('bti,ni->btn', x.astype(Bmat.dtype), Bmat) * gamma
        A = jnp.broadcast_to(lam, Bu.shape)

        def combine(e1, e2):
            a1, b1 = e1
            a2, b2 = e2
            return (a1 * a2, a2 * b1 + b2)
        _, states = jax.lax.associative_scan(combine, (A, Bu), axis=1)
        Cmat = C_re + 1j * C_im
        y = jnp.einsum('btn,on->bto', states, Cmat).real + jnp.einsum('bti,oi->bto', x, D)
        return y

    def _L3_ffn_ref(x, sg, su, sd, rg, ru, rd, wr, rb):
        import jax, jax.numpy as jnp
        import numpy as np
        H, I, E_ROUTED, TOP_K = (256, 704, 7, 2)
        B, S = (4, 512)

        def _expert(h, g, u, d):
            return jnp.einsum('...i,hi->...h', jax.nn.silu(h @ g.T) * (h @ u.T), d)
        shared_out = _expert(x, sg, su, sd)
        logits = x @ wr.T + rb
        probs = jax.nn.softmax(logits, axis=-1)
        scores, idx = jax.lax.top_k(probs, TOP_K)
        scores = scores / scores.sum(axis=-1, keepdims=True)
        w = jnp.sum(scores[..., None] * jax.nn.one_hot(idx, E_ROUTED, dtype=x.dtype), axis=-2)
        out = shared_out
        for e in range(E_ROUTED):
            out = out + w[..., e:e + 1] * _expert(x, rg[e], ru[e], rd[e])
        return out
    h = _L0_tok_ref(x, L0_tok_W, L0_tok_b)
    h = h + _L0_attn_ref(_layernorm(h, axis=-1), L0_attn_A, L0_attn_B, L0_attn_C, L0_attn_gamma, L0_attn_beta)
    h = h + _L0_ffn_ref(_layernorm(h, axis=-1), L0_ffn_rms_w, L0_ffn_gate_w, L0_ffn_W1, L0_ffn_b1, L0_ffn_W2, L0_ffn_b2)
    h = h + _L1_attn_ref(_layernorm(h, axis=-1), L1_attn_W_in, L1_attn_W_x, L1_attn_W_dt, L1_attn_b_dt, L1_attn_A_log, L1_attn_D_param, L1_attn_W_out, L1_attn_ln_g, L1_attn_ln_b)
    h = h + _L1_ffn_ref(_layernorm(h, axis=-1), L1_ffn_gate_W, L1_ffn_gate_b, L1_ffn_W1, L1_ffn_b1, L1_ffn_g1, L1_ffn_be1, L1_ffn_W2, L1_ffn_b2, L1_ffn_g2, L1_ffn_be2)
    h = h + _L2_attn_ref(_layernorm(h, axis=-1), L2_attn_w_up, L2_attn_b_up, L2_attn_conv_w, L2_attn_conv_b, L2_attn_skip, L2_attn_w_f, L2_attn_w_i, L2_attn_w_h, L2_attn_w_down, L2_attn_b_down)
    h = h + _L2_ffn_ref(_layernorm(h, axis=-1), L2_ffn_gate_w, L2_ffn_w1, L2_ffn_w2, L2_ffn_w3, L2_ffn_sw1, L2_ffn_sw2, L2_ffn_sw3)
    h = h + _L3_attn_ref(_layernorm(h, axis=-1), L3_attn_nu_log, L3_attn_theta_log, L3_attn_gamma_log, L3_attn_B_re, L3_attn_B_im, L3_attn_C_re, L3_attn_C_im, L3_attn_D)
    h = h + _L3_ffn_ref(_layernorm(h, axis=-1), L3_ffn_sg, L3_ffn_su, L3_ffn_sd, L3_ffn_rg, L3_ffn_ru, L3_ffn_rd, L3_ffn_wr, L3_ffn_rb)
    return h

_drawn_inputs = setup_inputs


def setup_inputs(seed=0):
    import zlib

    import numpy as np

    out = dict(_drawn_inputs(seed))
    spreads = {'L0_tok_b': (0.0, 0.1),
     'L0_attn_gamma': (1.0, 0.2),
     'L0_attn_beta': (0.0, 0.1),
     'L0_ffn_rms_w': (1.0, 0.6),
     'L0_ffn_b1': (0.0, 0.755),
     'L0_ffn_b2': (0.0, 0.36),
     'L1_attn_D_param': (1.0, 0.6),
     'L1_attn_ln_g': (1.0, 0.2),
     'L1_attn_ln_b': (0.0, 0.1),
     'L1_ffn_gate_b': (0.0, 0.1),
     'L1_ffn_b1': (0.0, 0.1),
     'L1_ffn_g1': (1.0, 0.2),
     'L1_ffn_be1': (0.0, 0.417),
     'L1_ffn_b2': (0.0, 0.1),
     'L1_ffn_g2': (1.0, 0.2),
     'L1_ffn_be2': (0.0, 0.399),
     'L2_attn_b_up': (0.0, 0.289),
     'L2_attn_conv_b': (0.0, 0.509),
     'L2_attn_skip': (1.0, 0.6),
     'L2_attn_b_down': (0.0, 0.289),
     'L3_ffn_rb': (0.0, 0.8)}
    factors = {'L0_attn_A': 5.567,
     'L0_attn_B': 2.744,
     'L0_ffn_W1': 2.942,
     'L0_ffn_W2': 3.13,
     'L1_attn_W_x': 8.0,
     'L1_attn_W_dt': 8.0,
     'L1_attn_b_dt': 8.0,
     'L1_attn_A_log': 8.0,
     'L2_attn_w_f': 21.377,
     'L2_attn_w_i': 31.953,
     'L2_attn_w_h': 8.0,
     'L3_ffn_sg': 8.0,
     'L3_ffn_su': 8.0,
     'L3_ffn_sd': 8.0,
     'L3_ffn_rg': 8.0,
     'L3_ffn_ru': 8.0,
     'L3_ffn_rd': 8.0,
     'L3_ffn_wr': 8.0}
    for name, (base, spread) in spreads.items():
        noise = np.random.default_rng([zlib.crc32(name.encode()), seed]).standard_normal(out[name].shape)
        drawn = base * np.exp(spread * noise) if base else spread * noise
        out[name] = jnp.asarray(drawn.astype(out[name].dtype))
    for name, factor in factors.items():
        out[name] = (out[name] * factor).astype(out[name].dtype)
    return out
```

```python
from contextlib import ExitStack

import numpy as np

import concourse.bass as bass
from concourse import mybir

F32 = mybir.dt.float32
I32 = mybir.dt.int32
U32 = mybir.dt.uint32
ALU = mybir.AluOpType
ACT = mybir.ActivationFunctionType
AX = mybir.AxisListType

NB, L = 16, 36
T = NB * L
D = 256
KD = D // 128
TT = 96
NT = T // TT
TH = T // 2
E = 8
F0 = 1024
C0 = F0 // 128
E1 = 4
NS = 16
INNER = 512
KI = INNER // 128
F2 = 704
CP = 2 * F2 // 128
NPAIR = 4
FS = 384
CS = FS // 128
WCH = 3 * 256
PATCH_K = 768 // 128
NEG = -3.0e38
VARIANT = [0] * (F2 // 128) + [1] + [2] * (F2 // 128)
ATANH = [1.0 / (2 * k + 1) for k in range(9)]
TWO_PI_HI = 6.28125
TWO_PI_LO = float(2 * np.pi - 6.28125)
ROUND_MAGIC = 12582912.0
LN_EPS, RMS_EPS = 1e-5, 1e-6

COL = {}
_n = 0
for _name, _w in [("rms_w", KD), ("b1_0", E * C0), ("b_dt", KD), ("D_param", KD), ("A_log", KD * NS), ("g1", E1 * KD),
                  ("be1", E1 * KD), ("conv_w", 4 * KI), ("conv_b", KI), ("skip", KI), ("b_up", 2 * KI), ("nu", 1),
                  ("theta", 1), ("gamma", 1)]:
    COL[_name] = _n
    _n += _w
NCOL = _n
ROW = {}
_n = 0
for _name, _w in [("tok_b", D), ("gamma", D), ("beta", D), ("ln_g", D), ("ln_b", D), ("b_down", D), ("g2", E1 * D),
                  ("gate_b1", E), ("gate_b3", E), ("b1", E1 * D), ("b2", E1 * D)]:
    ROW[_name] = _n
    _n += _w
NROW_BC = ROW["b1"]
NROW = _n
SUB = {"attn0": 0, "ffn0": 1, "attn1": 2, "ffn1": 3, "attn2": 4, "ffn2": 5, "attn3": 6, "ffn3": 7}
GATES = {"ffn0": 0, "ffn1": 1, "ffn2": 2, "ffn3": 3}


def tower(nc, patches, w_tok, w_rnn, w_moe0, b2_moe0, w_in, w_x, w_dt, w_out, w_l1, be2_l1, w_up, w_gates, w_down,
          w_moe2, w_sh2, w_lru, w_moe3, gate_w, cols, rows, ident_in, sel_in, out, bc_scratch):
    ctx = ExitStack()
    with ctx:
        def sb(name, shape, dt=F32):
            return ctx.enter_context(nc.sbuf_tensor(name, shape, dt))

        sems = {}

        def sem(name):
            if name not in sems:
                sems[name] = ctx.enter_context(nc.semaphore(name))
            return sems[name]

        PS = ctx.enter_context(nc.psum_tensor("PS", [128, 8, 512], F32))

        def CM(d, h):
            return PS[:, 2 * h + d, 0:TH]

        def TM(j, n=1):
            return PS[0:TT, 4 + j // 2, (j % 2) * D:(j % 2 + n) * D]

        H = sb("H", [TT, NT, D])
        XH = sb("XH", [TT, NT, D])
        XT = sb("XT", [128, KD, T])
        TMP = sb("TMP", [TT, NT, D])
        YT = sb("YT", [128, KD, T])
        ident = sb("ident", [128, 128])
        sel = sb("sel", [E, E + NPAIR, 128])
        colv = sb("colv", [128, NCOL])
        rowv = sb("rowv", [TT, NROW_BC])
        row1 = sb("row1", [1, NROW - NROW_BC])
        ones1 = sb("ones1", [1, TT])
        zero8 = sb("zero8", [E, 128])
        gatew = sb("gatew", [128, 4, KD, E])
        stats = sb("stats", [TT, NT, 6])
        mv = sb("mv", [TT, NT, 2])
        rs = sb("rs", [TT, NT, 6])
        rs_i = sb("rs_i", [TT, NT], I32)
        wrnn_s = sb("wrnn_s", [128, 3, KD, D])
        win_s = sb("win_s", [128, KD, 2 * D])
        wx_s = sb("wx_s", [128, KD, D + 2 * NS])
        wdt_s = sb("wdt_s", [128, KD, D])
        wout_s = sb("wout_s", [128, KD, D])
        wl1_s = sb("wl1_s", [128, 2, E1, KD, D])
        be2_s = sb("be2_s", [E, D])
        b20_s = sb("b20_s", [E, D])
        wlru_s = sb("wlru_s", [128, 4, D])
        wlruD_s = sb("wlruD_s", [128, KD, D])
        combT = sb("combT", [E, T])
        comb = sb("comb", [TT, NT, E])
        gl = sb("gl", [TT, NT, E])
        gm = sb("gm", [TT, NT, 8])
        gi = sb("gi", [TT, NT, 8], U32)
        gf = sb("gf", [TT, NT, 8])
        ge = sb("ge", [TT, NT, E])
        gk = sb("gk", [TT, NT, E])
        gs = sb("gs", [TT, NT])
        iota8 = sb("iota8", [TT, E], I32)
        iota8f = sb("iota8f", [TT, E])
        ARENA = 22500
        b1_e = sb("b1_e", [128, C0])
        arena = sb("arena", [128, ARENA])
        combB = arena[:, 0:12 * T].rearrange("p (v t) -> p v t", v=12)
        o = 12 * T
        ring = arena[:, o:o + CP * WCH].rearrange("p (c w) -> p c w", c=CP)
        o += CP * WCH
        NSLOT = 4
        act_s = arena[:, o:o + NSLOT * TH].rearrange("p (s t) -> p s t", s=NSLOT)
        o += NSLOT * TH
        uc_s = arena[:, o:o + NSLOT * TH].rearrange("p (s t) -> p s t", s=NSLOT)
        o += NSLOT * TH
        hid_s = arena[:, o:o + NSLOT * TH].rearrange("p (s t) -> p s t", s=NSLOT)
        o += NSLOT * TH
        assert o <= ARENA, o

        def part(at, *shape):
            n = int(np.prod(shape))
            assert at + n <= ARENA, (at + n, ARENA)
            names = "abc"[:len(shape)]
            if len(shape) == 1:
                return arena[:, at:at + n]
            return arena[:, at:at + n].rearrange(f"p ({' '.join(names)}) -> p {' '.join(names)}",
                                                 **dict(zip(names, shape)))

        patch_s = part(0, PATCH_K, T)
        wtok_s = part(PATCH_K * T, PATCH_K, D)
        HN = part(PATCH_K * (T + D), KD, T)
        U1 = KD * T
        xs, zs, dr, dl, dx, ys = (part(i * U1, KD, T) for i in range(6))
        dA = part(6 * U1, 2, KD, T)
        dBx = part(8 * U1, 2, KD, T)
        hs_ = part(10 * U1, 2, KD, T)
        hC = part(12 * U1, 2, KD, T)
        bcB = part(14 * U1, 2, T)
        bcC = part(15 * U1, 2, T)
        bc_s = part(16 * U1, T)
        A_s = part(16 * U1 + T, KD, NS)
        diagD = part(16 * U1 + T + KD * NS, KD, 128)
        n1 = part(0, 2, D)
        n1T = part(2 * D, 2, KD, TT)
        e1tmp = part(2 * D + 2 * KD * TT, 2, D)
        U2 = KI * T
        wup_s = part(0, KD, 2 * INNER)
        wg_s = part(2 * 2 * INNER, 3, KI, 128)
        wdn_s = part(2 * 2 * INNER + 3 * KI * 128, KI, D)
        o2 = 2 * 2 * INNER + 3 * KI * 128 + KI * D
        xm = part(o2, KI, T)
        zz = part(o2 + U2, KI, T)
        ac = part(o2 + 2 * U2, KI, T)
        df = part(o2 + 3 * U2, KI, T)
        ws = [part(o2 + 4 * U2 + i * T, T) for i in range(6)]
        cosT, sinT, ncosg, cosg, sing = (sb(n, [128, L]) for n in ("cosT", "sinT", "nsinT", "cosg", "sing"))
        nsinT = ncosg
        lam = sb("lam", [128, T])
        lru_c = sb("lru_c", [128, 12])
        lt = [part(i * T, T) for i in range(10)]

        block = ctx.enter_context(nc.Block())

        def col(name, i=0):
            return colv[:, COL[name] + i:COL[name] + i + 1]

        def row(name, w=D, i=0):
            return rowv[:, ROW[name] + i * w:ROW[name] + (i + 1) * w]

        @block.sync
        def _(sp):
            def load(dst, src, name):
                sp.dma_start(dst, src).then_inc(sem("ld_" + name), 16)

            for k in range(PATCH_K):
                load(patch_s[:, k], patches[:, k], "patch")
                load(wtok_s[:, k], w_tok[:, k], "patch")
            load(ident[:, :], ident_in, "const")
            load(sel[:, :, :], sel_in, "const")
            load(colv[:, :], cols, "const")
            load(rowv[:, :], rows[:, 0:NROW_BC].to_broadcast([TT, NROW_BC]), "const")
            load(row1[:, :], rows[:, NROW_BC:NROW], "const")
            load(gatew[:, :, :, :], gate_w, "const")
            load(wrnn_s[:, :, :, :], w_rnn, "rnn")
            load(b20_s[:, :], b2_moe0, "rnn")
            load(win_s[:, :, :], w_in, "l1a")
            load(wx_s[:, :, :], w_x, "l1a")
            load(wdt_s[:, :, :], w_dt, "l1a")
            load(wout_s[:, :, :], w_out, "l1a")
            load(wl1_s[:, :, :, :, :], w_l1, "l1f")
            load(be2_s[:, :], be2_l1, "l1f")
            load(wlru_s[:, :, :], w_lru[:, 0:4], "lru")
            load(wlruD_s[:, :, :], w_lru[:, 4:6], "lru")

            sp.wait_ge(sem("tm_ready"), NT)
            for c in range(C0):
                sp.dma_start(ring[:, c, 0:512], w_moe0[0, c]).then_inc(sem(f"ring{c}"), 16)
            with sp.Fori(1, E) as e:
                for c in range(C0):
                    sp.wait_ge(sem("slot_free"), C0 * (e - 1) + (c + 1))
                    sp.dma_start(ring[:, c, 0:512], w_moe0[e, c]).then_inc(sem(f"ring{c}"), 16)

            sp.wait_ge(sem("bc_rows"), 2)
            sp.dma_start(bc_scratch, bc_s[0:2 * NS, :]).then_inc(sem("bc_stored"), 16)
            sp.wait_ge(sem("bc_stored"), 16)
            for n in range(2):
                for dst, r in ((bcB, 0), (bcC, NS)):
                    sp.dma_start(dst[:, n], bc_scratch[r + n:r + n + 1, :].to_broadcast([128, T]))\
                        .then_inc(sem(f"bc_spread{n}"), 16)
            with sp.Fori(1, NS // 2) as i:
                for n in range(2):
                    sp.wait_ge(sem("dbx_done"), 2 * i + (n - 1))
                    sp.wait_ge(sem("hc_done"), 2 * i + (n - 1))
                    for dst, r in ((bcB, 0), (bcC, NS)):
                        sp.dma_start(dst[:, n], bc_scratch[bass.ds(2 * i + (r + n), 1), :].to_broadcast([128, T]))\
                            .then_inc(sem(f"bc_spread{n}"), 16)

            sp.wait_ge(sem("ffn1_out"), 1)
            load(wup_s, w_up, "l2a")
            load(wg_s, w_gates, "l2a")
            load(wdn_s, w_down, "l2a")

            sp.wait_ge(sem("h_done"), 5)
            for c in range(CS):
                sp.dma_start(ring[:, c, :], w_sh2[c]).then_inc(sem(f"ring{c}"), 16)
            for c in range(CS, CP):
                sp.dma_start(ring[:, c, :], w_moe2[0, c]).then_inc(sem(f"ring{c}"), 16)
            for c in range(CS):
                sp.wait_ge(sem("slot_free"), E * C0 + c + 1)
                sp.dma_start(ring[:, c, :], w_moe2[0, c]).then_inc(sem(f"ring{c}"), 16)
            with sp.Fori(1, NPAIR) as q:
                for c in range(CP):
                    sp.wait_ge(sem("slot_free"), CP * (q - 1) + (E * C0 + CS + c + 1))
                    sp.dma_start(ring[:, c, :], w_moe2[q, c]).then_inc(sem(f"ring{c}"), 16)

            sp.wait_ge(sem("h_done"), 7)
            for c in range(CP):
                sp.dma_start(ring[:, c, :], w_moe3[0, c]).then_inc(sem(f"ring{c}"), 16)
            with sp.Fori(1, NPAIR) as q:
                for c in range(CP):
                    sp.wait_ge(sem("slot_free"), CP * (q - 1) + (E * C0 + CS + NPAIR * CP + c + 1))
                    sp.dma_start(ring[:, c, :], w_moe3[q, c]).then_inc(sem(f"ring{c}"), 16)

            out_v = out.rearrange("b l d -> (b l) d").rearrange("(j p) d -> p j d", p=TT)
            for j in range(NT):
                sp.wait_ge(sem("out_tile"), j + 1)
                sp.dma_start(out_v[:, j], H[:, j]).then_inc(sem("stored"), 16)
            sp.wait_ge(sem("stored"), 16 * NT)

        RING0 = [E] * C0 + [0] * (CP - C0)
        RING_SH = [RING0[c] + (1 if c < CS else 0) for c in range(CP)]
        RING3 = [RING_SH[c] + NPAIR for c in range(CP)]

        ST0 = 2 * C0
        ST2 = 2 * CP
        BASE2S = E * ST0
        BASE2 = BASE2S + 2 * CS
        BASE3 = BASE2 + NPAIR * ST2
        SF2S = E * C0
        SF2 = SF2S + CS
        SF3 = SF2 + NPAIR * CP

        @block.tensor
        def _(pe):
            def mm(out_, l, r, start=True, stop=True):
                return nc.tensor.matmul(out_, l, r, start=start, stop=stop, skip_group_check=True)

            def transpose_x(name):
                s = SUB[name]
                for j in range(NT):
                    pe.wait_ge(sem("xh_ready"), NT * s + j + 1)
                    for d in range(KD):
                        o_ = PS[:, 2 * (j // 3) + d, TT * (j % 3):TT * (j % 3 + 1)]
                        last = nc.tensor.transpose(o_, XH[:, j, 128 * d:128 * (d + 1)], ident[0:TT, 0:TT])
                    if j % 3 == 2:
                        last.then_inc(sem("xt_psum"), 1)

            def gate_logits(name):
                s = SUB[name]
                pe.wait_ge(sem("xt_ready"), 2 * s + 2)
                for j in range(NT):
                    for k in range(KD):
                        last = mm(PS[0:TT, 7, E * j:E * (j + 1)], XT[:, k, TT * j:TT * (j + 1)],
                                  gatew[:, GATES[name], k, :], k == 0, k == KD - 1)
                last.then_inc(sem("logits"), 1)

            def spread_gates(name, variants):
                g = GATES[name]
                pe.wait_ge(sem("comb_ready"), g + 1)
                for j in range(NT):
                    last = nc.tensor.transpose(PS[0:E, 4 + j // 3, TT * (j % 3):TT * (j % 3 + 1)], comb[:, j, :],
                                               ident[0:TT, 0:TT])
                last.then_inc(sem("combT_psum"), 1)
                pe.wait_ge(sem("combT_ready"), g + 1)
                for i, v in enumerate(variants):
                    if i >= 2:
                        pe.wait_ge(sem(f"combB_copied_{name}"), i - 1)
                    for h in range(2):
                        last = mm(PS[:, 4 + 2 * (i % 2) + h, 0:TH], sel[:, v, :], combT[:, TH * h:TH * (h + 1)])
                    last.then_inc(sem(f"combB_psum_{name}"), 1)

            def token_products(name, tiles_of, n_k, rhs, pre=None):
                s = SUB[name]
                for j in range(NT):
                    for k in range(n_k):
                        last = mm(TM(j), tiles_of(k, j), rhs(k), k == 0, k == n_k - 1)
                    last.then_inc(sem("tm_ready"), 1)

            def tsl(j):
                return slice(TT * j, TT * (j + 1))

            def hsl(h):
                return slice(TH * h, TH * (h + 1))

            pe.wait_ge(sem("ld_patch"), 16 * 2 * PATCH_K)
            token_products("attn0", lambda k, j: patch_s[:, k, tsl(j)], PATCH_K, lambda k: wtok_s[:, k, :])

            pe.wait_ge(sem("ld_const"), 16 * 6)
            transpose_x("attn0")
            pe.wait_ge(sem("ld_rnn"), 32)
            pe.wait_ge(sem("xt_ready"), 2)
            for m in range(KD):
                for lh in range(2):
                    for k in range(KD):
                        xv = XT[:, k, :].rearrange("p (b l) -> p l b", l=L)[:, 18 * lh:18 * (lh + 1), :]
                        last = mm(PS[:, 4 + 2 * lh + m, 0:TH], wrnn_s[:, 1, k, 128 * m:128 * (m + 1)], xv, k == 0, False)
            last.then_inc(sem("rnn_x"), 1)
            HNv = HN[:, :, :].rearrange("p k (b l) -> p k b l", l=L)

            def rnn_step(lh, at, t_prev):
                for m in range(KD):
                    for k in range(KD):
                        last = mm(PS[:, 4 + 2 * lh + m, bass.ds(at, NB)], wrnn_s[:, 0, k, 128 * m:128 * (m + 1)],
                                  HNv[:, k, :, bass.ds(t_prev, 1)], False, False)
                return last

            with pe.Fori(1, 18) as t:
                pe.wait_ge(sem("rnn_h"), t)
                rnn_step(0, t * NB, t - 1).then_inc(sem("rnn_z"), 1)
            with pe.Fori(18, 36) as t:
                pe.wait_ge(sem("rnn_h"), t)
                rnn_step(1, t * NB - 18 * NB, t - 1).then_inc(sem("rnn_z"), 1)
            pe.wait_ge(sem("rnn_h"), L)
            token_products("attn0", lambda k, j: HN[:, k, tsl(j)], KD, lambda k: wrnn_s[:, 2, k, :])

            transpose_x("ffn0")
            gate_logits("ffn0")
            spread_gates("ffn0", range(E))
            pe.wait_ge(sem("combB_ready"), 1)
            for h in range(2):
                for d in range(KD):
                    mm(CM(d, h), b20_s[:, 128 * d:128 * (d + 1)], combT[:, hsl(h)], True, False)

            def up0(i, e):
                c, h = i // 2, i % 2
                if h == 0:
                    pe.wait_ge(sem(f"ring{c}"), 16 * e + 16)
                for k in range(KD):
                    last = mm(PS[:, 4 + i % 4, 0:TH], ring[:, c, 128 * k:128 * (k + 1)], XT[:, k, hsl(h)], k == 0, k == KD - 1)
                last.then_inc(sem("up_done"), 1)

            def down0(i, e):
                c, h = i // 2, i % 2
                pe.wait_ge(sem("hid_ready"), ST0 * e + (i + 1))
                for d in range(KD):
                    last = mm(CM(d, h), ring[:, c, 256 + 128 * d:256 + 128 * (d + 1)], hid_s[:, i % NSLOT, :],
                              False, False)
                if h == 1:
                    last.then_inc(sem("slot_free"), 1)
                return last

            up0(0, 0)
            up0(1, 0)
            with pe.Fori(0, E - 1) as e:
                for i in range(ST0):
                    up0(i + 2, e) if i + 2 < ST0 else up0(i + 2 - ST0, e + 1)
                    down0(i, e)
            for i in range(ST0):
                if i + 2 < ST0:
                    up0(i + 2, E - 1)
                down0(i, E - 1)

            def residual_tiles(n_acc):
                for j in range(NT):
                    if j % 3 == 0:
                        pe.wait_ge(sem("yt_ready"), 2 * (n_acc - 1) + 1 + j // 3)
                    for d in range(KD):
                        last = nc.tensor.transpose(PS[0:TT, 4 + j // 2, (j % 2) * D + 128 * d:(j % 2) * D + 128 * (d + 1)],
                                                   YT[:, d, tsl(j)], ident[:, :])
                    last.then_inc(sem("tm_ready"), 1)

            residual_tiles(1)

            transpose_x("attn1")
            pe.wait_ge(sem("ld_l1a"), 64)
            pe.wait_ge(sem("xt_ready"), 2 * SUB["attn1"] + 2)
            for m in range(2 * KD):
                for h in range(2):
                    for k in range(KD):
                        last = mm(PS[:, 4 + 2 * (m % 2) + h, 0:TH], win_s[:, k, 128 * m:128 * (m + 1)], XT[:, k, hsl(h)],
                                  k == 0, k == KD - 1)
                last.then_inc(sem("xz_psum"), 1)
                if m == 1:
                    pe.wait_ge(sem("xz_read"), 2)
            for h in range(2):
                for k in range(KD):
                    last = mm(PS[0:2 * NS, h, 0:TH], wx_s[:, k, D:D + 2 * NS], xs[:, k, hsl(h)], k == 0, k == KD - 1)
            last.then_inc(sem("bc_psum"), 1)
            pe.wait_ge(sem("xz_read"), 4)
            for m in range(KD):
                for h in range(2):
                    for k in range(KD):
                        last = mm(PS[:, 4 + 2 * h + m, 0:TH], wx_s[:, k, 128 * m:128 * (m + 1)], xs[:, k, hsl(h)],
                                  k == 0, k == KD - 1)
            last.then_inc(sem("dr_psum"), 1)
            pe.wait_ge(sem("dr_ready"), 2)
            for m in range(KD):
                for h in range(2):
                    for k in range(KD):
                        last = mm(PS[:, 4 + 2 * h + m, 0:TH], wdt_s[:, k, 128 * m:128 * (m + 1)], dr[:, k, hsl(h)],
                                  k == 0, k == KD - 1)
            last.then_inc(sem("dt_psum"), 1)
            pe.wait_ge(sem("bc_rows"), 2)
            pe.wait_ge(sem("diag_ready"), 1)
            for h in range(2):
                for d in range(KD):
                    mm(CM(d, h), diagD[:, d, :], xs[:, d, hsl(h)], True, False)
            pe.sem_inc(sem("hc_read"), 2)
            with pe.Fori(0, NS // 2) as i:
                for n in range(2):
                    pe.wait_ge(sem("hc_done"), 2 * i + (n + 1))
                    for h in range(2):
                        for d in range(KD):
                            last = mm(CM(d, h), ident[:, :], hC[:, n, d, hsl(h)], False, False)
                    last.then_inc(sem("hc_read"), 1)
            pe.wait_ge(sem("ys_ready"), 1)
            token_products("attn1", lambda k, j: ys[:, k, tsl(j)], KD, lambda k: wout_s[:, k, :])

            transpose_x("ffn1")
            gate_logits("ffn1")
            pe.wait_ge(sem("comb_ready"), GATES["ffn1"] + 1)
            for j in range(NT):
                last = nc.tensor.transpose(PS[0:E, 4 + j // 3, TT * (j % 3):TT * (j % 3 + 1)], comb[:, j, :],
                                           ident[0:TT, 0:TT])
            last.then_inc(sem("combT_psum"), 1)
            pe.wait_ge(sem("combT_ready"), GATES["ffn1"] + 1)
            pe.wait_ge(sem("ld_l1f"), 32)
            for j in range(NT):
                last = mm(TM(j), combT[:, tsl(j)], be2_s[:, :])
                last.then_inc(sem("tm_ready"), 1)
            r1 = lambda i: row1[:, i * D:(i + 1) * D]
            for s in range(E1 * NT):
                e, j = s // NT, s % NT
                b = s % 2
                z1 = PS[0:TT, b, 0:D]
                if s >= 2:
                    pe.wait_ge(sem("e1_n1"), s - 1)
                for k in range(KD):
                    mm(z1, XT[:, k, tsl(j)], wl1_s[:, 0, e, k, :], k == 0, False)
                mm(z1, ones1[:, :], r1(e), False, True).then_inc(sem("e1_z1"), 1)
                pe.wait_ge(sem("e1_n1"), s + 1)
                for d in range(KD):
                    last = nc.tensor.transpose(PS[:, 2 + b, TT * d:TT * (d + 1)],
                                               n1[0:TT, b, 128 * d:128 * (d + 1)], ident[0:TT, 0:TT])
                last.then_inc(sem("e1_t"), 1)
                z2 = PS[0:TT, 4 + b, 0:D]
                pe.wait_ge(sem("e1_h"), s + 1)
                if s >= 2:
                    pe.wait_ge(sem("e1_z2_read"), s - 1)
                for k in range(KD):
                    mm(z2, n1T[:, b, k, :], wl1_s[:, 1, e, k, :], k == 0, False)
                mm(z2, ones1[:, :], r1(E1 + e), False, True).then_inc(sem("e1_z2"), 1)

            transpose_x("attn2")
            pe.wait_ge(sem("ld_l2a"), 48)
            pe.wait_ge(sem("xt_ready"), 2 * SUB["attn2"] + 2)
            for m in range(2 * KI):
                if m >= 4:
                    pe.wait_ge(sem("up_read"), m - 3)
                for h in range(2):
                    for k in range(KD):
                        last = mm(PS[:, 2 * (m % 4) + h, 0:TH], wup_s[:, k, 128 * m:128 * (m + 1)], XT[:, k, hsl(h)],
                                  k == 0, k == KD - 1)
                last.then_inc(sem("up_psum"), 1)
            pe.wait_ge(sem("up_read"), 2 * KI)
            for m in range(KI):
                pe.wait_ge(sem("ac_ready"), m + 1)
                if m >= 1:
                    pe.wait_ge(sem("gates_read"), m)
                for g in range(3):
                    for h in range(2):
                        last = mm(PS[:, 2 * g + h, 0:TH], wg_s[:, g, m, :], ac[:, m, hsl(h)])
                last.then_inc(sem("gates_psum"), 1)
            pe.wait_ge(sem("h2_ready"), KI)
            token_products("attn2", lambda k, j: xm[:, k, tsl(j)], KI, lambda k: wdn_s[:, k, :])

            def gated(i, ring_count, q=None):
                c, h = i // 2, i % 2
                if h == 0:
                    pe.wait_ge(sem(f"ring{c}"), ring_count)
                for v in range(2):
                    for k in range(KD):
                        last = mm(PS[:, 4 + 2 * (i % 2) + v, 0:TH],
                                  ring[:, c, 256 * v + 128 * k:256 * v + 128 * (k + 1)], XT[:, k, hsl(h)],
                                  k == 0, k == KD - 1)
                last.then_inc(sem("up_done"), 1)

            def down(i, count):
                c, h = i // 2, i % 2
                pe.wait_ge(sem("hid_ready"), count)
                for d in range(KD):
                    last = mm(CM(d, h), ring[:, c, 512 + 128 * d:512 + 128 * (d + 1)], hid_s[:, i % 2, :],
                              False, False)
                if h == 1:
                    last.then_inc(sem("slot_free"), 1)

            def start_acc():
                for h in range(2):
                    for d in range(KD):
                        mm(CM(d, h), zero8[:, :], combT[:, hsl(h)], True, False)

            def pair_stage(base, counts):
                pe.wait_ge(sem("silu_done"), base)
                pe.wait_ge(sem("hid_ready"), base)
                gated(0, 16 * (counts[0] + 1))
                gated(1, 16 * (counts[0] + 1))
                with pe.Fori(0, NPAIR - 1) as q:
                    for i in range(ST2):
                        n = i + 2
                        pe.wait_ge(sem("silu_done"), ST2 * q + (base + n - 1))
                        pe.wait_ge(sem("uc_done"), ST2 * q + (base + n - 1 - E * ST0))
                        if n < ST2:
                            gated(n, 16 * q + 16 * (counts[n // 2] + 1))
                        else:
                            gated(n - ST2, 16 * q + 16 * (counts[(n - ST2) // 2] + 2))
                        down(i, ST2 * q + (base + i + 1))
                q = NPAIR - 1
                for i in range(ST2):
                    n = i + 2
                    if n < ST2:
                        pe.wait_ge(sem("silu_done"), ST2 * q + (base + n - 1))
                        pe.wait_ge(sem("uc_done"), ST2 * q + (base + n - 1 - E * ST0))
                        gated(n, 16 * (q + counts[n // 2] + 1))
                    down(i, ST2 * q + base + i + 1)

            transpose_x("ffn2")
            gate_logits("ffn2")
            spread_gates("ffn2", [v for q in range(NPAIR) for v in (2 * q, E + q, 2 * q + 1)])
            pe.wait_ge(sem("combB_ready"), 2)
            start_acc()
            gated(0, 16 * (RING0[0] + 1))
            gated(1, 16 * (RING0[0] + 1))
            for i in range(2 * CS):
                if i + 2 < 2 * CS:
                    pe.wait_ge(sem("silu_done"), BASE2S + i + 1)
                    pe.wait_ge(sem("hid_ready"), BASE2S + i + 1)
                    gated(i + 2, 16 * (RING0[(i + 2) // 2] + 1))
                down(i, BASE2S + i + 1)
            pair_stage(BASE2, RING_SH)
            residual_tiles(2)

            transpose_x("attn3")
            pe.wait_ge(sem("ld_lru"), 32)
            pe.wait_ge(sem("xt_ready"), 2 * SUB["attn3"] + 2)
            for v in range(2):
                for h in range(2):
                    for k in range(KD):
                        last = mm(PS[:, 4 + 2 * v + h, 0:TH], wlru_s[:, v, 128 * k:128 * (k + 1)], XT[:, k, hsl(h)],
                                  k == 0, k == KD - 1)
            last.then_inc(sem("u_psum"), 1)
            pe.wait_ge(sem("s_ready"), 2)
            for j in range(NT):
                mm(TM(j), lt[8][:, tsl(j)], wlru_s[:, 2, :], True, False)
                mm(TM(j), lt[9][:, tsl(j)], wlru_s[:, 3, :], False, False)
                for k in range(KD):
                    last = mm(TM(j), XT[:, k, tsl(j)], wlruD_s[:, k, :], False, k == KD - 1)
                last.then_inc(sem("tm_ready"), 1)

            transpose_x("ffn3")
            gate_logits("ffn3")
            spread_gates("ffn3", [v for q in range(NPAIR) for v in (2 * q, E + q, 2 * q + 1)])
            pe.wait_ge(sem("combB_ready"), 3)
            start_acc()
            pair_stage(BASE3, RING3)
            residual_tiles(3)

        @block.scalar
        def _(act):
            def xt_copy(name, scale=None):
                s = SUB[name]
                for h in range(2):
                    act.wait_ge(sem("xt_psum"), 2 * s + h + 1)
                    if scale is None:
                        nc.scalar.activation(XT[:, :, TH * h:TH * (h + 1)], PS[:, 2 * h:2 * h + 2, 0:TH], ACT.Copy)\
                            .then_inc(sem("xt_ready"), 1)
                    else:
                        for d in range(KD):
                            last = nc.scalar.activation(XT[:, d, TH * h:TH * (h + 1)], CM(d, h), ACT.Copy,
                                                        scale=col(scale, d))
                        last.then_inc(sem("xt_ready"), 1)

            def gate_exp(name):
                g = GATES[name]
                act.wait_ge(sem("gate_shifted"), g + 1)
                nc.scalar.activation(ge[:, :, :], gl[:, :, :], ACT.Exp).then_inc(sem("gate_exp"), 1)
                act.wait_ge(sem("combT_psum"), g + 1)
                nc.scalar.activation(combT[:, :].rearrange("p (h t) -> p h t", h=2), PS[0:E, 4:6, 0:TH], ACT.Copy)\
                    .then_inc(sem("combT_ready"), 1)

            def spread_copy(name, n, g):
                for i in range(n):
                    act.wait_ge(sem(f"combB_psum_{name}"), i + 1)
                    b = 4 + 2 * (i % 2)
                    last = nc.scalar.activation(combB[:, i, :].rearrange("p (h t) -> p h t", h=2), PS[:, b:b + 2, 0:TH],
                                                ACT.Copy)
                    last.then_inc(sem(f"combB_copied_{name}"), 1)
                act.wait_ge(sem(f"combB_copied_{name}"), n)
                act.sem_inc(sem("combB_ready"), 1)

            def acc_copy(n_acc):
                act.wait_ge(sem("slot_free"), (SF2, SF3, SF3 + NPAIR * CP)[n_acc - 1] - (CS if n_acc == 1 else 0))
                for h in range(2):
                    nc.scalar.activation(YT[:, :, TH * h:TH * (h + 1)], PS[:, 2 * h:2 * h + 2, 0:TH], ACT.Copy)\
                        .then_inc(sem("yt_ready"), 1)

            act.wait_ge(sem("ld_const"), 16 * 6)
            nc.scalar.activation(lru_c[:, 0:1], col("nu"), ACT.Exp).then_inc(sem("lru_a"), 1)
            nc.scalar.activation(lru_c[:, 2:3], col("theta"), ACT.Exp).then_inc(sem("lru_a"), 1)
            nc.scalar.activation(lru_c[:, 3:4], col("gamma"), ACT.Exp).then_inc(sem("lru_a"), 1)
            act.wait_ge(sem("lru_a"), 3)
            nc.scalar.activation(lru_c[:, 1:2], lru_c[:, 0:1], ACT.Exp, scale=-1.0).then_inc(sem("lru_b"), 1)
            act.wait_ge(sem("lru_reduced"), 1)
            nc.scalar.activation(sinT[:, 1:2], lru_c[:, 6:7], ACT.Sin).then_inc(sem("lru_sc"), 1)
            nc.scalar.activation(cosT[:, 1:2], lru_c[:, 7:8], ACT.Sin).then_inc(sem("lru_sc"), 1)

            xt_copy("attn0")
            HNv = HN[:, :, :].rearrange("p k (b l) -> p k b l", l=L)
            act.wait_ge(sem("rnn_x"), 1)
            nc.scalar.activation(HNv[:, :, :, 0:1], PS[:, 4:6, 0:NB], ACT.Tanh).then_inc(sem("rnn_h"), 1)
            with act.Fori(1, 18) as t:
                act.wait_ge(sem("rnn_z"), t)
                act.wait_ge(sem("rnn_x"), 1)
                nc.scalar.activation(HNv[:, :, :, bass.ds(t, 1)], PS[:, 4:6, bass.ds(t * NB, NB)], ACT.Tanh)\
                    .then_inc(sem("rnn_h"), 1)
            with act.Fori(18, 36) as t:
                act.wait_ge(sem("rnn_z"), t)
                act.wait_ge(sem("rnn_x"), 1)
                nc.scalar.activation(HNv[:, :, :, bass.ds(t, 1)], PS[:, 6:8, bass.ds(t * NB - 18 * NB, NB)], ACT.Tanh)\
                    .then_inc(sem("rnn_h"), 1)

            xt_copy("ffn0", "rms_w")
            gate_exp("ffn0")
            spread_copy("ffn0", E, 0)
            with act.Fori(0, E) as e:
                for i in range(ST0):
                    c = i // 2
                    act.wait_ge(sem("up_done"), ST0 * e + (i + 1))
                    if i == 0:
                        act.wait_ge(sem("b1_ready"), e + 1)
                    nc.scalar.activation(act_s[:, i % NSLOT, :], PS[:, 4 + i % 4, 0:TH], ACT.Silu,
                                         bias=b1_e[:, c:c + 1])\
                        .then_inc(sem("silu_done"), 1)
            acc_copy(1)

            xt_copy("attn1")
            for m in range(4):
                act.wait_ge(sem("xz_psum"), m + 1)
                b = 4 + 2 * (m % 2)
                dst = xs[:, m, :] if m < 2 else zs[:, m - 2, :]
                nc.scalar.activation(dst.rearrange("p (h t) -> p h t", h=2), PS[:, b:b + 2, 0:TH],
                                     ACT.Copy if m < 2 else ACT.Silu).then_inc(sem("xz_read"), 1)
            act.wait_ge(sem("bc_psum"), 1)
            for h in range(2):
                nc.scalar.activation(bc_s[0:2 * NS, TH * h:TH * (h + 1)], PS[0:2 * NS, h, 0:TH], ACT.Copy)\
                    .then_inc(sem("bc_rows"), 1)
            act.wait_ge(sem("dr_psum"), 1)
            for h in range(2):
                nc.scalar.activation(dr[:, :, TH * h:TH * (h + 1)], PS[:, 4 + 2 * h:6 + 2 * h, 0:TH], ACT.Copy)\
                    .then_inc(sem("dr_ready"), 1)
            nc.scalar.activation(A_s[:, :, :], colv[:, COL["A_log"]:COL["A_log"] + KD * NS]
                                 .rearrange("p (k n) -> p k n", k=KD), ACT.Exp).then_inc(sem("A_exp"), 1)
            act.wait_ge(sem("dt_biased"), 1)
            nc.scalar.activation(hs_[:, 0], dr[:, :, :], ACT.Abs).then_inc(sem("dt_abs"), 1)
            act.wait_ge(sem("dt_abs"), 1)
            nc.scalar.activation(dA[:, 0], hs_[:, 0], ACT.Exp, scale=-1.0).then_inc(sem("dt_e"), 1)
            act.wait_ge(sem("delta_ready"), 1)
            with act.Fori(0, NS // 2) as i:
                for n in range(2):
                    act.wait_ge(sem("scan_credit"), 2 * i + (n + 1))
                    for d in range(KD):
                        act.wait_ge(sem("delta_ready"), 1)
                        last = nc.scalar.activation(dA[:, n, d, :], dl[:, d, :], ACT.Exp,
                                                    scale=A_s[:, d, bass.ds(2 * i + n, 1)])
                    last.then_inc(sem("dA_ready"), 1)

            xt_copy("ffn1")
            gate_exp("ffn1")
            for s in range(E1 * NT):
                e, b = s // NT, s % 2
                act.wait_ge(sem("e1_t"), s + 1)
                if s >= 2:
                    act.wait_ge(sem("e1_z2"), s - 1)
                for d in range(KD):
                    last = nc.scalar.activation(n1T[:, b, d, :], PS[:, 2 + b, TT * d:TT * (d + 1)], ACT.Relu,
                                                bias=col("be1", e * KD + d), scale=col("g1", e * KD + d))
                last.then_inc(sem("e1_h"), 1)

            xt_copy("attn2")
            for m in range(2 * KI):
                act.wait_ge(sem("up_psum"), m + 1)
                b = 2 * (m % 4)
                dst = xm[:, m, :] if m < KI else zz[:, m - KI, :]
                nc.scalar.activation(dst.rearrange("p (h t) -> p h t", h=2), PS[:, b:b + 2, 0:TH],
                                     ACT.Identity if m < KI else ACT.Silu, bias=col("b_up", m)).then_inc(sem("up_read"), 1)
            for m in range(KI):
                act.wait_ge(sem("conv_ready"), m + 1)
                nc.scalar.activation(ac[:, m, :], df[:, m, :], ACT.Silu).then_inc(sem("ac_ready"), 1)

            def two(x):
                return x.rearrange("p (h t) -> p h t", h=2)

            for m in range(KI):
                act.wait_ge(sem("gates_psum"), m + 1)
                if m >= 1:
                    act.wait_ge(sem("diff_ready"), m)
                    act.wait_ge(sem("scan2_done"), m)
                for g in range(2):
                    nc.scalar.activation(two(ws[g]), PS[:, 2 * g:2 * g + 2, 0:TH], ACT.Abs).then_inc(sem("g_abs"), 1)
                for g in range(2):
                    act.wait_ge(sem("g_abs"), 2 * m + g + 1)
                    nc.scalar.activation(ws[2 + g], ws[g], ACT.Exp, scale=-1.0).then_inc(sem("g_exp"), 1)
                for g in range(2):
                    act.wait_ge(sem("g_exp"), 2 * m + g + 1)
                    nc.scalar.activation(ws[g], ws[2 + g], ACT.Ln, bias=1.0).then_inc(sem("g_ln"), 1)
                act.wait_ge(sem("diff_ready"), m + 1)
                nc.scalar.activation(ws[2], df[:, m, :], ACT.Sigmoid, scale=-1.0).then_inc(sem("sig"), 1)
                nc.scalar.activation(ws[3], df[:, m, :], ACT.Sigmoid).then_inc(sem("sig"), 1)
                nc.scalar.activation(two(ws[4]), PS[:, 4:6, 0:TH], ACT.Sigmoid).then_inc(sem("sig"), 1)

            def silu_step(i, done):
                act.wait_ge(sem("up_done"), done + 1)
                act.wait_ge(sem("hid_ready"), done - 1)
                nc.scalar.activation(act_s[:, i % 2, :], PS[:, 4 + 2 * (i % 2), 0:TH], ACT.Silu)\
                    .then_inc(sem("silu_done"), 1)

            def silu_pairs(base):
                with act.Fori(0, NPAIR) as q:
                    for i in range(ST2):
                        silu_step(i, ST2 * q + (base + i))

            xt_copy("ffn2")
            gate_exp("ffn2")
            spread_copy("ffn2", 3 * NPAIR, 2)
            for i in range(2 * CS):
                silu_step(i, BASE2S + i)
            silu_pairs(BASE2)
            acc_copy(2)

            xt_copy("attn3")
            xt_copy("ffn3")
            gate_exp("ffn3")
            spread_copy("ffn3", 3 * NPAIR, 3)
            silu_pairs(BASE3)
            acc_copy(3)

        @block.gpsimd
        def _(pool):
            nc.gpsimd.iota(iota8[:, :], pattern=[[1, E]], base=0, channel_multiplier=0).then_inc(sem("iota"), 1)
            nc.gpsimd.memset(ones1[:, :], 1.0).then_inc(sem("pool_const"), 1)
            nc.gpsimd.memset(zero8[:, :], 0.0).then_inc(sem("pool_const"), 1)
            with pool.Fori(0, NS // 2) as i:
                for n in range(2):
                    pool.wait_ge(sem("scan_done"), 2 * i + (n + 1))
                    pool.wait_ge(sem("hc_read"), 2 * i + (n + 1))
                    pool.wait_ge(sem(f"bc_spread{n}"), 32 * i + 32)
                    nc.gpsimd.tensor_tensor(hC[:, n, :, :], hs_[:, n, :, :],
                                            bcC[:, n:n + 1, :].to_broadcast([128, KD, T]), ALU.mult)\
                        .then_inc(sem("hc_done"), 1)

        @block.vector
        def _(dve):
            v = nc.vector
            chain = [0]

            def link(ins):
                chain[0] += 1
                ins.then_inc(sem("dve_step"), 1)
                dve.wait_ge(sem("dve_step"), chain[0])

            def mark(ins):
                chain[0] += 1
                ins.then_inc(sem("dve_step"), 1)

            def join():
                dve.wait_ge(sem("dve_step"), chain[0])

            def tile_in(before, j):
                dve.wait_ge(sem("tm_ready"), before + 2 * (j // 2) + 2)

            def rsqrt(dst, var, eps):
                x, y, a = rs[:, :, 0], rs[:, :, 1], rs[:, :, 2]
                link(v.tensor_scalar(x, var, eps, None, ALU.add))
                link(v.tensor_scalar(rs_i[:, :], rs[:, :, 0].bitcast(I32), 1, None, ALU.logical_shift_right))
                link(v.tensor_scalar(y.bitcast(I32), rs_i[:, :], -1.0, 1597463007.0, ALU.mult, ALU.add))
                for n in range(3):
                    link(v.tensor_tensor(a, y, y, ALU.mult))
                    link(v.scalar_tensor_tensor(a, a, -0.5, x, ALU.mult, ALU.mult))
                    link(v.scalar_tensor_tensor(dst if n == 2 else y, a, 1.5, y, ALU.add, ALU.mult))

            def tile_stats(src, j):
                v_in = src
                link(v.bn_stats(stats[:, j, :], v_in))
                mark(v.bn_aggr(mv[:, j, :], stats[:, j, :]))

            RSTD = rs[:, :, 3]

            def norm_to_xh(rstd=None):
                for j in range(NT):
                    v.tensor_scalar(XH[:, j, :], H[:, j, :], mv[:, j, 0:1], rs[:, j, 3:4], ALU.subtract, ALU.mult)\
                        .then_inc(sem("xh_ready"), 1)

            def layer_norm_h():
                join()
                rsqrt(RSTD, mv[:, :, 1], LN_EPS)
                norm_to_xh()

            def gates(name, second, over_chosen, bias=None, shared_first=False):
                g = GATES[name]
                if g == 0:
                    dve.wait_ge(sem("iota"), 1)
                    link(v.tensor_copy(iota8f[:, :], iota8[:, :]))
                dve.wait_ge(sem("logits"), g + 1)
                lp = PS[0:TT, 7, 0:NT * E].rearrange("p (j e) -> p j e", e=E)
                if bias is None:
                    link(v.tensor_copy(gl[:, :, :], lp))
                else:
                    link(v.tensor_tensor(gl[:, :, :], lp, row(bias, E)[:, None, :].to_broadcast([TT, NT, E]), ALU.add))
                for j in range(NT):
                    mark(v.max(gm[:, j, :], gl[:, j, :]))
                join()
                for j in range(NT):
                    mark(v.max_index(gi[:, j, :], gm[:, j, :], gl[:, j, :]))
                join()
                v.tensor_tensor(gl[:, :, :], gl[:, :, :], gm[:, :, 0:1].to_broadcast([TT, NT, E]), ALU.subtract)\
                    .then_inc(sem("gate_shifted"), 1)
                link(v.tensor_copy(gf[:, :, :], gi[:, :, :]))
                io = iota8f[:, None, :].to_broadcast([TT, NT, E])
                link(v.tensor_tensor(gk[:, :, :], io, gf[:, :, 0:1].to_broadcast([TT, NT, E]), ALU.is_equal))
                if second:
                    link(v.tensor_tensor(comb[:, :, :], io, gf[:, :, 1:2].to_broadcast([TT, NT, E]), ALU.is_equal))
                    link(v.tensor_tensor(gk[:, :, :], gk[:, :, :], comb[:, :, :], ALU.add))
                dve.wait_ge(sem("gate_exp"), g + 1)
                link(v.tensor_tensor(gk[:, :, :], gk[:, :, :], ge[:, :, :], ALU.mult))
                link(v.tensor_reduce(gs[:, :], (gk if over_chosen else ge)[:, :, :], AX.X, ALU.add))
                link(v.reciprocal(gs[:, :], gs[:, :]))
                ins = v.tensor_tensor(comb[:, :, :], gk[:, :, :], gs[:, :, None].to_broadcast([TT, NT, E]), ALU.mult)
                if shared_first:
                    link(ins)
                    ins = v.memset(comb[:, :, 0:1], 1.0)
                ins.then_inc(sem("comb_ready"), 1)

            def add_tm(j, tile):
                link(v.tensor_tensor(H[:, j, :], H[:, j, :], TM(j), ALU.add))

            dve.wait_ge(sem("lru_b"), 1)
            c_ = lambda i: lru_c[:, i:i + 1]
            link(v.tensor_scalar(c_(5), c_(2), float(np.pi / 2), None, ALU.add))
            link(v.tensor_copy(c_(4), c_(2)))
            link(v.tensor_scalar(lru_c[:, 8:10], lru_c[:, 4:6], float(1 / (2 * np.pi)), ROUND_MAGIC, ALU.mult, ALU.add))
            link(v.tensor_scalar(lru_c[:, 8:10], lru_c[:, 8:10], -ROUND_MAGIC, None, ALU.add))
            link(v.scalar_tensor_tensor(lru_c[:, 4:6], lru_c[:, 8:10], -TWO_PI_HI, lru_c[:, 4:6], ALU.mult, ALU.add))
            link(v.scalar_tensor_tensor(lru_c[:, 4:6], lru_c[:, 8:10], -TWO_PI_LO, lru_c[:, 4:6], ALU.mult, ALU.add))
            v.tensor_scalar(lru_c[:, 6:8], lru_c[:, 4:6], -3.1415925, 3.1415925, ALU.max, ALU.min)\
                .then_inc(sem("lru_reduced"), 1)
            mark(v.memset(cosT[:, 0:1], 1.0))
            mark(v.memset(sinT[:, 0:1], 0.0))
            join()
            dve.wait_ge(sem("lru_sc"), 2)
            n = 1
            while n < L - 1:
                w = min(n, L - 1 - n)
                cr, si = cosT[:, n:n + 1], sinT[:, n:n + 1]
                C1, S1 = cosT[:, 1:1 + w], sinT[:, 1:1 + w]
                C2, S2 = cosT[:, n + 1:n + 1 + w], sinT[:, n + 1:n + 1 + w]
                mark(v.tensor_scalar(cosg[:, 0:w], S1, si, None, ALU.mult))
                mark(v.tensor_scalar(sing[:, 0:w], S1, cr, None, ALU.mult))
                join()
                mark(v.scalar_tensor_tensor(C2, C1, cr, cosg[:, 0:w], ALU.mult, ALU.subtract))
                mark(v.scalar_tensor_tensor(S2, C1, si, sing[:, 0:w], ALU.mult, ALU.add))
                join()
                n += w
            mark(v.tensor_scalar(cosg[:, :], cosT[:, :], c_(3), None, ALU.mult))
            mark(v.tensor_scalar(sing[:, :], sinT[:, :], c_(3), None, ALU.mult))
            mark(v.tensor_scalar(nsinT[:, :], sinT[:, :], -1.0, None, ALU.mult))
            link(v.memset(lam[:, :], 1.0))
            link(v.memset(lam[:, :].rearrange("p (b l) -> p b l", l=L)[:, :, 0:1], 0.0))
            link(v.tensor_scalar(lam[:, :], lam[:, :], c_(1), None, ALU.mult))

            for j in range(NT):
                tile_in(0, j)
                link(v.tensor_tensor(H[:, j, :], TM(j), row("tok_b"), ALU.add))
                tile_stats(H[:, j, :], j)
            layer_norm_h()

            def normed_residual(tm0, scale_row, shift_row):
                for j in range(NT):
                    mark(v.tensor_tensor(H[:, j, :], H[:, j, :], row(shift_row), ALU.add))
                for j in range(NT):
                    tile_in(tm0, j)
                    link(v.tensor_tensor(TMP[:, j, :], TM(j), XH[:, j, :], ALU.add))
                    tile_stats(TMP[:, j, :], j)
                join()
                rsqrt(RSTD, mv[:, :, 1], LN_EPS)
                for j in range(NT):
                    link(v.scalar_tensor_tensor(TMP[:, j, :], TMP[:, j, :], mv[:, j, 0:1], row(scale_row), ALU.subtract,
                                                ALU.mult))
                    link(v.scalar_tensor_tensor(H[:, j, :], TMP[:, j, :], rs[:, j, 3:4], H[:, j, :], ALU.mult, ALU.add))
                for j in range(NT):
                    tile_stats(H[:, j, :], j)

            normed_residual(NT, "gamma", "beta")
            join()
            rsqrt(RSTD, mv[:, :, 1], LN_EPS)
            link(v.tensor_tensor(rs[:, :, 4], RSTD, RSTD, ALU.mult))
            link(v.tensor_tensor(rs[:, :, 4], rs[:, :, 4], mv[:, :, 1], ALU.mult))
            rsqrt(rs[:, :, 5], rs[:, :, 4], RMS_EPS)
            link(v.tensor_tensor(RSTD, RSTD, rs[:, :, 5], ALU.mult))
            norm_to_xh()
            gates("ffn0", False, False)

            dve.wait_ge(sem("combB_ready"), 1)
            v.tensor_copy(b1_e[:, :], colv[:, COL["b1_0"]:COL["b1_0"] + C0]).then_inc(sem("b1_ready"), 1)
            with dve.Fori(0, E) as e:
                for i in range(ST0):
                    dve.wait_ge(sem("silu_done"), ST0 * e + (i + 1))
                    v.tensor_tensor(hid_s[:, i % NSLOT, :], act_s[:, i % NSLOT, :],
                                    combB[:, bass.ds(e, 1), TH * (i % 2):TH * (i % 2 + 1)], ALU.mult)\
                        .then_inc(sem("hid_ready"), 1)
                v.tensor_copy(b1_e[:, :], colv[:, bass.ds(C0 * e + (COL["b1_0"] + C0), C0)]).then_inc(sem("b1_ready"), 1)

            def residual(tm0):
                for j in range(NT):
                    tile_in(tm0, j)
                    add_tm(j, None)
                    tile_stats(H[:, j, :], j)

            residual(2 * NT)

            layer_norm_h()
            for d in range(KD):
                last = v.tensor_scalar(diagD[:, d, :], ident[:, :], col("D_param", d), None, ALU.mult)
                mark(last)
            join()
            dve.sem_inc(sem("diag_ready"), 1)
            dve.wait_ge(sem("A_exp"), 1)
            link(v.tensor_scalar(A_s[:, :, :], A_s[:, :, :], -1.0, None, ALU.mult))
            dve.wait_ge(sem("dt_psum"), 1)
            for m in range(KD):
                last = v.tensor_scalar(dr[:, m, :].rearrange("p (h t) -> p h t", h=2), PS[:, 4 + m:8:2, 0:TH],
                                       col("b_dt", m), None, ALU.add)
                mark(last)
            join()
            dve.sem_inc(sem("dt_biased"), 1)
            ee, s1, s2, pl = dA[:, 0], dA[:, 1], dBx[:, 0], dBx[:, 1]
            dve.wait_ge(sem("dt_e"), 1)
            link(v.tensor_scalar(s2, ee, 2.0, None, ALU.add))
            link(v.reciprocal(s1, s2))
            link(v.tensor_tensor(s1, s1, ee, ALU.mult))
            link(v.tensor_tensor(s2, s1, s1, ALU.mult))
            link(v.tensor_scalar(pl, s2, ATANH[-1], ATANH[-2], ALU.mult, ALU.add))
            for a in ATANH[-3::-1]:
                link(v.tensor_tensor(pl, pl, s2, ALU.mult))
                link(v.tensor_scalar(pl, pl, a, None, ALU.add))
            link(v.scalar_tensor_tensor(pl, pl, 2.0, s1, ALU.mult, ALU.mult))
            link(v.scalar_tensor_tensor(dl[:, :, :], dr[:, :, :], 0.0, pl, ALU.max, ALU.add))
            link(v.tensor_tensor(dx[:, :, :], dl[:, :, :], xs[:, :, :], ALU.mult))
            dve.sem_inc(sem("delta_ready"), 1)
            dve.sem_inc(sem("scan_credit"), 2)
            with dve.Fori(0, NS // 2) as i:
                for n in range(2):
                    dve.wait_ge(sem(f"bc_spread{n}"), 32 * i + 32)
                    v.tensor_tensor(dBx[:, n, :, :], dx[:, :, :], bcB[:, n:n + 1, :].to_broadcast([128, KD, T]), ALU.mult)\
                        .then_inc(sem("dbx_done"), 1)
                    dve.wait_ge(sem("dA_ready"), 2 * i + (n + 1))
                    v.memset(dA[:, n].rearrange("p k (b l) -> p (k b) l", l=L)[:, :, 0:1], 0.0)\
                        .then_inc(sem("dA_cut"), 1)
                    dve.wait_ge(sem("dA_cut"), 2 * i + (n + 1))
                    dve.wait_ge(sem("dbx_done"), 2 * i + (n + 1))
                    dve.wait_ge(sem("hc_read"), 2 * i + (n + 1))
                    v.tensor_tensor_scan(hs_[:, n].rearrange("p k t -> p (k t)"), dA[:, n].rearrange("p k t -> p (k t)"),
                                         dBx[:, n].rearrange("p k t -> p (k t)"), 0.0, ALU.mult, ALU.add)\
                        .then_inc(sem("scan_done"), 1)
                    dve.wait_ge(sem("scan_done"), 2 * i + (n + 1))
                    dve.sem_inc(sem("scan_credit"), 1)
            dve.wait_ge(sem("hc_read"), NS + 2)
            link(v.tensor_tensor(ys[:, :, 0:TH], PS[:, 0:2, 0:TH], zs[:, :, 0:TH], ALU.mult))
            v.tensor_tensor(ys[:, :, TH:T], PS[:, 2:4, 0:TH], zs[:, :, TH:T], ALU.mult).then_inc(sem("ys_ready"), 1)
            normed_residual(3 * NT, "ln_g", "ln_b")

            layer_norm_h()
            gates("ffn1", True, True, "gate_b1")
            for j in range(NT):
                mark(v.tensor_tensor(H[:, j, :], H[:, j, :], XH[:, j, :], ALU.add))
            for j in range(NT):
                tile_in(4 * NT, j)
                join()
                mark(v.tensor_tensor(H[:, j, :], H[:, j, :], TM(j), ALU.add))
            join()

            def one_rstd(dst, var):
                x, y, a = rs[:, 0, 0:1], rs[:, 0, 1:2], rs[:, 0, 2:3]
                link(v.tensor_scalar(x, var, LN_EPS, None, ALU.add))
                link(v.tensor_scalar(rs_i[:, 0:1], x.bitcast(I32), 1, None, ALU.logical_shift_right))
                link(v.tensor_scalar(y.bitcast(I32), rs_i[:, 0:1], -1.0, 1597463007.0, ALU.mult, ALU.add))
                for n in range(3):
                    link(v.tensor_tensor(a, y, y, ALU.mult))
                    link(v.scalar_tensor_tensor(a, a, -0.5, x, ALU.mult, ALU.mult))
                    link(v.scalar_tensor_tensor(dst if n == 2 else y, a, 1.5, y, ALU.add, ALU.mult))

            for s in range(E1 * NT):
                e, j, b = s // NT, s % NT, s % 2
                z1 = PS[0:TT, b, 0:D]
                z2 = PS[0:TT, 4 + b, 0:D]
                dve.wait_ge(sem("e1_z1"), s + 1)
                tile_stats(z1, 0)
                join()
                one_rstd(rs[:, 0, 3:4], mv[:, 0, 1:2])
                if s >= 2:
                    dve.wait_ge(sem("e1_t"), s - 1)
                v.tensor_scalar(n1[0:TT, b, :], z1, mv[:, 0, 0:1], rs[:, 0, 3:4], ALU.subtract, ALU.mult)\
                    .then_inc(sem("e1_n1"), 1)
                dve.wait_ge(sem("e1_z2"), s + 1)
                dve.wait_ge(sem("e1_n1"), s + 1)
                tile_stats(z2, 0)
                join()
                one_rstd(rs[:, 0, 3:4], mv[:, 0, 1:2])
                link(v.tensor_tensor(rs[:, 0, 3:4], rs[:, 0, 3:4], comb[:, j, e:e + 1], ALU.mult))
                last = v.scalar_tensor_tensor(e1tmp[0:TT, b, :], z2, mv[:, 0, 0:1], row("g2", D, e), ALU.subtract, ALU.mult)
                last.then_inc(sem("e1_z2_read"), 1)
                dve.wait_ge(sem("e1_z2_read"), s + 1)
                link(v.scalar_tensor_tensor(H[:, j, :], e1tmp[0:TT, b, :], rs[:, 0, 3:4], H[:, j, :], ALU.mult, ALU.add))
            dve.sem_inc(sem("ffn1_out"), 1)
            for j in range(NT):
                tile_stats(H[:, j, :], j)

            layer_norm_h()
            for j in range(NT):
                mark(v.tensor_tensor(H[:, j, :], H[:, j, :], row("b_down"), ALU.add))
            for m in range(KI):
                dve.wait_ge(sem("up_read"), m + 1)
                link(v.tensor_scalar(df[:, m, :], xm[:, m, :], col("conv_w", 4 * m + 3), col("conv_b", m), ALU.mult, ALU.add))
                for back in range(1, 4):
                    xv = xm[:, m, :].rearrange("p (b l) -> p b l", l=L)[:, :, 0:L - back]
                    dv = df[:, m, :].rearrange("p (b l) -> p b l", l=L)[:, :, back:L]
                    ins = v.scalar_tensor_tensor(dv, xv, col("conv_w", 4 * m + 3 - back), dv, ALU.mult, ALU.add)
                    if back < 3:
                        link(ins)
                    else:
                        ins.then_inc(sem("conv_ready"), 1)

            def two(x):
                return x.rearrange("p (h t) -> p h t", h=2)

            for m in range(KI):
                dve.wait_ge(sem("g_ln"), 2 * m + 2)
                for g in range(2):
                    mark(v.scalar_tensor_tensor(two(ws[g]), PS[:, 2 * g:2 * g + 2, 0:TH], 0.0, two(ws[g]), ALU.min,
                                                ALU.subtract))
                join()
                v.tensor_tensor(df[:, m, :], ws[1], ws[0], ALU.subtract).then_inc(sem("diff_ready"), 1)
                dve.wait_ge(sem("sig"), 3 * m + 3)
                v.scalar_tensor_tensor(two(ws[5]), PS[:, 4:6, 0:TH], 0.5, two(ws[4]), ALU.add, ALU.max)\
                    .then_inc(sem("gates_read"), 1)
                dve.wait_ge(sem("gates_read"), m + 1)
                mark(v.tensor_tensor(ws[5], ws[5], ws[3], ALU.mult))
                mark(v.memset(ws[2].rearrange("p (b l) -> p b l", l=L)[:, :, 0:1], 0.0))
                join()
                v.tensor_tensor_scan(xm[:, m, :], ws[2], ws[5], 0.0, ALU.mult, ALU.add).then_inc(sem("scan2_done"), 1)
                dve.wait_ge(sem("scan2_done"), m + 1)
                xv = xm[:, m, :].rearrange("p (b l) -> p b l", l=L)
                link(v.scalar_tensor_tensor(df[:, m, :].rearrange("p (b l) -> p b l", l=L),
                                            ac[:, m, :].rearrange("p (b l) -> p b l", l=L), col("skip", m),
                                            xv[:, :, L - 1:L].to_broadcast([128, NB, L]), ALU.mult, ALU.add))
                v.tensor_tensor(xm[:, m, :], df[:, m, :], zz[:, m, :], ALU.mult).then_inc(sem("h2_ready"), 1)
            residual(5 * NT)
            join()
            dve.sem_inc(sem("h_done"), 5)

            def hid_slot_free(i, done, chunks):
                if i % 2:
                    dve.wait_ge(sem("slot_free"), chunks + i // 2)
                else:
                    dve.wait_ge(sem("up_done"), done + 2)

            def pair_hidden(base, chunks):
                with dve.Fori(0, NPAIR) as q:
                    for i in range(ST2):
                        c, h = i // 2, i % 2
                        dve.wait_ge(sem("up_done"), ST2 * q + (base + i + 1))
                        v.tensor_tensor(uc_s[:, h, :], PS[:, 5 + 2 * h, 0:TH],
                                        combB[:, bass.ds(3 * q + VARIANT[c], 1), TH * h:TH * (h + 1)], ALU.mult)\
                            .then_inc(sem("uc_done"), 1)
                        dve.wait_ge(sem("silu_done"), ST2 * q + (base + i + 1))
                        dve.wait_ge(sem("uc_done"), ST2 * q + (base + i + 1 - E * ST0))
                        hid_slot_free(i, ST2 * q + (base + i), CP * q + chunks)
                        v.tensor_tensor(hid_s[:, h, :], act_s[:, h, :], uc_s[:, h, :], ALU.mult)\
                            .then_inc(sem("hid_ready"), 1)

            layer_norm_h()
            gates("ffn2", True, False)
            for i in range(2 * CS):
                dve.wait_ge(sem("up_done"), BASE2S + i + 1)
                dve.wait_ge(sem("silu_done"), BASE2S + i + 1)
                hid_slot_free(i, BASE2S + i, SF2S)
                v.tensor_tensor(hid_s[:, i % 2, :], act_s[:, i % 2, :], PS[:, 5 + 2 * (i % 2), 0:TH], ALU.mult)\
                    .then_inc(sem("hid_ready"), 1)
                dve.sem_inc(sem("uc_done"), 1)
            pair_hidden(BASE2, SF2)
            residual(6 * NT)

            layer_norm_h()
            dve.wait_ge(sem("u_psum"), 1)
            ur = PS[:, 4:6, 0:TH].rearrange("p h (b l) -> p h b l", l=L)
            ui = PS[:, 6:8, 0:TH].rearrange("p h (b l) -> p h b l", l=L)

            def tab(t):
                return t[:, None, None, :].to_broadcast([128, 2, NB // 2, L])

            def tab3(t):
                return t[:, None, :].to_broadcast([128, NB, L])

            def hb(x):
                return x.rearrange("p (h b l) -> p h b l", h=2, l=L)

            def bl(x):
                return x.rearrange("p (b l) -> p b l", l=L)

            mark(v.tensor_tensor(hb(lt[0]), ur, tab(cosg), ALU.mult))
            mark(v.tensor_tensor(hb(lt[1]), ui, tab(sing), ALU.mult))
            mark(v.tensor_tensor(hb(lt[2]), ui, tab(cosg), ALU.mult))
            mark(v.tensor_tensor(hb(lt[3]), ur, tab(sing), ALU.mult))
            join()
            mark(v.tensor_tensor(lt[4], lt[0], lt[1], ALU.add))
            mark(v.tensor_tensor(lt[5], lt[2], lt[3], ALU.subtract))
            join()
            mark(v.tensor_tensor_scan(lt[6], lam[:, :], lt[4], 0.0, ALU.mult, ALU.add))
            mark(v.tensor_tensor_scan(lt[7], lam[:, :], lt[5], 0.0, ALU.mult, ALU.add))
            join()
            mark(v.tensor_tensor(bl(lt[0]), bl(lt[6]), tab3(cosT), ALU.mult))
            mark(v.tensor_tensor(bl(lt[1]), bl(lt[7]), tab3(sinT), ALU.mult))
            mark(v.tensor_tensor(bl(lt[2]), bl(lt[6]), tab3(nsinT), ALU.mult))
            mark(v.tensor_tensor(bl(lt[3]), bl(lt[7]), tab3(cosT), ALU.mult))
            join()
            v.tensor_tensor(lt[8], lt[0], lt[1], ALU.subtract).then_inc(sem("s_ready"), 1)
            v.tensor_tensor(lt[9], lt[2], lt[3], ALU.subtract).then_inc(sem("s_ready"), 1)
            residual(7 * NT)
            join()
            dve.sem_inc(sem("h_done"), 2)

            layer_norm_h()
            gates("ffn3", True, True, "gate_b3", shared_first=True)
            pair_hidden(BASE3, SF3)
            for j in range(NT):
                tile_in(8 * NT, j)
                v.tensor_tensor(H[:, j, :], H[:, j, :], TM(j), ALU.add).then_inc(sem("out_tile"), 1)


def kernel(**inputs):
    import concourse.bacc as bacc
    from concourse.bass_utils import run_bass_kernel_spmd

    x = {k: np.asarray(v) for k, v in inputs.items()}

    def km(w):
        k, n = w.shape
        return w.reshape(k // 128, 128, n).transpose(1, 0, 2)

    def cv(w):
        w = w.reshape(-1, 128)
        return w.T

    a = {}
    xx = x["x"]
    B_, C_, H_, W_ = xx.shape
    p = xx.reshape(B_, C_, H_ // 16, 16, W_ // 16, 16).transpose(0, 1, 2, 4, 3, 5).reshape(T, 768)
    a["patches"] = km(p.T)
    a["w_tok"] = km(x["L0_tok_W"].T)
    a["w_rnn"] = np.stack([km(x["L0_attn_" + n].T) for n in "ABC"], 1)
    w1 = x["L0_ffn_W1"].reshape(E, KD, 128, C0, 128).transpose(0, 3, 2, 1, 4).reshape(E, C0, 128, 256)
    w2 = x["L0_ffn_W2"].reshape(E, C0, 128, D)
    a["w_moe0"] = np.concatenate([w1, w2], -1)
    a["b2_moe0"] = x["L0_ffn_b2"]
    a["w_in"] = km(x["L1_attn_W_in"])
    a["w_x"] = km(x["L1_attn_W_x"])
    a["w_dt"] = km(x["L1_attn_W_dt"])
    a["w_out"] = km(x["L1_attn_W_out"])
    a["w_l1"] = np.stack([np.stack([km(x["L1_ffn_" + n][e]) for e in range(E1)], 1) for n in ("W1", "W2")], 1)
    a["be2_l1"] = np.concatenate([x["L1_ffn_be2"], np.zeros((E - E1, D), np.float32)])
    a["w_up"] = km(x["L2_attn_w_up"].T)
    g = np.zeros((3, KI, 32, 4, 32, 4), np.float32)
    for n, name in enumerate(("w_f", "w_i", "w_h")):
        w = x["L2_attn_" + name].reshape(KI, 32, 4, 4)
        for r in range(32):
            g[n, :, r, :, r, :] = w[:, r].transpose(0, 2, 1)
    a["w_gates"] = g.reshape(3, KI, 128, 128).transpose(2, 0, 1, 3)
    a["w_down"] = km(x["L2_attn_w_down"].T)

    def gated_chunks(wg, wu, wd):
        def up(w):
            w = w.transpose(1, 0, 2).reshape(KD, 128, -1, 128)
            return w.transpose(2, 1, 0, 3).reshape(-1, 128, 256)
        return np.concatenate([up(wg), up(wu), wd.reshape(-1, 128, D)], -1)

    a["w_moe2"] = gated_chunks(x["L2_ffn_w1"], x["L2_ffn_w3"], x["L2_ffn_w2"]).reshape(NPAIR, CP, 128, WCH)
    a["w_sh2"] = gated_chunks(x["L2_ffn_sw1"][None], x["L2_ffn_sw3"][None], x["L2_ffn_sw2"][None])
    a["w_lru"] = np.stack([km(x["L3_attn_B_re"].T).reshape(128, D), km(x["L3_attn_B_im"].T).reshape(128, D),
                           x["L3_attn_C_re"].T, x["L3_attn_C_im"].T, *km(x["L3_attn_D"].T).transpose(1, 0, 2)], 1)
    join = lambda s, r: np.concatenate([x["L3_ffn_" + s][None], x["L3_ffn_" + r]])
    a["w_moe3"] = gated_chunks(join("sg", "rg").transpose(0, 2, 1), join("su", "ru").transpose(0, 2, 1),
                               join("sd", "rd").transpose(0, 2, 1)).reshape(NPAIR, CP, 128, WCH)
    zpad = lambda w: np.concatenate([w, np.zeros((D, E - w.shape[1]), np.float32)], 1)
    zfirst = lambda w: np.concatenate([np.zeros((D, 1), np.float32), w], 1)
    a["gate_w"] = np.stack([km(zpad(w)) for w in (x["L0_ffn_gate_w"].T, x["L1_ffn_gate_W"], x["L2_ffn_gate_w"].T)]
                           + [km(zfirst(x["L3_ffn_wr"].T))], 1)
    al = x["L1_attn_A_log"].reshape(KD, 128, NS).transpose(1, 0, 2).reshape(128, KD * NS)
    cw = x["L2_attn_conv_w"].reshape(KI, 128, 4).transpose(1, 0, 2).reshape(128, 4 * KI)
    a["cols"] = np.concatenate([cv(x["L0_ffn_rms_w"]), cv(x["L0_ffn_b1"]), cv(x["L1_attn_b_dt"]), cv(x["L1_attn_D_param"]),
                                al, cv(x["L1_ffn_g1"]), cv(x["L1_ffn_be1"]), cw, cv(x["L2_attn_conv_b"]),
                                cv(x["L2_attn_skip"]), cv(x["L2_attn_b_up"]), cv(x["L3_attn_nu_log"]),
                                cv(x["L3_attn_theta_log"]), cv(x["L3_attn_gamma_log"])], 1)
    pad = lambda w: np.concatenate([w, np.full(E - len(w), NEG, np.float32)])
    a["rows"] = np.concatenate([x["L0_tok_b"], x["L0_attn_gamma"], x["L0_attn_beta"], x["L1_attn_ln_g"], x["L1_attn_ln_b"],
                                x["L2_attn_b_down"], x["L1_ffn_g2"].ravel(), pad(x["L1_ffn_gate_b"]),
                                np.float32([NEG]), x["L3_ffn_rb"], x["L1_ffn_b1"].ravel(), x["L1_ffn_b2"].ravel()])[None]
    a["ident_in"] = np.eye(128, dtype=np.float32)
    s = np.zeros((E, E + NPAIR, 128), np.float32)
    for e in range(E):
        s[e, e] = 1
    for q in range(NPAIR):
        s[2 * q, E + q, :64] = 1
        s[2 * q + 1, E + q, 64:] = 1
    a["sel_in"] = s
    a = {k: np.ascontiguousarray(w, dtype=np.float32) for k, w in a.items()}

    nc = bacc.Bacc("TRN2", target_bir_lowering=False, num_devices=1)
    args = {k: nc.dram_tensor(k, w.shape, F32, kind="ExternalInput").ap() for k, w in a.items()}
    out = nc.dram_tensor("out", (NB, L, D), F32, kind="ExternalOutput").ap()
    bc_scratch = nc.dram_tensor("bc_scratch", (2 * NS, T), F32, kind="Internal").ap()
    tower(nc, **args, out=out, bc_scratch=bc_scratch)
    r = run_bass_kernel_spmd(nc, [a], core_ids=[0])
    return r.results[0]["out"]
```

```python
from contextlib import ExitStack

import numpy as np

import concourse.bass as bass
from concourse import mybir

F32 = mybir.dt.float32
BF16 = mybir.dt.bfloat16
I32 = mybir.dt.int32
U32 = mybir.dt.uint32
ALU = mybir.AluOpType
ACT = mybir.ActivationFunctionType
AX = mybir.AxisListType

NB, L = 16, 36
T = NB * L
D = 256
KD = D // 128
TT = 96
NT = T // TT
TH = T // 2
E = 8
F0 = 1024
C0 = F0 // 128
E1 = 4
NS = 16
INNER = 512
KI = INNER // 128
F2 = 704
CH2 = 6
FS = 384
CS = FS // 128
PATCH_K = 768 // 128
NEG = -3.0e38
SB = 128
NBLK = {"ffn0": (T + E * (SB - 1)) // SB, "ffn2": (2 * T + E * (SB - 1)) // SB, "ffn3": (2 * T + (E - 1) * (SB - 1)) // SB}
MAXB = max(NBLK.values())
NEXP = {"ffn0": E, "ffn2": E, "ffn3": E - 1}
HU = {"ffn0": (512, 512), "ffn2": (384, 320), "ffn3": (384, 320)}
HC = {"ffn0": (4, 4), "ffn2": (3, 3), "ffn3": (3, 3)}
HLEN = {n: tuple((1 if n == "ffn0" else 2) * KD * HU[n][x] + HC[n][x] * D + (HC[n][x] if n == "ffn0" else 0)
                 for x in range(2)) for n in NBLK}
WLEN = max(sum(v) for v in HLEN.values())
SH2 = 2 * KD * FS + CS * D
ATANH = [1.0 / (2 * k + 1) for k in range(9)]
TWO_PI_HI = 6.28125
TWO_PI_LO = float(2 * np.pi - 6.28125)
ROUND_MAGIC = 12582912.0
LN_EPS, RMS_EPS = 1e-5, 1e-6

COL = {}
_n = 0
for _name, _w in [("rms_w", KD), ("b_dt", KD), ("D_param", KD), ("A_log", KD * NS), ("g1", E1 * KD),
                  ("be1", E1 * KD), ("conv_w", 4 * KI), ("conv_b", KI), ("skip", KI), ("b_up", 2 * KI), ("nu", 1),
                  ("theta", 1), ("gamma", 1)]:
    COL[_name] = _n
    _n += _w
NCOL = _n
ROW = {}
_n = 0
for _name, _w in [("tok_b", D), ("gamma", D), ("beta", D), ("ln_g", D), ("ln_b", D), ("b_down", D), ("g2", E1 * D),
                  ("gate_b1", E), ("gate_b3", E), ("b1", E1 * D), ("b2", E1 * D)]:
    ROW[_name] = _n
    _n += _w
NROW_BC = ROW["b1"]
NROW = _n
SUB = {"attn0": 0, "ffn0": 1, "attn1": 2, "ffn1": 3, "attn2": 4, "ffn2": 5, "attn3": 6, "ffn3": 7}
GATES = {"ffn0": 0, "ffn1": 1, "ffn2": 2, "ffn3": 3}


def tower(nc, patches, w_tok, w_rnn, w_moe0, b2_moe0, w_in, w_x, w_dt, w_out, w_l1, be2_l1, w_up, w_gates, w_down,
          w_moe2, w_sh2, w_lru, w_moe3, w_sh3, gate_w, cols, rows, ident_in, tri_in, out, bc_scratch,
          x_slots, y_slots):
    ctx = ExitStack()
    with ctx:
        def sb(name, shape, dt=F32):
            return ctx.enter_context(nc.sbuf_tensor(name, shape, dt))

        sems = {}

        def sem(name):
            if name not in sems:
                sems[name] = ctx.enter_context(nc.semaphore(name))
            return sems[name]

        PS = ctx.enter_context(nc.psum_tensor("PS", [128, 8, 512], F32))

        def CM(d, h):
            return PS[:, 2 * h + d, 0:TH]

        def TM(j, n=1):
            return PS[0:TT, 4 + j // 2, (j % 2) * D:(j % 2 + n) * D]

        H = sb("H", [TT, NT, D])
        XH = sb("XH", [TT, NT, D])
        XT = sb("XT", [128, KD, T])
        TMP = sb("TMP", [TT, NT, D])
        YT = sb("YT", [128, KD, T])
        ident = sb("ident", [128, 128])
        tri = sb("tri", [TT, 3, TT])
        colv = sb("colv", [128, NCOL])
        rowv = sb("rowv", [TT, NROW_BC])
        bias_p = sb("bias_p", [3, NROW - NROW_BC], BF16)
        ones3 = sb("ones3", [3, TT], BF16)
        gatew = sb("gatew", [128, 4, KD, E])
        stats = sb("stats", [TT, NT, 6])
        mv = sb("mv", [TT, NT, 2])
        rs = sb("rs", [TT, NT, 6])
        rs_i = sb("rs_i", [TT, NT], I32)
        wrnn_s = sb("wrnn_s", [128, 3, KD, D])
        win_s = sb("win_s", [128, KD, 2 * D])
        wx_s = sb("wx_s", [128, KD, D + 2 * NS])
        wdt_s = sb("wdt_s", [128, KD, D])
        wout_s = sb("wout_s", [128, KD, D])
        wl1_s = sb("wl1_s", [128, 2, E1, KD, D])
        be2_s = sb("be2_s", [E, D])
        b20_s = sb("b20_s", [E, D])
        wlru_s = sb("wlru_s", [128, 4, D])
        wlruD_s = sb("wlruD_s", [128, KD, D])
        combT = sb("combT", [E, T])
        comb = sb("comb", [TT, NT, E])
        gl = sb("gl", [TT, NT, E])
        gm = sb("gm", [TT, NT, 8])
        gi = sb("gi", [TT, NT, 8], U32)
        gf = sb("gf", [TT, NT, 8])
        ge = sb("ge", [TT, NT, E])
        gk = sb("gk", [TT, NT, E])
        gs = sb("gs", [TT, NT])
        iota8 = sb("iota8", [TT, E], I32)
        iota8f = sb("iota8f", [TT, E])
        ARENA = 22500
        arena = sb("arena", [128, ARENA])
        o = 0

        def take(*shape):
            nonlocal o
            o += int(np.prod(shape))
            return part(o - int(np.prod(shape)), *shape)

        def part(at, *shape):
            n = int(np.prod(shape))
            assert at + n <= ARENA, (at + n, ARENA)
            names = "abc"[:len(shape)]
            if len(shape) == 1:
                return arena[:, at:at + n]
            return arena[:, at:at + n].rearrange(f"p ({' '.join(names)}) -> p {' '.join(names)}",
                                                 **dict(zip(names, shape)))

        wbuf = [take(WLEN) for _ in range(2)]
        xslot = [take(D) for _ in range(2)]
        xbT = [take(KD, SB) for _ in range(2)]
        sg_s = [take(512) for _ in range(2)]
        hid_b = [take(512) for _ in range(2)]
        y_s = [take(D) for _ in range(2)]
        sact = take(2, TH)
        shid = take(2, TH)
        Yg = take(2, NT * D)
        assert o <= ARENA, o
        wsh = sb("wsh", [128, sum(HLEN["ffn2"])])
        msk = sb("msk", [TT, 2, E, NT])
        mks = sb("mks", [TT, E, NT])
        cnt = sb("cnt", [TT, E, NT])
        pre = sb("pre", [TT, E, NT])
        posf = sb("posf", [TT, 2, E, NT])
        pos = sb("pos", [TT, 2, NT])
        posu = sb("posu", [TT, 2, NT], U32)
        nblk = sb("nblk", [TT, 3, E])
        wgt = sb("wgt", [TT, 2, NT])
        eid_f = sb("eid_f", [1, MAXB, E])
        eid_s = sb("eid_s", [1, MAXB])
        eid = sb("eid", [1, MAXB], I32)
        iob = sb("iob", [1, MAXB], I32)
        iobf = sb("iobf", [1, MAXB])
        zrow = sb("zrow", [128, D])
        patch_s = part(0, PATCH_K, T)
        wtok_s = part(PATCH_K * T, PATCH_K, D)
        HN = part(PATCH_K * (T + D), KD, T)
        bias_f = [part(PATCH_K * (T + D) + (KD + 4 * i) * T, NROW - NROW_BC)[0:3] for i in range(4)]
        U1 = KD * T
        xs, zs, dr, dl, dx, ys = (part(i * U1, KD, T) for i in range(6))
        dA = part(6 * U1, 2, KD, T)
        dBx = part(8 * U1, 2, KD, T)
        hs_ = part(10 * U1, 2, KD, T)
        hC = part(12 * U1, 2, KD, T)
        bcB = part(14 * U1, 2, T)
        bcC = part(15 * U1, 2, T)
        bc_s = part(16 * U1, T)
        A_s = part(16 * U1 + T, KD, NS)
        diagD = part(16 * U1 + T + KD * NS, KD, 128)
        n1 = part(0, NT, D)
        n1T = part(NT * D, KD, T)
        eu = part(NT * D + KD * T, 2, NT, D)
        r1, nmr1, r2, nmr2 = (sb(n, [TT, NT]) for n in ("r1", "nmr1", "r2", "nmr2"))
        U2 = KI * T
        wup_s = part(0, KD, 2 * INNER)
        wg_s = part(2 * 2 * INNER, 3, KI, 128)
        wdn_s = part(2 * 2 * INNER + 3 * KI * 128, KI, D)
        o2 = 2 * 2 * INNER + 3 * KI * 128 + KI * D
        xm = part(o2, KI, T)
        zz = part(o2 + U2, KI, T)
        ac = part(o2 + 2 * U2, KI, T)
        df = part(o2 + 3 * U2, KI, T)
        ws = [part(o2 + 4 * U2 + i * T, T) for i in range(6)]
        cosT, sinT, ncosg, cosg, sing = (sb(n, [128, L]) for n in ("cosT", "sinT", "nsinT", "cosg", "sing"))
        nsinT = ncosg
        lam = sb("lam", [128, T])
        lru_c = sb("lru_c", [128, 12])
        lt = [part(i * T, T) for i in range(10)]

        block = ctx.enter_context(nc.Block())

        STAGE = {"ffn0": 0, "ffn2": 1, "ffn3": 2}
        BLK0, USE0 = {}, {}
        n_, u_ = 0, [0, 0]
        for name in STAGE:
            BLK0[name], USE0[name] = n_, tuple(u_)
            n_ += NBLK[name]
            u_ = [u_[0] + (NBLK[name] + 1) // 2, u_[1] + NBLK[name] // 2]
        ALLB, ALLU = n_, u_
        SHN = {"ffn2": 0, "ffn3": 2 * CS}
        SCAT = [NT, 3 * NT, 5 * NT]

        def over_blocks(eng, nb, emit):
            emit(0, 0, 0)
            with eng.Fori(0, (nb - 1) // 2) as i:
                emit(2 * i + 1, i, 1)
                emit(2 * i + 2, i + 1, 0)
            if nb % 2 == 0:
                emit(nb - 1, (nb - 1) // 2, 1)

        def col(name, i=0):
            return colv[:, COL[name] + i:COL[name] + i + 1]

        def row(name, w=D, i=0):
            return rowv[:, ROW[name] + i * w:ROW[name] + (i + 1) * w]

        @block.sync
        def _(sp):
            def load(dst, src, name):
                sp.dma_start(dst, src).then_inc(sem("ld_" + name), 16)

            for k in range(PATCH_K):
                load(patch_s[:, k], patches[:, k], "patch")
                load(wtok_s[:, k], w_tok[:, k], "patch")
            load(ident[:, :], ident_in, "const")
            load(tri[:, :, :], tri_in, "const")
            load(colv[:, :], cols, "const")
            load(rowv[:, :], rows[:, 0:NROW_BC].to_broadcast([TT, NROW_BC]), "const")
            load(bias_f[0], rows[:, NROW_BC:NROW].to_broadcast([3, NROW - NROW_BC]), "const")
            load(gatew[:, :, :, :], gate_w, "const")
            load(wrnn_s[:, :, :, :], w_rnn, "rnn")
            load(b20_s[:, :], b2_moe0, "rnn")
            load(win_s[:, :, :], w_in, "l1a")
            load(wx_s[:, :, :], w_x, "l1a")
            load(wdt_s[:, :, :], w_dt, "l1a")
            load(wout_s[:, :, :], w_out, "l1a")
            load(wl1_s[:, :, :, :, :], w_l1, "l1f")
            load(be2_s[:, :], be2_l1, "l1f")
            load(wsh[:, 0:SH2], w_sh2, "sh2")
            load(wlru_s[:, :, :], w_lru[:, 0:4], "lru")
            load(wlruD_s[:, :, :], w_lru[:, 4:6], "lru")

            sp.wait_ge(sem("pool_const"), 2)
            for b in range(MAXB):
                sp.dma_start(x_slots[SB * b:SB * (b + 1), :], zrow[:, :]).then_inc(sem("slots_zero"), 16)

            def expert_blocks(name, w):
                s = STAGE[name]
                nb, at = NBLK[name], BLK0[name]

                def expert_of(b):
                    return sp.value_load(eid[0:1, bass.ds(b, 1)], min_val=0, max_val=NEXP[name] - 1)

                def half(e, p, x):
                    o_ = sum(HLEN[name][:x])
                    n_ = HLEN[name][x]
                    src = w[bass.ds(e, 1), :, o_:o_ + n_].rearrange("e p n -> (e p) n")
                    sp.dma_start(wbuf[p][:, o_:o_ + n_], src).then_inc(sem(f"w{p}{x}"), 16)

                def rows_in(b, p):
                    sp.dma_start(xslot[p], x_slots[bass.ds(SB * b, SB), :]).then_inc(sem(f"x{p}"), 16)

                def rows_out(b, p):
                    sp.wait_ge(sem("y_sb"), b + (at + 1 + 2))
                    sp.dma_start(y_slots[bass.ds(SB * b, SB), :], y_s[p]).then_inc(sem(f"y{p}"), 16)

                def emit(b, hb, p, last=False):
                    if not last:
                        e = expert_of(b + 2)
                        sp.wait_ge(sem("downd"), 2 * b + (2 * at + 1))
                        rows_in(b + 2, p)
                        half(e, p, 0)
                        sp.wait_ge(sem("downd"), 2 * b + (2 * at + 2))
                        half(e, p, 1)
                    rows_out(b, p)

                sp.wait_ge(sem("eid_ready"), s + 1)
                for b in range(2):
                    e = expert_of(b)
                    for x in range(2):
                        half(e, b, x)
                sp.wait_ge(sem("scattered"), 16 * SCAT[s])
                for b in range(2):
                    rows_in(b, b)
                over_blocks(sp, nb - 2, emit)
                for b in range(nb - 2, nb):
                    emit(b, b // 2, b % 2, last=True)

            expert_blocks("ffn0", w_moe0)

            sp.wait_ge(sem("bc_rows"), 2)
            sp.dma_start(bc_scratch, bc_s[0:2 * NS, :]).then_inc(sem("bc_stored"), 16)
            sp.wait_ge(sem("bc_stored"), 16)
            for n in range(2):
                for dst, r in ((bcB, 0), (bcC, NS)):
                    sp.dma_start(dst[:, n], bc_scratch[r + n:r + n + 1, :].to_broadcast([128, T]))\
                        .then_inc(sem(f"bc_spread{n}"), 16)
            with sp.Fori(1, NS // 2) as i:
                for n in range(2):
                    sp.wait_ge(sem("dbx_done"), 2 * i + (n - 1))
                    sp.wait_ge(sem("hc_done"), 2 * i + (n - 1))
                    for dst, r in ((bcB, 0), (bcC, NS)):
                        sp.dma_start(dst[:, n], bc_scratch[bass.ds(2 * i + (r + n), 1), :].to_broadcast([128, T]))\
                            .then_inc(sem(f"bc_spread{n}"), 16)

            sp.wait_ge(sem("ffn1_out"), 1)
            load(wup_s, w_up, "l2a")
            load(wg_s, w_gates, "l2a")
            load(wdn_s, w_down, "l2a")

            expert_blocks("ffn2", w_moe2)
            load(wsh[:, :], w_sh3, "sh3")
            expert_blocks("ffn3", w_moe3)

            out_v = out.rearrange("b l d -> (b l) d").rearrange("(j p) d -> p j d", p=TT)
            for j in range(NT):
                sp.wait_ge(sem("out_tile"), j + 1)
                sp.dma_start(out_v[:, j], H[:, j]).then_inc(sem("stored"), 16)
            sp.wait_ge(sem("stored"), 16 * NT)

        @block.tensor
        def _(pe):
            def mm(out_, l, r, start=True, stop=True):
                return nc.tensor.matmul(out_, l, r, start=start, stop=stop, skip_group_check=True)

            def transpose_x(name):
                s = SUB[name]
                for j in range(NT):
                    pe.wait_ge(sem("xh_ready"), NT * s + j + 1)
                    for d in range(KD):
                        o_ = PS[:, 2 * (j // 3) + d, TT * (j % 3):TT * (j % 3 + 1)]
                        last = nc.tensor.transpose(o_, XH[:, j, 128 * d:128 * (d + 1)], ident[0:TT, 0:TT])
                    if j % 3 == 2:
                        last.then_inc(sem("xt_psum"), 1)

            def gate_logits(name):
                s = SUB[name]
                pe.wait_ge(sem("xt_ready"), 2 * s + 2)
                for j in range(NT):
                    for k in range(KD):
                        last = mm(PS[0:TT, 3, E * j:E * (j + 1)], XT[:, k, TT * j:TT * (j + 1)],
                                  gatew[:, GATES[name], k, :], k == 0, k == KD - 1)
                last.then_inc(sem("logits"), 1)

            def ranks(name):
                pe.wait_ge(sem("masks"), STAGE[name] + 1)
                mv_ = mks[:, :, :].rearrange("p e j -> p (e j)")
                mm(PS[0:TT, 3, 64:64 + E * NT], tri[:, 0, :], mv_)
                mm(PS[0:TT, 3, 128:128 + E * NT], tri[:, 1, :], mv_).then_inc(sem("ranks"), 1)

            def routed(name):
                at, nb = BLK0[name], NBLK[name]
                two_in = name != "ffn0"
                nv = 2 if two_in else 1

                def x_transposes(b, hb, p):
                    pe.wait_ge(sem(f"x{p}"), 16 * hb + 16 * (USE0[name][p] + 1))
                    for d in range(KD):
                        last = nc.tensor.transpose(PS[:, 6 + p, SB * d:SB * (d + 1)], xslot[p][:, 128 * d:128 * (d + 1)],
                                                   ident[:, :])
                    last.then_inc(sem("xt_t"), 1)

                def up(b, hb, p, x):
                    pe.wait_ge(sem(f"w{p}{x}"), 16 * hb + 16 * (USE0[name][p] + 1))
                    if x == 0:
                        pe.wait_ge(sem("xbT"), b + (at + 1))
                    w_, hu = wbuf[p][:, sum(HLEN[name][:x]):], HU[name][x]
                    for v_ in range(nv):
                        for c in range(HC[name][x]):
                            for k in range(KD):
                                o_ = (v_ * KD + k) * hu + 128 * c
                                last = mm(PS[:, 2 * x + v_, SB * c:SB * (c + 1)], w_[:, o_:o_ + 128], xbT[p][:, k, :],
                                          k == 0, k == KD - 1)
                    last.then_inc(sem("upd"), 1)

                def down(b, p, x):
                    pe.wait_ge(sem("hid2"), 2 * b + (2 * at + x + 1))
                    if x == 0:
                        pe.wait_ge(sem("y_sb"), b + (at + 1))
                    o_ = sum(HLEN[name][:x]) + nv * KD * HU[name][x]
                    n_c = HC[name][x]
                    for c in range(n_c):
                        rows_ = min(128, HU[name][x] - 128 * c)
                        last = mm(PS[:, 4 + p, 0:D], hid_b[x][0:rows_, SB * c:SB * (c + 1)],
                                  wbuf[p][0:rows_, o_ + D * c:o_ + D * (c + 1)], x == 0 and c == 0, x == 1 and c == n_c - 1)
                    last.then_inc(sem("downd"), 1)

                def emit(b, hb, p, first=False, last=False):
                    up(b, hb, p, 0)
                    if not first:
                        down(b - 1, 1 - p, 1)
                    if not last:
                        x_transposes(b + 1, hb + p, 1 - p)
                    up(b, hb, p, 1)
                    down(b, p, 0)

                x_transposes(0, 0, 0)
                emit(0, 0, 0, first=True)
                with pe.Fori(0, (nb - 2) // 2) as i:
                    emit(2 * i + 1, i, 1)
                    emit(2 * i + 2, i + 1, 0)
                if nb % 2:
                    emit(nb - 2, (nb - 2) // 2, 1)
                emit(nb - 1, (nb - 1) // 2, (nb - 1) % 2, last=True)
                down(nb - 1, (nb - 1) % 2, 1)

            def residual_tiles(n_acc):
                for j in range(NT):
                    if j % 3 == 0:
                        pe.wait_ge(sem("yt_ready"), 2 * (n_acc - 1) + 1 + j // 3)
                    for d in range(KD):
                        last = nc.tensor.transpose(PS[0:TT, 4 + j // 2, (j % 2) * D + 128 * d:(j % 2) * D + 128 * (d + 1)],
                                                   YT[:, d, tsl(j)], ident[:, :])
                    last.then_inc(sem("tm_ready"), 1)

            def shared(name, widths):
                n = SHN[name]
                f = sum(widths)
                steps = len(widths)

                def up(h, c):
                    i = n + steps * h + c
                    if c >= 2 or h:
                        pe.wait_ge(sem("shid"), i - 1)
                    for v_ in range(2):
                        for k in range(KD):
                            o_ = (v_ * KD + k) * f + 128 * c
                            last = mm(PS[:, 4 + 2 * (i % 2) + v_, 0:TH], wsh[:, o_:o_ + 128], XT[:, k, hsl(h)],
                                      k == 0, k == KD - 1)
                    last.then_inc(sem("sup"), 1)

                def down(h, c):
                    i = n + steps * h + c
                    pe.wait_ge(sem("shid"), i + 1)
                    if h and c == 0:
                        pe.wait_ge(sem("yt_ready"), 2 * (STAGE[name] - 1) + 1)
                    for d in range(KD):
                        o_ = 2 * KD * f + D * c + 128 * d
                        last = mm(PS[:, d, 0:TH], wsh[0:widths[c], o_:o_ + 128], shid[0:widths[c], i % 2, :],
                                  c == 0, c == steps - 1)
                    last.then_inc(sem("sdown"), 1)

                order = [(h, c) for h in range(2) for c in range(steps)]
                up(*order[0])
                for a_, b_ in zip(order, order[1:] + [None]):
                    if b_:
                        up(*b_)
                    down(*a_)
                residual_tiles(STAGE[name])

            def token_products(name, tiles_of, n_k, rhs, pre=None):
                s = SUB[name]
                for j in range(NT):
                    for k in range(n_k):
                        last = mm(TM(j), tiles_of(k, j), rhs(k), k == 0, k == n_k - 1)
                    last.then_inc(sem("tm_ready"), 1)

            def tsl(j):
                return slice(TT * j, TT * (j + 1))

            def hsl(h):
                return slice(TH * h, TH * (h + 1))

            pe.wait_ge(sem("ld_patch"), 16 * 2 * PATCH_K)
            token_products("attn0", lambda k, j: patch_s[:, k, tsl(j)], PATCH_K, lambda k: wtok_s[:, k, :])

            pe.wait_ge(sem("ld_const"), 16 * 6)
            transpose_x("attn0")
            pe.wait_ge(sem("ld_rnn"), 32)
            pe.wait_ge(sem("xt_ready"), 2)
            for m in range(KD):
                for lh in range(2):
                    for k in range(KD):
                        xv = XT[:, k, :].rearrange("p (b l) -> p l b", l=L)[:, 18 * lh:18 * (lh + 1), :]
                        last = mm(PS[:, 4 + 2 * lh + m, 0:TH], wrnn_s[:, 1, k, 128 * m:128 * (m + 1)], xv, k == 0, False)
            last.then_inc(sem("rnn_x"), 1)
            HNv = HN[:, :, :].rearrange("p k (b l) -> p k b l", l=L)

            def rnn_step(lh, at, t_prev):
                for m in range(KD):
                    for k in range(KD):
                        last = mm(PS[:, 4 + 2 * lh + m, bass.ds(at, NB)], wrnn_s[:, 0, k, 128 * m:128 * (m + 1)],
                                  HNv[:, k, :, bass.ds(t_prev, 1)], False, False)
                return last

            with pe.Fori(1, 18) as t:
                pe.wait_ge(sem("rnn_h"), t)
                rnn_step(0, t * NB, t - 1).then_inc(sem("rnn_z"), 1)
            with pe.Fori(18, 36) as t:
                pe.wait_ge(sem("rnn_h"), t)
                rnn_step(1, t * NB - 18 * NB, t - 1).then_inc(sem("rnn_z"), 1)
            pe.wait_ge(sem("rnn_h"), L)
            token_products("attn0", lambda k, j: HN[:, k, tsl(j)], KD, lambda k: wrnn_s[:, 2, k, :])

            transpose_x("ffn0")
            gate_logits("ffn0")
            ranks("ffn0")
            pe.wait_ge(sem("comb_ready"), 1)
            for j in range(NT):
                last = nc.tensor.transpose(PS[0:E, j // 3, TT * (j % 3):TT * (j % 3 + 1)], comb[:, j, :],
                                           ident[0:TT, 0:TT])
            last.then_inc(sem("combT_psum"), 1)
            pe.wait_ge(sem("combT_ready"), 1)
            for j in range(NT):
                mm(TM(j), combT[:, tsl(j)], b20_s[:, :]).then_inc(sem("tm_ready"), 1)
            pe.wait_ge(sem("side_added"), 1)
            routed("ffn0")

            transpose_x("attn1")
            pe.wait_ge(sem("ld_l1a"), 64)
            pe.wait_ge(sem("xt_ready"), 2 * SUB["attn1"] + 2)
            for m in range(2 * KD):
                for h in range(2):
                    for k in range(KD):
                        last = mm(PS[:, 4 + 2 * (m % 2) + h, 0:TH], win_s[:, k, 128 * m:128 * (m + 1)], XT[:, k, hsl(h)],
                                  k == 0, k == KD - 1)
                last.then_inc(sem("xz_psum"), 1)
                if m == 1:
                    pe.wait_ge(sem("xz_read"), 2)
            for h in range(2):
                for k in range(KD):
                    last = mm(PS[0:2 * NS, h, 0:TH], wx_s[:, k, D:D + 2 * NS], xs[:, k, hsl(h)], k == 0, k == KD - 1)
            last.then_inc(sem("bc_psum"), 1)
            pe.wait_ge(sem("xz_read"), 4)
            for m in range(KD):
                for h in range(2):
                    for k in range(KD):
                        last = mm(PS[:, 4 + 2 * h + m, 0:TH], wx_s[:, k, 128 * m:128 * (m + 1)], xs[:, k, hsl(h)],
                                  k == 0, k == KD - 1)
            last.then_inc(sem("dr_psum"), 1)
            pe.wait_ge(sem("dr_ready"), 2)
            for m in range(KD):
                for h in range(2):
                    for k in range(KD):
                        last = mm(PS[:, 4 + 2 * h + m, 0:TH], wdt_s[:, k, 128 * m:128 * (m + 1)], dr[:, k, hsl(h)],
                                  k == 0, k == KD - 1)
            last.then_inc(sem("dt_psum"), 1)
            pe.wait_ge(sem("bc_rows"), 2)
            pe.wait_ge(sem("diag_ready"), 1)
            for h in range(2):
                for d in range(KD):
                    mm(CM(d, h), diagD[:, d, :], xs[:, d, hsl(h)], True, False)
            pe.sem_inc(sem("hc_read"), 2)
            with pe.Fori(0, NS // 2) as i:
                for n in range(2):
                    pe.wait_ge(sem("hc_done"), 2 * i + (n + 1))
                    for h in range(2):
                        for d in range(KD):
                            last = mm(CM(d, h), ident[:, :], hC[:, n, d, hsl(h)], False, False)
                    last.then_inc(sem("hc_read"), 1)
            pe.wait_ge(sem("ys_ready"), 1)
            token_products("attn1", lambda k, j: ys[:, k, tsl(j)], KD, lambda k: wout_s[:, k, :])

            transpose_x("ffn1")
            gate_logits("ffn1")
            pe.wait_ge(sem("comb_ready"), GATES["ffn1"] + 1)
            for j in range(NT):
                last = nc.tensor.transpose(PS[0:E, j // 3, TT * (j % 3):TT * (j % 3 + 1)], comb[:, j, :],
                                           ident[0:TT, 0:TT])
            last.then_inc(sem("combT_psum"), 1)
            pe.wait_ge(sem("combT_ready"), GATES["ffn1"] + 1)
            pe.wait_ge(sem("ld_l1f"), 32)
            for j in range(NT):
                last = mm(TM(j), combT[:, tsl(j)], be2_s[:, :])
                last.then_inc(sem("tm_ready"), 1)
            def first_products(e):
                for q in range(NT // 2):
                    if e:
                        pe.wait_ge(sem("e1_n1"), 3 * (e - 1) + q + 1)
                    for j in (2 * q, 2 * q + 1):
                        z = PS[0:TT, q, (j % 2) * D:(j % 2 + 1) * D]
                        mm(z, ones3[:, :], bias_p[:, e * D:(e + 1) * D], True, False)
                        for k in range(KD):
                            last = mm(z, XT[:, k, tsl(j)], wl1_s[:, 0, e, k, :], False, k == KD - 1)
                    last.then_inc(sem("e1_z1"), 1)

            def n1_transposes(e):
                for q in range(NT // 2):
                    i = 3 * e + q
                    pe.wait_ge(sem("e1_n1"), i + 1)
                    if i >= 2:
                        pe.wait_ge(sem("e1_h"), i - 1)
                    for d in range(KD):
                        for j in (2 * q, 2 * q + 1):
                            last = nc.tensor.transpose(PS[:, 3 + 4 * (i % 2), (2 * d + j % 2) * TT:(2 * d + j % 2 + 1) * TT],
                                                       n1[0:TT, j, 128 * d:128 * (d + 1)], ident[0:TT, 0:TT])
                    last.then_inc(sem("e1_t"), 1)

            def second_products(e):
                for q in range(NT // 2):
                    pe.wait_ge(sem("e1_h"), 3 * e + q + 1)
                    if e:
                        pe.wait_ge(sem("e1_u"), 3 * (e - 1) + q + 1)
                    for j in (2 * q, 2 * q + 1):
                        z = PS[0:TT, 4 + q, (j % 2) * D:(j % 2 + 1) * D]
                        mm(z, ones3[:, :], bias_p[:, (E1 + e) * D:(E1 + e + 1) * D], True, False)
                        for k in range(KD):
                            last = mm(z, n1T[:, k, tsl(j)], wl1_s[:, 1, e, k, :], False, k == KD - 1)
                    last.then_inc(sem("e1_z2"), 1)

            pe.wait_ge(sem("bias_ready"), 1)
            for e in range(E1 + 1):
                if e < E1:
                    first_products(e)
                if e:
                    second_products(e - 1)
                if e < E1:
                    n1_transposes(e)

            transpose_x("attn2")
            pe.wait_ge(sem("ld_l2a"), 48)
            pe.wait_ge(sem("xt_ready"), 2 * SUB["attn2"] + 2)
            for m in range(2 * KI):
                if m >= 4:
                    pe.wait_ge(sem("up_read"), m - 3)
                for h in range(2):
                    for k in range(KD):
                        last = mm(PS[:, 2 * (m % 4) + h, 0:TH], wup_s[:, k, 128 * m:128 * (m + 1)], XT[:, k, hsl(h)],
                                  k == 0, k == KD - 1)
                last.then_inc(sem("up_psum"), 1)
            pe.wait_ge(sem("up_read"), 2 * KI)
            for m in range(KI):
                pe.wait_ge(sem("ac_ready"), m + 1)
                if m >= 1:
                    pe.wait_ge(sem("gates_read"), m)
                for g in range(3):
                    for h in range(2):
                        last = mm(PS[:, 2 * g + h, 0:TH], wg_s[:, g, m, :], ac[:, m, hsl(h)])
                last.then_inc(sem("gates_psum"), 1)
            pe.wait_ge(sem("h2_ready"), KI)
            token_products("attn2", lambda k, j: xm[:, k, tsl(j)], KI, lambda k: wdn_s[:, k, :])

            transpose_x("ffn2")
            gate_logits("ffn2")
            ranks("ffn2")
            pe.wait_ge(sem("ld_sh2"), 16)
            shared("ffn2", [128] * CS)
            pe.wait_ge(sem("side_added"), 2)
            routed("ffn2")

            transpose_x("attn3")
            pe.wait_ge(sem("ld_lru"), 32)
            pe.wait_ge(sem("xt_ready"), 2 * SUB["attn3"] + 2)
            for v in range(2):
                for h in range(2):
                    for k in range(KD):
                        last = mm(PS[:, 4 + 2 * v + h, 0:TH], wlru_s[:, v, 128 * k:128 * (k + 1)], XT[:, k, hsl(h)],
                                  k == 0, k == KD - 1)
            last.then_inc(sem("u_psum"), 1)
            pe.wait_ge(sem("s_ready"), 2)
            for j in range(NT):
                mm(TM(j), lt[8][:, tsl(j)], wlru_s[:, 2, :], True, False)
                mm(TM(j), lt[9][:, tsl(j)], wlru_s[:, 3, :], False, False)
                for k in range(KD):
                    last = mm(TM(j), XT[:, k, tsl(j)], wlruD_s[:, k, :], False, k == KD - 1)
                last.then_inc(sem("tm_ready"), 1)

            transpose_x("ffn3")
            gate_logits("ffn3")
            ranks("ffn3")
            pe.wait_ge(sem("ld_sh3"), 16)
            shared("ffn3", [128] * (CH2 - 1) + [64])
            pe.wait_ge(sem("side_added"), 3)
            routed("ffn3")

        @block.scalar
        def _(act):
            def xt_copy(name, scale=None):
                s = SUB[name]
                for h in range(2):
                    act.wait_ge(sem("xt_psum"), 2 * s + h + 1)
                    if scale is None:
                        nc.scalar.activation(XT[:, :, TH * h:TH * (h + 1)], PS[:, 2 * h:2 * h + 2, 0:TH], ACT.Copy)\
                            .then_inc(sem("xt_ready"), 1)
                    else:
                        for d in range(KD):
                            last = nc.scalar.activation(XT[:, d, TH * h:TH * (h + 1)], CM(d, h), ACT.Copy,
                                                        scale=col(scale, d))
                        last.then_inc(sem("xt_ready"), 1)

            def gate_exp(name, with_comb):
                g = GATES[name]
                act.wait_ge(sem("gate_shifted"), g + 1)
                nc.scalar.activation(ge[:, :, :], gl[:, :, :], ACT.Exp).then_inc(sem("gate_exp"), 1)
                if with_comb:
                    act.wait_ge(sem("combT_psum"), g + 1)
                    nc.scalar.activation(combT[:, :].rearrange("p (h t) -> p h t", h=2), PS[0:E, 0:2, 0:TH], ACT.Copy)\
                        .then_inc(sem("combT_ready"), 1)

            def routed(name):
                at, nb = BLK0[name], NBLK[name]
                two_in = name != "ffn0"

                def x_copy(b, p):
                    act.wait_ge(sem("xt_t"), b + (at + 1))
                    if two_in:
                        nc.scalar.activation(xbT[p], PS[:, 6 + p, 0:KD * SB].rearrange("p (k s) -> p k s", k=KD), ACT.Copy)\
                            .then_inc(sem("xbT"), 1)
                    else:
                        for d in range(KD):
                            last = nc.scalar.activation(xbT[p][:, d, :], PS[:, 6 + p, SB * d:SB * (d + 1)], ACT.Copy,
                                                        scale=col("rms_w", d))
                        last.then_inc(sem("xbT"), 1)

                def silu(b, p, x):
                    act.wait_ge(sem("upd"), 2 * b + (2 * at + x + 1))
                    if two_in:
                        nc.scalar.activation(sg_s[x][:, 0:3 * SB], PS[:, 2 * x, 0:3 * SB], ACT.Silu)\
                            .then_inc(sem("silu2"), 1)
                    else:
                        o_ = sum(HLEN[name][:x]) + HLEN[name][x] - HC[name][x]
                        for c in range(HC[name][x]):
                            last = nc.scalar.activation(hid_b[x][:, SB * c:SB * (c + 1)], PS[:, 2 * x, SB * c:SB * (c + 1)],
                                                        ACT.Silu, bias=wbuf[p][:, o_ + c:o_ + c + 1])
                        last.then_inc(sem("hid2"), 1)

                def y_copy(b, hb, p):
                    act.wait_ge(sem("downd"), 2 * b + (2 * at + 2))
                    act.wait_ge(sem(f"y{p}"), 16 * hb + 16 * (USE0[name][p] + 1))
                    nc.scalar.activation(y_s[p], PS[:, 4 + p, 0:D], ACT.Copy).then_inc(sem("y_sb"), 1)

                def emit(b, hb, p, first=False, last=False):
                    silu(b, p, 0)
                    if not first:
                        y_copy(b - 1, hb - 1 + p, 1 - p)
                    if not last:
                        x_copy(b + 1, 1 - p)
                    silu(b, p, 1)

                x_copy(0, 0)
                emit(0, 0, 0, first=True)
                with act.Fori(0, (nb - 2) // 2) as i:
                    emit(2 * i + 1, i, 1)
                    emit(2 * i + 2, i + 1, 0)
                if nb % 2:
                    emit(nb - 2, (nb - 2) // 2, 1)
                emit(nb - 1, (nb - 1) // 2, (nb - 1) % 2, last=True)
                y_copy(nb - 1, (nb - 1) // 2, (nb - 1) % 2)

            def shared(name, steps):
                for i in range(SHN[name], SHN[name] + 2 * steps):
                    act.wait_ge(sem("sup"), i + 1)
                    if i >= 2:
                        act.wait_ge(sem("shid"), i - 1)
                    nc.scalar.activation(sact[:, i % 2, :], PS[:, 4 + 2 * (i % 2), 0:TH], ACT.Silu).then_inc(sem("ssilu"), 1)
                    if (i - SHN[name]) % steps == steps - 1:
                        h = (i - SHN[name]) // steps
                        act.wait_ge(sem("sdown"), i + 1)
                        nc.scalar.activation(YT[:, :, TH * h:TH * (h + 1)], PS[:, 0:2, 0:TH], ACT.Copy)\
                            .then_inc(sem("yt_ready"), 1)

            act.wait_ge(sem("ld_const"), 16 * 6)
            nc.scalar.activation(lru_c[:, 0:1], col("nu"), ACT.Exp).then_inc(sem("lru_a"), 1)
            nc.scalar.activation(lru_c[:, 2:3], col("theta"), ACT.Exp).then_inc(sem("lru_a"), 1)
            nc.scalar.activation(lru_c[:, 3:4], col("gamma"), ACT.Exp).then_inc(sem("lru_a"), 1)
            act.wait_ge(sem("lru_a"), 3)
            nc.scalar.activation(lru_c[:, 1:2], lru_c[:, 0:1], ACT.Exp, scale=-1.0).then_inc(sem("lru_b"), 1)
            act.wait_ge(sem("lru_reduced"), 1)
            nc.scalar.activation(sinT[:, 1:2], lru_c[:, 6:7], ACT.Sin).then_inc(sem("lru_sc"), 1)
            nc.scalar.activation(cosT[:, 1:2], lru_c[:, 7:8], ACT.Sin).then_inc(sem("lru_sc"), 1)

            xt_copy("attn0")
            HNv = HN[:, :, :].rearrange("p k (b l) -> p k b l", l=L)
            act.wait_ge(sem("rnn_x"), 1)
            nc.scalar.activation(HNv[:, :, :, 0:1], PS[:, 4:6, 0:NB], ACT.Tanh).then_inc(sem("rnn_h"), 1)
            with act.Fori(1, 18) as t:
                act.wait_ge(sem("rnn_z"), t)
                act.wait_ge(sem("rnn_x"), 1)
                nc.scalar.activation(HNv[:, :, :, bass.ds(t, 1)], PS[:, 4:6, bass.ds(t * NB, NB)], ACT.Tanh)\
                    .then_inc(sem("rnn_h"), 1)
            with act.Fori(18, 36) as t:
                act.wait_ge(sem("rnn_z"), t)
                act.wait_ge(sem("rnn_x"), 1)
                nc.scalar.activation(HNv[:, :, :, bass.ds(t, 1)], PS[:, 6:8, bass.ds(t * NB - 18 * NB, NB)], ACT.Tanh)\
                    .then_inc(sem("rnn_h"), 1)

            xt_copy("ffn0", "rms_w")
            gate_exp("ffn0", True)
            act.sem_inc(sem("y_sb"), 2)
            act.sem_inc(sem("y0"), 16)
            act.sem_inc(sem("y1"), 16)
            routed("ffn0")

            xt_copy("attn1")
            for m in range(4):
                act.wait_ge(sem("xz_psum"), m + 1)
                b = 4 + 2 * (m % 2)
                dst = xs[:, m, :] if m < 2 else zs[:, m - 2, :]
                nc.scalar.activation(dst.rearrange("p (h t) -> p h t", h=2), PS[:, b:b + 2, 0:TH],
                                     ACT.Copy if m < 2 else ACT.Silu).then_inc(sem("xz_read"), 1)
            act.wait_ge(sem("bc_psum"), 1)
            for h in range(2):
                nc.scalar.activation(bc_s[0:2 * NS, TH * h:TH * (h + 1)], PS[0:2 * NS, h, 0:TH], ACT.Copy)\
                    .then_inc(sem("bc_rows"), 1)
            act.wait_ge(sem("dr_psum"), 1)
            for h in range(2):
                nc.scalar.activation(dr[:, :, TH * h:TH * (h + 1)], PS[:, 4 + 2 * h:6 + 2 * h, 0:TH], ACT.Copy)\
                    .then_inc(sem("dr_ready"), 1)
            nc.scalar.activation(A_s[:, :, :], colv[:, COL["A_log"]:COL["A_log"] + KD * NS]
                                 .rearrange("p (k n) -> p k n", k=KD), ACT.Exp).then_inc(sem("A_exp"), 1)
            act.wait_ge(sem("dt_biased"), 1)
            nc.scalar.activation(hs_[:, 0], dr[:, :, :], ACT.Abs).then_inc(sem("dt_abs"), 1)
            act.wait_ge(sem("dt_abs"), 1)
            nc.scalar.activation(dA[:, 0], hs_[:, 0], ACT.Exp, scale=-1.0).then_inc(sem("dt_e"), 1)
            act.wait_ge(sem("delta_ready"), 1)
            with act.Fori(0, NS // 2) as i:
                for n in range(2):
                    act.wait_ge(sem("scan_credit"), 2 * i + (n + 1))
                    for d in range(KD):
                        act.wait_ge(sem("delta_ready"), 1)
                        last = nc.scalar.activation(dA[:, n, d, :], dl[:, d, :], ACT.Exp,
                                                    scale=A_s[:, d, bass.ds(2 * i + n, 1)])
                    last.then_inc(sem("dA_ready"), 1)

            xt_copy("ffn1")
            gate_exp("ffn1", True)
            for e in range(E1 + 1):
                if e < E1:
                    act.wait_ge(sem("e1_r1"), e + 1)
                    for j in range(NT):
                        if e:
                            act.wait_ge(sem("e1_t"), 3 * e)
                        ins = nc.scalar.activation(n1[0:TT, j, :], PS[0:TT, j // 2, (j % 2) * D:(j % 2 + 1) * D],
                                                   ACT.Identity, bias=nmr1[:, j:j + 1], scale=r1[:, j:j + 1])
                        if j % 2:
                            ins.then_inc(sem("e1_n1"), 1)
                    for q in range(NT // 2):
                        i = 3 * e + q
                        act.wait_ge(sem("e1_t"), i + 1)
                        if e:
                            act.wait_ge(sem("e1_z2"), 3 * e)
                        for d in range(KD):
                            last = nc.scalar.activation(n1T[:, d, 2 * TT * q:2 * TT * (q + 1)],
                                                        PS[:, 3 + 4 * (i % 2), 2 * TT * d:2 * TT * (d + 1)], ACT.Relu,
                                                        bias=col("be1", e * KD + d), scale=col("g1", e * KD + d))
                        last.then_inc(sem("e1_h"), 1)
                if e:
                    f = e - 1
                    act.wait_ge(sem("e1_r2"), f + 1)
                    for j in range(NT):
                        if f >= 2:
                            act.wait_ge(sem("e1_add"), 3 * (f - 2) + j // 2 + 1)
                        ins = nc.scalar.activation(eu[0:TT, f % 2, j, :], PS[0:TT, 4 + j // 2, (j % 2) * D:(j % 2 + 1) * D],
                                                   ACT.Identity, bias=nmr2[:, j:j + 1], scale=r2[:, j:j + 1])
                        if j % 2:
                            ins.then_inc(sem("e1_u"), 1)

            xt_copy("attn2")
            for m in range(2 * KI):
                act.wait_ge(sem("up_psum"), m + 1)
                b = 2 * (m % 4)
                dst = xm[:, m, :] if m < KI else zz[:, m - KI, :]
                nc.scalar.activation(dst.rearrange("p (h t) -> p h t", h=2), PS[:, b:b + 2, 0:TH],
                                     ACT.Identity if m < KI else ACT.Silu, bias=col("b_up", m)).then_inc(sem("up_read"), 1)
            for m in range(KI):
                act.wait_ge(sem("conv_ready"), m + 1)
                nc.scalar.activation(ac[:, m, :], df[:, m, :], ACT.Silu).then_inc(sem("ac_ready"), 1)

            def two(x):
                return x.rearrange("p (h t) -> p h t", h=2)

            for m in range(KI):
                act.wait_ge(sem("gates_psum"), m + 1)
                if m >= 1:
                    act.wait_ge(sem("diff_ready"), m)
                    act.wait_ge(sem("scan2_done"), m)
                for g in range(2):
                    nc.scalar.activation(two(ws[g]), PS[:, 2 * g:2 * g + 2, 0:TH], ACT.Abs).then_inc(sem("g_abs"), 1)
                for g in range(2):
                    act.wait_ge(sem("g_abs"), 2 * m + g + 1)
                    nc.scalar.activation(ws[2 + g], ws[g], ACT.Exp, scale=-1.0).then_inc(sem("g_exp"), 1)
                for g in range(2):
                    act.wait_ge(sem("g_exp"), 2 * m + g + 1)
                    nc.scalar.activation(ws[g], ws[2 + g], ACT.Ln, bias=1.0).then_inc(sem("g_ln"), 1)
                act.wait_ge(sem("diff_ready"), m + 1)
                nc.scalar.activation(ws[2], df[:, m, :], ACT.Sigmoid, scale=-1.0).then_inc(sem("sig"), 1)
                nc.scalar.activation(ws[3], df[:, m, :], ACT.Sigmoid).then_inc(sem("sig"), 1)
                nc.scalar.activation(two(ws[4]), PS[:, 4:6, 0:TH], ACT.Sigmoid).then_inc(sem("sig"), 1)

            xt_copy("ffn2")
            gate_exp("ffn2", False)
            shared("ffn2", CS)
            routed("ffn2")
            xt_copy("attn3")
            xt_copy("ffn3")
            gate_exp("ffn3", False)
            shared("ffn3", CH2)
            routed("ffn3")

        @block.gpsimd
        def _(pool):
            nc.gpsimd.iota(iota8[:, :], pattern=[[1, E]], base=0, channel_multiplier=0).then_inc(sem("iota"), 1)
            nc.gpsimd.memset(ones3[:, :], 1.0).then_inc(sem("pool_const"), 1)
            nc.gpsimd.memset(zrow[:, :], 0.0).then_inc(sem("pool_const"), 1)
            nc.gpsimd.iota(iob[:, :], pattern=[[1, MAXB]], base=0, channel_multiplier=0).then_inc(sem("iota"), 1)

            def dispatch(name, choices):
                s = STAGE[name]
                pool.wait_ge(sem("pos_ready"), s + 1)
                if s == 0:
                    pool.wait_ge(sem("slots_zero"), 16 * MAXB)
                for k in range(choices):
                    for j in range(NT):
                        pool.indirect_dma_start(x_slots, bass.IndirectOffsetOnAxis(ap=posu[:, k, j:j + 1], axis=0),
                                                XH[:, j, :], None).then_inc(sem("scattered"), 16)

            def collect(name, choices):
                s = STAGE[name]
                for p in range(2):
                    last = USE0[name][p] + (NBLK[name] + 1 - p) // 2
                    pool.wait_ge(sem(f"y{p}"), 16 * (last + 1))
                for j in range(NT):
                    for k in range(choices):
                        pool.indirect_dma_start(Yg[0:TT, k, j * D:(j + 1) * D], None, y_slots[0:SB * NBLK[name], :],
                                                bass.IndirectOffsetOnAxis(ap=posu[:, k, j:j + 1], axis=0))\
                            .then_inc(sem(f"row{k}{j}"), 16)

            dispatch("ffn0", 1)
            collect("ffn0", 1)
            with pool.Fori(0, NS // 2) as i:
                for n in range(2):
                    pool.wait_ge(sem("scan_done"), 2 * i + (n + 1))
                    pool.wait_ge(sem("hc_read"), 2 * i + (n + 1))
                    pool.wait_ge(sem(f"bc_spread{n}"), 32 * i + 32)
                    nc.gpsimd.tensor_tensor(hC[:, n, :, :], hs_[:, n, :, :],
                                            bcC[:, n:n + 1, :].to_broadcast([128, KD, T]), ALU.mult)\
                        .then_inc(sem("hc_done"), 1)
            for e in range(E1):
                for q in range(NT // 2):
                    pool.wait_ge(sem("e1_u"), 3 * e + q + 1)
                    u = eu[0:TT, e % 2, 2 * q:2 * q + 2, :]
                    nc.gpsimd.tensor_tensor(u, u, row("g2", D, e)[:, None, :].to_broadcast([TT, 2, D]), ALU.mult)\
                        .then_inc(sem("e1_ug"), 1)
            dispatch("ffn2", 2)
            collect("ffn2", 2)
            dispatch("ffn3", 2)
            collect("ffn3", 2)

        @block.vector
        def _(dve):
            v = nc.vector
            chain = [0]

            def link(ins):
                chain[0] += 1
                ins.then_inc(sem("dve_step"), 1)
                dve.wait_ge(sem("dve_step"), chain[0])

            def mark(ins):
                chain[0] += 1
                ins.then_inc(sem("dve_step"), 1)

            def join():
                dve.wait_ge(sem("dve_step"), chain[0])

            def tile_in(before, j):
                dve.wait_ge(sem("tm_ready"), before + 2 * (j // 2) + 2)

            def rsqrt(dst, var, eps):
                x, y, a = rs[:, :, 0], rs[:, :, 1], rs[:, :, 2]
                link(v.tensor_scalar(x, var, eps, None, ALU.add))
                link(v.tensor_scalar(rs_i[:, :], rs[:, :, 0].bitcast(I32), 1, None, ALU.logical_shift_right))
                link(v.tensor_scalar(y.bitcast(I32), rs_i[:, :], -1.0, 1597463007.0, ALU.mult, ALU.add))
                for n in range(3):
                    link(v.tensor_tensor(a, y, y, ALU.mult))
                    link(v.scalar_tensor_tensor(a, a, -0.5, x, ALU.mult, ALU.mult))
                    link(v.scalar_tensor_tensor(dst if n == 2 else y, a, 1.5, y, ALU.add, ALU.mult))

            def tile_stats(src, j):
                v_in = src
                link(v.bn_stats(stats[:, j, :], v_in))
                mark(v.bn_aggr(mv[:, j, :], stats[:, j, :]))

            RSTD = rs[:, :, 3]

            def norm_to_xh(rstd=None):
                for j in range(NT):
                    v.tensor_scalar(XH[:, j, :], H[:, j, :], mv[:, j, 0:1], rs[:, j, 3:4], ALU.subtract, ALU.mult)\
                        .then_inc(sem("xh_ready"), 1)

            def layer_norm_h():
                join()
                rsqrt(RSTD, mv[:, :, 1], LN_EPS)
                norm_to_xh()

            def gates(name, second, over_chosen, bias=None):
                g = GATES[name]
                if g == 0:
                    dve.wait_ge(sem("iota"), 2)
                    mark(v.tensor_copy(iota8f[:, :], iota8[:, :]))
                    mark(v.tensor_copy(iobf[:, :], iob[:, :]))
                dve.wait_ge(sem("logits"), g + 1)
                lp = PS[0:TT, 3, 0:NT * E].rearrange("p (j e) -> p j e", e=E)
                if bias is None:
                    mark(v.tensor_copy(gl[:, :, :], lp))
                else:
                    mark(v.tensor_tensor(gl[:, :, :], lp, row(bias, E)[:, None, :].to_broadcast([TT, NT, E]), ALU.add))
                join()
                for j in range(NT):
                    mark(v.max(gm[:, j, :], gl[:, j, :]))
                join()
                for j in range(NT):
                    mark(v.max_index(gi[:, j, :], gm[:, j, :], gl[:, j, :]))
                join()
                v.tensor_tensor(gl[:, :, :], gl[:, :, :], gm[:, :, 0:1].to_broadcast([TT, NT, E]), ALU.subtract)\
                    .then_inc(sem("gate_shifted"), 1)
                link(v.tensor_copy(gf[:, :, :], gi[:, :, :]))
                io = iota8f[:, :, None].to_broadcast([TT, E, NT])
                for k in range(2 if second else 1):
                    mark(v.tensor_tensor(msk[:, k], io, gf[:, None, :, k].to_broadcast([TT, E, NT]), ALU.is_equal))
                join()
                if second:
                    ins = v.tensor_tensor(mks[:, :, :], msk[:, 0], msk[:, 1], ALU.add)
                else:
                    ins = v.tensor_copy(mks[:, :, :], msk[:, 0])
                if name in STAGE:
                    ins.then_inc(sem("masks"), 1)
                else:
                    link(ins)

            def weights(name, second, over_chosen, with_comb):
                g = GATES[name]
                dve.wait_ge(sem("gate_exp"), g + 1)
                dve.wait_ge(sem("masks"), STAGE[name] + 1) if name in STAGE else None
                mkt = mks[:, :, :].rearrange("p e j -> p j e")
                link(v.tensor_tensor(gk[:, :, :], mkt, ge[:, :, :], ALU.mult))
                link(v.tensor_reduce(gs[:, :], (gk if over_chosen else ge)[:, :, :], AX.X, ALU.add))
                link(v.reciprocal(gs[:, :], gs[:, :]))
                if with_comb:
                    v.tensor_tensor(comb[:, :, :], gk[:, :, :], gs[:, :, None].to_broadcast([TT, NT, E]), ALU.mult)\
                        .then_inc(sem("comb_ready"), 1)
                if name in STAGE:
                    if with_comb:
                        dve.wait_ge(sem("comb_ready"), g + 1)
                    for k in range(2 if second else 1):
                        link(v.tensor_tensor(gk[:, :, :], msk[:, k].rearrange("p e j -> p j e"), ge[:, :, :], ALU.mult))
                        link(v.tensor_reduce(wgt[:, k, :], gk[:, :, :], AX.X, ALU.add))
                        link(v.tensor_tensor(wgt[:, k, :], wgt[:, k, :], gs[:, :], ALU.mult))

            def places(name, second):
                s = STAGE[name]
                nk = 2 if second else 1
                dve.wait_ge(sem("ranks"), s + 1)
                ej = lambda x: x.rearrange("p (e j) -> p e j", j=NT)
                link(v.tensor_copy(cnt[:, :, :], ej(PS[0:TT, 3, 128:128 + E * NT])))
                flat = lambda x: x.rearrange("p e j -> p (e j)")
                link(v.tensor_tensor_scan(flat(pre[:, :, :]), tri[:, 2, 0:E * NT], flat(cnt[:, :, :]), 0.0, ALU.mult,
                                          ALU.add))
                n_, incl, excl = nblk[:, 0, :], nblk[:, 1, :], nblk[:, 2, :]
                link(v.tensor_scalar(n_, pre[:, :, NT - 1], 1.0 / SB, (SB - 1) / SB - 0.5 + 0.5 / SB, ALU.mult, ALU.add))
                link(v.tensor_scalar(n_, n_, ROUND_MAGIC, None, ALU.add))
                link(v.tensor_scalar(n_, n_, -ROUND_MAGIC, None, ALU.add))
                link(v.tensor_tensor_scan(incl, tri[:, 1, 0:E], n_, 0.0, ALU.mult, ALU.add))
                mark(v.tensor_tensor(eid_f[:, :, :], iobf[:, :, None].to_broadcast([1, MAXB, E]),
                                     nblk[0:1, 1:2, :].to_broadcast([1, MAXB, E]), ALU.is_ge))
                mark(v.tensor_tensor(excl, incl, n_, ALU.subtract))
                mark(v.tensor_tensor(pre[:, :, :], pre[:, :, :], cnt[:, :, :], ALU.subtract))
                join()
                mark(v.tensor_reduce(eid_s[:, :], eid_f[:, :, :], AX.X, ALU.add))
                mark(v.tensor_tensor(pre[:, :, :], pre[:, :, :], ej(PS[0:TT, 3, 64:64 + E * NT]), ALU.add))
                join()
                v.tensor_scalar(eid[:, :], eid_s[:, :], float(NEXP[name] - 1), None, ALU.min).then_inc(sem("eid_ready"), 1)
                link(v.scalar_tensor_tensor(pre[:, :, :], excl[:, :, None].to_broadcast([TT, E, NT]), float(SB),
                                            pre[:, :, :], ALU.mult, ALU.add))
                for k in range(nk):
                    mark(v.tensor_tensor(posf[:, k], msk[:, k], pre[:, :, :], ALU.mult))
                join()
                for k in range(nk):
                    mark(v.tensor_reduce(pos[:, k, :], posf[:, k].rearrange("p e j -> p j e"), AX.X, ALU.add))
                join()
                v.tensor_copy(posu[:, 0:nk, :], pos[:, 0:nk, :]).then_inc(sem("pos_ready"), 1)

            def side_tiles(tm0, n):
                for j in range(NT):
                    tile_in(tm0, j)
                    ins = v.tensor_tensor(H[:, j, :], H[:, j, :], TM(j), ALU.add)
                    if j < NT - 1:
                        mark(ins)
                    else:
                        ins.then_inc(sem("side_added"), 1)
                join()
                dve.wait_ge(sem("side_added"), n)

            def shared(name, steps):
                for i in range(SHN[name], SHN[name] + 2 * steps):
                    dve.wait_ge(sem("sup"), i + 1)
                    dve.wait_ge(sem("ssilu"), i + 1)
                    if i >= 2:
                        dve.wait_ge(sem("sdown"), i - 1)
                    v.tensor_tensor(shid[:, i % 2, :], sact[:, i % 2, :], PS[:, 5 + 2 * (i % 2), 0:TH], ALU.mult)\
                        .then_inc(sem("shid"), 1)

            def routed(name):
                at, nb = BLK0[name], NBLK[name]

                def emit(b, hb, p):
                    for x in range(2):
                        dve.wait_ge(sem("silu2"), 2 * b + (2 * at + x + 1 - 2 * NBLK["ffn0"]))
                        v.tensor_tensor(hid_b[x][:, 0:3 * SB], sg_s[x][:, 0:3 * SB], PS[:, 2 * x + 1, 0:3 * SB], ALU.mult)\
                            .then_inc(sem("hid2"), 1)

                over_blocks(dve, nb, emit)

            def collect(name, choices, uses, then):
                for j in range(NT):
                    for k in range(choices):
                        dve.wait_ge(sem(f"row{k}{j}"), 16 * uses[k])
                        link_or = v.scalar_tensor_tensor(H[:, j, :], Yg[0:TT, k, j * D:(j + 1) * D], wgt[:, k, j:j + 1],
                                                         H[:, j, :], ALU.mult, ALU.add)
                        if k == choices - 1 and then is None:
                            link_or.then_inc(sem("out_tile"), 1)
                        else:
                            link(link_or)
                    if then:
                        tile_stats(H[:, j, :], j)

            def add_tm(j, tile):
                link(v.tensor_tensor(H[:, j, :], H[:, j, :], TM(j), ALU.add))

            dve.wait_ge(sem("lru_b"), 1)
            c_ = lambda i: lru_c[:, i:i + 1]
            link(v.tensor_scalar(c_(5), c_(2), float(np.pi / 2), None, ALU.add))
            link(v.tensor_copy(c_(4), c_(2)))
            link(v.tensor_scalar(lru_c[:, 8:10], lru_c[:, 4:6], float(1 / (2 * np.pi)), ROUND_MAGIC, ALU.mult, ALU.add))
            link(v.tensor_scalar(lru_c[:, 8:10], lru_c[:, 8:10], -ROUND_MAGIC, None, ALU.add))
            link(v.scalar_tensor_tensor(lru_c[:, 4:6], lru_c[:, 8:10], -TWO_PI_HI, lru_c[:, 4:6], ALU.mult, ALU.add))
            link(v.scalar_tensor_tensor(lru_c[:, 4:6], lru_c[:, 8:10], -TWO_PI_LO, lru_c[:, 4:6], ALU.mult, ALU.add))
            v.tensor_scalar(lru_c[:, 6:8], lru_c[:, 4:6], -3.1415925, 3.1415925, ALU.max, ALU.min)\
                .then_inc(sem("lru_reduced"), 1)
            mark(v.memset(cosT[:, 0:1], 1.0))
            mark(v.memset(sinT[:, 0:1], 0.0))
            join()
            dve.wait_ge(sem("lru_sc"), 2)
            n = 1
            while n < L - 1:
                w = min(n, L - 1 - n)
                cr, si = cosT[:, n:n + 1], sinT[:, n:n + 1]
                C1, S1 = cosT[:, 1:1 + w], sinT[:, 1:1 + w]
                C2, S2 = cosT[:, n + 1:n + 1 + w], sinT[:, n + 1:n + 1 + w]
                mark(v.tensor_scalar(cosg[:, 0:w], S1, si, None, ALU.mult))
                mark(v.tensor_scalar(sing[:, 0:w], S1, cr, None, ALU.mult))
                join()
                mark(v.scalar_tensor_tensor(C2, C1, cr, cosg[:, 0:w], ALU.mult, ALU.subtract))
                mark(v.scalar_tensor_tensor(S2, C1, si, sing[:, 0:w], ALU.mult, ALU.add))
                join()
                n += w
            mark(v.tensor_scalar(cosg[:, :], cosT[:, :], c_(3), None, ALU.mult))
            mark(v.tensor_scalar(sing[:, :], sinT[:, :], c_(3), None, ALU.mult))
            mark(v.tensor_scalar(nsinT[:, :], sinT[:, :], -1.0, None, ALU.mult))
            link(v.memset(lam[:, :], 1.0))
            link(v.memset(lam[:, :].rearrange("p (b l) -> p b l", l=L)[:, :, 0:1], 0.0))
            link(v.tensor_scalar(lam[:, :], lam[:, :], c_(1), None, ALU.mult))

            for j in range(NT):
                tile_in(0, j)
                link(v.tensor_tensor(H[:, j, :], TM(j), row("tok_b"), ALU.add))
                tile_stats(H[:, j, :], j)
            layer_norm_h()

            def normed_residual(tm0, scale_row, shift_row):
                for j in range(NT):
                    mark(v.tensor_tensor(H[:, j, :], H[:, j, :], row(shift_row), ALU.add))
                for j in range(NT):
                    tile_in(tm0, j)
                    link(v.tensor_tensor(TMP[:, j, :], TM(j), XH[:, j, :], ALU.add))
                    tile_stats(TMP[:, j, :], j)
                join()
                rsqrt(RSTD, mv[:, :, 1], LN_EPS)
                for j in range(NT):
                    link(v.scalar_tensor_tensor(TMP[:, j, :], TMP[:, j, :], mv[:, j, 0:1], row(scale_row), ALU.subtract,
                                                ALU.mult))
                    link(v.scalar_tensor_tensor(H[:, j, :], TMP[:, j, :], rs[:, j, 3:4], H[:, j, :], ALU.mult, ALU.add))
                for j in range(NT):
                    tile_stats(H[:, j, :], j)

            dve.wait_ge(sem("ld_const"), 16 * 6)
            bf, bd = bias_f[0], bias_f[1]
            hi, mid = (bias_f[i].bitcast(BF16)[:, 0:NROW - NROW_BC] for i in (2, 3))
            parts = bias_p[:, :]
            part_row = lambda i: ident[0:3, i:i + 1]
            link(v.tensor_copy(hi, bf))
            link(v.tensor_tensor(bd, bf, hi, ALU.subtract))
            link(v.tensor_copy(mid, bd))
            link(v.tensor_tensor(bd, bd, mid, ALU.subtract))
            link(v.tensor_scalar(parts, bd, part_row(2), None, ALU.mult))
            link(v.scalar_tensor_tensor(parts, mid, part_row(1), parts, ALU.mult, ALU.add))
            v.scalar_tensor_tensor(parts, hi, part_row(0), parts, ALU.mult, ALU.add).then_inc(sem("bias_ready"), 1)

            normed_residual(NT, "gamma", "beta")
            join()
            rsqrt(RSTD, mv[:, :, 1], LN_EPS)
            link(v.tensor_tensor(rs[:, :, 4], RSTD, RSTD, ALU.mult))
            link(v.tensor_tensor(rs[:, :, 4], rs[:, :, 4], mv[:, :, 1], ALU.mult))
            rsqrt(rs[:, :, 5], rs[:, :, 4], RMS_EPS)
            link(v.tensor_tensor(RSTD, RSTD, rs[:, :, 5], ALU.mult))
            norm_to_xh()
            gates("ffn0", False, False)
            places("ffn0", False)
            weights("ffn0", False, False, True)
            side_tiles(2 * NT, 1)
            collect("ffn0", 1, (1, 0), True)

            def residual(tm0):
                for j in range(NT):
                    tile_in(tm0, j)
                    add_tm(j, None)
                    tile_stats(H[:, j, :], j)


            layer_norm_h()
            for d in range(KD):
                last = v.tensor_scalar(diagD[:, d, :], ident[:, :], col("D_param", d), None, ALU.mult)
                mark(last)
            join()
            dve.sem_inc(sem("diag_ready"), 1)
            dve.wait_ge(sem("A_exp"), 1)
            link(v.tensor_scalar(A_s[:, :, :], A_s[:, :, :], -1.0, None, ALU.mult))
            dve.wait_ge(sem("dt_psum"), 1)
            for m in range(KD):
                last = v.tensor_scalar(dr[:, m, :].rearrange("p (h t) -> p h t", h=2), PS[:, 4 + m:8:2, 0:TH],
                                       col("b_dt", m), None, ALU.add)
                mark(last)
            join()
            dve.sem_inc(sem("dt_biased"), 1)
            ee, s1, s2, pl = dA[:, 0], dA[:, 1], dBx[:, 0], dBx[:, 1]
            dve.wait_ge(sem("dt_e"), 1)
            link(v.tensor_scalar(s2, ee, 2.0, None, ALU.add))
            link(v.reciprocal(s1, s2))
            link(v.tensor_tensor(s1, s1, ee, ALU.mult))
            link(v.tensor_tensor(s2, s1, s1, ALU.mult))
            link(v.tensor_scalar(pl, s2, ATANH[-1], ATANH[-2], ALU.mult, ALU.add))
            for a in ATANH[-3::-1]:
                link(v.tensor_tensor(pl, pl, s2, ALU.mult))
                link(v.tensor_scalar(pl, pl, a, None, ALU.add))
            link(v.scalar_tensor_tensor(pl, pl, 2.0, s1, ALU.mult, ALU.mult))
            link(v.scalar_tensor_tensor(dl[:, :, :], dr[:, :, :], 0.0, pl, ALU.max, ALU.add))
            link(v.tensor_tensor(dx[:, :, :], dl[:, :, :], xs[:, :, :], ALU.mult))
            dve.sem_inc(sem("delta_ready"), 1)
            dve.sem_inc(sem("scan_credit"), 2)
            with dve.Fori(0, NS // 2) as i:
                for n in range(2):
                    dve.wait_ge(sem(f"bc_spread{n}"), 32 * i + 32)
                    v.tensor_tensor(dBx[:, n, :, :], dx[:, :, :], bcB[:, n:n + 1, :].to_broadcast([128, KD, T]), ALU.mult)\
                        .then_inc(sem("dbx_done"), 1)
                    dve.wait_ge(sem("dA_ready"), 2 * i + (n + 1))
                    v.memset(dA[:, n].rearrange("p k (b l) -> p (k b) l", l=L)[:, :, 0:1], 0.0)\
                        .then_inc(sem("dA_cut"), 1)
                    dve.wait_ge(sem("dA_cut"), 2 * i + (n + 1))
                    dve.wait_ge(sem("dbx_done"), 2 * i + (n + 1))
                    dve.wait_ge(sem("hc_read"), 2 * i + (n + 1))
                    v.tensor_tensor_scan(hs_[:, n].rearrange("p k t -> p (k t)"), dA[:, n].rearrange("p k t -> p (k t)"),
                                         dBx[:, n].rearrange("p k t -> p (k t)"), 0.0, ALU.mult, ALU.add)\
                        .then_inc(sem("scan_done"), 1)
                    dve.wait_ge(sem("scan_done"), 2 * i + (n + 1))
                    dve.sem_inc(sem("scan_credit"), 1)
            dve.wait_ge(sem("hc_read"), NS + 2)
            link(v.tensor_tensor(ys[:, :, 0:TH], PS[:, 0:2, 0:TH], zs[:, :, 0:TH], ALU.mult))
            v.tensor_tensor(ys[:, :, TH:T], PS[:, 2:4, 0:TH], zs[:, :, TH:T], ALU.mult).then_inc(sem("ys_ready"), 1)
            normed_residual(3 * NT, "ln_g", "ln_b")

            layer_norm_h()
            gates("ffn1", True, True, "gate_b1")
            weights("ffn1", True, True, True)
            for j in range(NT):
                mark(v.tensor_tensor(H[:, j, :], H[:, j, :], XH[:, j, :], ALU.add))
            for j in range(NT):
                tile_in(4 * NT, j)
                join()
                mark(v.tensor_tensor(H[:, j, :], H[:, j, :], TM(j), ALU.add))
            join()

            def add_pairs(e, stats_too=False):
                for q in range(NT // 2):
                    dve.wait_ge(sem("e1_ug"), 3 * e + q + 1)
                    dve.wait_ge(sem("e1_add"), 3 * (e - 1) + q + 1) if e else None
                    hp = H[:, 2 * q:2 * q + 2, :]
                    v.tensor_tensor(hp, hp, eu[0:TT, e % 2, 2 * q:2 * q + 2, :], ALU.add).then_inc(sem("e1_add"), 1)
                    if stats_too:
                        dve.wait_ge(sem("e1_add"), 3 * e + q + 1)
                        for j in (2 * q, 2 * q + 1):
                            tile_stats(H[:, j, :], j)

            def product_norm(ready, e, bank, scale, shift, done, weight=None):
                for j in range(NT):
                    dve.wait_ge(sem(ready), 3 * e + j // 2 + 1)
                    mark(v.bn_stats(stats[:, j, :], PS[0:TT, bank + j // 2, (j % 2) * D:(j % 2 + 1) * D]))
                join()
                for j in range(NT):
                    mark(v.bn_aggr(mv[:, j, :], stats[:, j, :]))
                join()
                rsqrt(scale[:, :], mv[:, :, 1], LN_EPS)
                if weight is not None:
                    link(v.tensor_tensor(scale[:, :], scale[:, :], weight, ALU.mult))
                v.scalar_tensor_tensor(shift[:, :], mv[:, :, 0], -1.0, scale[:, :], ALU.mult, ALU.mult)\
                    .then_inc(sem(done), 1)
                dve.wait_ge(sem(done), e + 1)

            for e in range(E1 + 1):
                if e < E1:
                    product_norm("e1_z1", e, 0, r1, nmr1, "e1_r1")
                if e >= 2:
                    add_pairs(e - 2)
                if e:
                    product_norm("e1_z2", e - 1, 4, r2, nmr2, "e1_r2", comb[:, :, e - 1])
            add_pairs(E1 - 1, True)
            dve.sem_inc(sem("ffn1_out"), 1)

            layer_norm_h()
            for j in range(NT):
                mark(v.tensor_tensor(H[:, j, :], H[:, j, :], row("b_down"), ALU.add))
            for m in range(KI):
                dve.wait_ge(sem("up_read"), m + 1)
                link(v.tensor_scalar(df[:, m, :], xm[:, m, :], col("conv_w", 4 * m + 3), col("conv_b", m), ALU.mult, ALU.add))
                for back in range(1, 4):
                    xv = xm[:, m, :].rearrange("p (b l) -> p b l", l=L)[:, :, 0:L - back]
                    dv = df[:, m, :].rearrange("p (b l) -> p b l", l=L)[:, :, back:L]
                    ins = v.scalar_tensor_tensor(dv, xv, col("conv_w", 4 * m + 3 - back), dv, ALU.mult, ALU.add)
                    if back < 3:
                        link(ins)
                    else:
                        ins.then_inc(sem("conv_ready"), 1)

            def two(x):
                return x.rearrange("p (h t) -> p h t", h=2)

            for m in range(KI):
                dve.wait_ge(sem("g_ln"), 2 * m + 2)
                for g in range(2):
                    mark(v.scalar_tensor_tensor(two(ws[g]), PS[:, 2 * g:2 * g + 2, 0:TH], 0.0, two(ws[g]), ALU.min,
                                                ALU.subtract))
                join()
                v.tensor_tensor(df[:, m, :], ws[1], ws[0], ALU.subtract).then_inc(sem("diff_ready"), 1)
                dve.wait_ge(sem("sig"), 3 * m + 3)
                v.scalar_tensor_tensor(two(ws[5]), PS[:, 4:6, 0:TH], 0.5, two(ws[4]), ALU.add, ALU.max)\
                    .then_inc(sem("gates_read"), 1)
                dve.wait_ge(sem("gates_read"), m + 1)
                mark(v.tensor_tensor(ws[5], ws[5], ws[3], ALU.mult))
                mark(v.memset(ws[2].rearrange("p (b l) -> p b l", l=L)[:, :, 0:1], 0.0))
                join()
                v.tensor_tensor_scan(xm[:, m, :], ws[2], ws[5], 0.0, ALU.mult, ALU.add).then_inc(sem("scan2_done"), 1)
                dve.wait_ge(sem("scan2_done"), m + 1)
                xv = xm[:, m, :].rearrange("p (b l) -> p b l", l=L)
                link(v.scalar_tensor_tensor(df[:, m, :].rearrange("p (b l) -> p b l", l=L),
                                            ac[:, m, :].rearrange("p (b l) -> p b l", l=L), col("skip", m),
                                            xv[:, :, L - 1:L].to_broadcast([128, NB, L]), ALU.mult, ALU.add))
                v.tensor_tensor(xm[:, m, :], df[:, m, :], zz[:, m, :], ALU.mult).then_inc(sem("h2_ready"), 1)
            residual(5 * NT)
            join()
            

            layer_norm_h()
            gates("ffn2", True, False)
            places("ffn2", True)
            weights("ffn2", True, False, False)
            shared("ffn2", CS)
            side_tiles(6 * NT, 2)
            routed("ffn2")
            collect("ffn2", 2, (2, 1), True)

            layer_norm_h()
            dve.wait_ge(sem("u_psum"), 1)
            ur = PS[:, 4:6, 0:TH].rearrange("p h (b l) -> p h b l", l=L)
            ui = PS[:, 6:8, 0:TH].rearrange("p h (b l) -> p h b l", l=L)

            def tab(t):
                return t[:, None, None, :].to_broadcast([128, 2, NB // 2, L])

            def tab3(t):
                return t[:, None, :].to_broadcast([128, NB, L])

            def hb(x):
                return x.rearrange("p (h b l) -> p h b l", h=2, l=L)

            def bl(x):
                return x.rearrange("p (b l) -> p b l", l=L)

            mark(v.tensor_tensor(hb(lt[0]), ur, tab(cosg), ALU.mult))
            mark(v.tensor_tensor(hb(lt[1]), ui, tab(sing), ALU.mult))
            mark(v.tensor_tensor(hb(lt[2]), ui, tab(cosg), ALU.mult))
            mark(v.tensor_tensor(hb(lt[3]), ur, tab(sing), ALU.mult))
            join()
            mark(v.tensor_tensor(lt[4], lt[0], lt[1], ALU.add))
            mark(v.tensor_tensor(lt[5], lt[2], lt[3], ALU.subtract))
            join()
            mark(v.tensor_tensor_scan(lt[6], lam[:, :], lt[4], 0.0, ALU.mult, ALU.add))
            mark(v.tensor_tensor_scan(lt[7], lam[:, :], lt[5], 0.0, ALU.mult, ALU.add))
            join()
            mark(v.tensor_tensor(bl(lt[0]), bl(lt[6]), tab3(cosT), ALU.mult))
            mark(v.tensor_tensor(bl(lt[1]), bl(lt[7]), tab3(sinT), ALU.mult))
            mark(v.tensor_tensor(bl(lt[2]), bl(lt[6]), tab3(nsinT), ALU.mult))
            mark(v.tensor_tensor(bl(lt[3]), bl(lt[7]), tab3(cosT), ALU.mult))
            join()
            v.tensor_tensor(lt[8], lt[0], lt[1], ALU.subtract).then_inc(sem("s_ready"), 1)
            v.tensor_tensor(lt[9], lt[2], lt[3], ALU.subtract).then_inc(sem("s_ready"), 1)
            residual(7 * NT)

            layer_norm_h()
            gates("ffn3", True, True, "gate_b3")
            places("ffn3", True)
            weights("ffn3", True, True, False)
            shared("ffn3", CH2)
            side_tiles(8 * NT, 3)
            routed("ffn3")
            collect("ffn3", 2, (3, 2), None)


def kernel(**inputs):
    import concourse.bacc as bacc
    from concourse.bass_utils import run_bass_kernel_spmd

    x = {k: np.asarray(v) for k, v in inputs.items()}

    def km(w):
        k, n = w.shape
        return w.reshape(k // 128, 128, n).transpose(1, 0, 2)

    def cv(w):
        w = w.reshape(-1, 128)
        return w.T

    a = {}
    xx = x["x"]
    B_, C_, H_, W_ = xx.shape
    p = xx.reshape(B_, C_, H_ // 16, 16, W_ // 16, 16).transpose(0, 1, 2, 4, 3, 5).reshape(T, 768)
    a["patches"] = km(p.T)
    a["w_tok"] = km(x["L0_tok_W"].T)
    a["w_rnn"] = np.stack([km(x["L0_attn_" + n].T) for n in "ABC"], 1)

    def records(name, up, wd, b1=None):
        n, parts, f0 = len(wd), [], 0
        for hu, hc in zip(HU[name], HC[name]):
            for w in up:
                parts.append(w[:, :, f0:f0 + hu].reshape(n, KD, 128, hu).transpose(0, 2, 1, 3).reshape(n, 128, -1))
            d_ = np.concatenate([wd[:, f0:f0 + hu], np.zeros((n, hc * 128 - hu, D), np.float32)], 1)
            parts.append(d_.reshape(n, hc, 128, D).transpose(0, 2, 1, 3).reshape(n, 128, -1))
            if b1 is not None:
                parts.append(b1[:, f0:f0 + hu].reshape(n, hc, 128).transpose(0, 2, 1))
            f0 += hu
        return np.concatenate(parts, -1)

    def flat_record(ups, wd):
        f = wd.shape[0]
        d_ = np.concatenate([wd, np.zeros((-f % 128, D), np.float32)])
        return np.concatenate([km(w).reshape(128, -1) for w in ups] + [km(d_).reshape(128, -1)], 1)

    a["w_moe0"] = records("ffn0", [x["L0_ffn_W1"]], x["L0_ffn_W2"], x["L0_ffn_b1"])
    a["b2_moe0"] = x["L0_ffn_b2"]
    a["w_in"] = km(x["L1_attn_W_in"])
    a["w_x"] = km(x["L1_attn_W_x"])
    a["w_dt"] = km(x["L1_attn_W_dt"])
    a["w_out"] = km(x["L1_attn_W_out"])
    a["w_l1"] = np.stack([np.stack([km(x["L1_ffn_" + n][e]) for e in range(E1)], 1) for n in ("W1", "W2")], 1)
    a["be2_l1"] = np.concatenate([x["L1_ffn_be2"], np.zeros((E - E1, D), np.float32)])
    a["w_up"] = km(x["L2_attn_w_up"].T)
    g = np.zeros((3, KI, 32, 4, 32, 4), np.float32)
    for n, name in enumerate(("w_f", "w_i", "w_h")):
        w = x["L2_attn_" + name].reshape(KI, 32, 4, 4)
        for r in range(32):
            g[n, :, r, :, r, :] = w[:, r].transpose(0, 2, 1)
    a["w_gates"] = g.reshape(3, KI, 128, 128).transpose(2, 0, 1, 3)
    a["w_down"] = km(x["L2_attn_w_down"].T)

    a["w_moe2"] = records("ffn2", [x["L2_ffn_w1"], x["L2_ffn_w3"]], x["L2_ffn_w2"])
    a["w_sh2"] = flat_record([x["L2_ffn_sw1"], x["L2_ffn_sw3"]], x["L2_ffn_sw2"])
    a["w_lru"] = np.stack([km(x["L3_attn_B_re"].T).reshape(128, D), km(x["L3_attn_B_im"].T).reshape(128, D),
                           x["L3_attn_C_re"].T, x["L3_attn_C_im"].T, *km(x["L3_attn_D"].T).transpose(1, 0, 2)], 1)
    tr = lambda w: w.transpose(0, 2, 1)
    a["w_moe3"] = records("ffn3", [tr(x["L3_ffn_rg"]), tr(x["L3_ffn_ru"])], tr(x["L3_ffn_rd"]))
    a["w_sh3"] = flat_record([x["L3_ffn_sg"].T, x["L3_ffn_su"].T], x["L3_ffn_sd"].T)
    zpad = lambda w: np.concatenate([w, np.zeros((D, E - w.shape[1]), np.float32)], 1)
    a["gate_w"] = np.stack([km(zpad(w)) for w in (x["L0_ffn_gate_w"].T, x["L1_ffn_gate_W"], x["L2_ffn_gate_w"].T,
                                                  x["L3_ffn_wr"].T)], 1)
    al = x["L1_attn_A_log"].reshape(KD, 128, NS).transpose(1, 0, 2).reshape(128, KD * NS)
    cw = x["L2_attn_conv_w"].reshape(KI, 128, 4).transpose(1, 0, 2).reshape(128, 4 * KI)
    a["cols"] = np.concatenate([cv(x["L0_ffn_rms_w"]), cv(x["L1_attn_b_dt"]), cv(x["L1_attn_D_param"]),
                                al, cv(x["L1_ffn_g1"]), cv(x["L1_ffn_be1"]), cw, cv(x["L2_attn_conv_b"]),
                                cv(x["L2_attn_skip"]), cv(x["L2_attn_b_up"]), cv(x["L3_attn_nu_log"]),
                                cv(x["L3_attn_theta_log"]), cv(x["L3_attn_gamma_log"])], 1)
    pad = lambda w: np.concatenate([w, np.full(E - len(w), NEG, np.float32)])
    a["rows"] = np.concatenate([x["L0_tok_b"], x["L0_attn_gamma"], x["L0_attn_beta"], x["L1_attn_ln_g"], x["L1_attn_ln_b"],
                                x["L2_attn_b_down"], x["L1_ffn_g2"].ravel(), pad(x["L1_ffn_gate_b"]),
                                pad(x["L3_ffn_rb"]), x["L1_ffn_b1"].ravel(), x["L1_ffn_b2"].ravel()])[None]
    a["ident_in"] = np.eye(128, dtype=np.float32)
    s = np.zeros((TT, 3, TT), np.float32)
    s[:, 0] = np.triu(np.ones((TT, TT)), 1)
    s[:, 1] = 1
    s[:, 2, :E * NT] = np.arange(E * NT) % NT != 0
    a["tri_in"] = s
    a = {k: np.ascontiguousarray(w, dtype=np.float32) for k, w in a.items()}

    nc = bacc.Bacc("TRN2", target_bir_lowering=False, num_devices=1)
    args = {k: nc.dram_tensor(k, w.shape, F32, kind="ExternalInput").ap() for k, w in a.items()}
    out = nc.dram_tensor("out", (NB, L, D), F32, kind="ExternalOutput").ap()
    bc_scratch = nc.dram_tensor("bc_scratch", (2 * NS, T), F32, kind="Internal").ap()
    x_slots = nc.dram_tensor("x_slots", (MAXB * SB, D), F32, kind="Internal").ap()
    y_slots = nc.dram_tensor("y_slots", (MAXB * SB, D), F32, kind="Internal").ap()
    tower(nc, **args, out=out, bc_scratch=bc_scratch, x_slots=x_slots, y_slots=y_slots)
    r = run_bass_kernel_spmd(nc, [a], core_ids=[0])
    return r.results[0]["out"]
```

```python
from contextlib import ExitStack

import numpy as np

import concourse.bass as bass
from concourse import mybir

F32 = mybir.dt.float32
BF16 = mybir.dt.bfloat16
I32 = mybir.dt.int32
U32 = mybir.dt.uint32
ALU = mybir.AluOpType
ACT = mybir.ActivationFunctionType
AX = mybir.AxisListType

NB, L = 16, 36
T = NB * L
D = 256
KD = D // 128
TT = 96
NT = T // TT
TH = T // 2
E = 8
F0 = 1024
E1 = 4
NS = 16
INNER = 512
KI = INNER // 128
F2 = 704
CH2 = 6
FS = 384
CS = FS // 128
PATCH_K = 768 // 128
NEG = -3.0e38
SB = 128
NBLK = {"ffn0": (T + E * (SB - 1)) // SB, "ffn2": (2 * T + E * (SB - 1)) // SB, "ffn3": (2 * T + (E - 1) * (SB - 1)) // SB}
MAXB = max(NBLK.values())
NEXP = {"ffn0": E, "ffn2": E, "ffn3": E - 1}
HU = {"ffn0": (F0 // 2, F0 // 2), "ffn2": (3 * 128, F2 - 3 * 128), "ffn3": (3 * 128, F2 - 3 * 128)}
HC = {n: tuple((hu + 127) // 128 for hu in v) for n, v in HU.items()}
HLEN = {n: tuple((1 if n == "ffn0" else 2) * KD * HU[n][x] + HC[n][x] * D + (HC[n][x] if n == "ffn0" else 0)
                 for x in range(2)) for n in NBLK}
WLEN = max(sum(v) for v in HLEN.values())
SH2 = 2 * KD * FS + CS * D
TWO_PI_HI = 6.28125
TWO_PI_LO = float(2 * np.pi - 6.28125)
ROUND_MAGIC = 12582912.0
LN_EPS, RMS_EPS = 1e-5, 1e-6

COL = {}
_n = 0
for _name, _w in [("rms_w", KD), ("b_dt", KD), ("D_param", KD), ("A_log", KD * NS), ("g1", E1 * KD),
                  ("be1", E1 * KD), ("conv_w", 4 * KI), ("conv_b", KI), ("skip", KI), ("b_up", 2 * KI), ("nu", 1),
                  ("theta", 1), ("gamma", 1)]:
    COL[_name] = _n
    _n += _w
NCOL = _n
ROW = {}
_n = 0
for _name, _w in [("tok_b", D), ("gamma", D), ("beta", D), ("ln_g", D), ("ln_b", D), ("b_down", D), ("g2", E1 * D),
                  ("gate_b1", E), ("gate_b3", E), ("b1", E1 * D), ("b2", E1 * D)]:
    ROW[_name] = _n
    _n += _w
NROW_BC = ROW["b1"]
NROW = _n
SUB = {"attn0": 0, "ffn0": 1, "attn1": 2, "ffn1": 3, "attn2": 4, "ffn2": 5, "attn3": 6, "ffn3": 7}
GATES = {"ffn0": 0, "ffn1": 1, "ffn2": 2, "ffn3": 3}


def tower(nc, patches, w_tok, w_rnn, w_moe0, b2_moe0, w_in, w_x, w_dt, w_out, w_l1, be2_l1, w_up, w_gates, w_down,
          w_moe2, w_sh2, w_lru, w_moe3, w_sh3, gate_w, cols, rows, ident_in, tri_in, out, bc_scratch,
          x_slots, y_slots):
    ctx = ExitStack()
    with ctx:
        def sb(name, shape, dt=F32):
            return ctx.enter_context(nc.sbuf_tensor(name, shape, dt))

        sems = {}

        def sem(name):
            if name not in sems:
                sems[name] = ctx.enter_context(nc.semaphore(name))
            return sems[name]

        PS = ctx.enter_context(nc.psum_tensor("PS", [128, 8, 512], F32))

        def CM(d, h):
            return PS[:, 2 * h + d, 0:TH]

        def TM(j, n=1):
            return PS[0:TT, 4 + j // 2, (j % 2) * D:(j % 2 + n) * D]

        H = sb("H", [TT, NT, D])
        XH = sb("XH", [TT, NT, D])
        XT = sb("XT", [128, KD, T])
        TMP = sb("TMP", [TT, NT, D])
        YT = sb("YT", [128, KD, T])
        ident = sb("ident", [128, 128])
        tri = sb("tri", [TT, 3, TT])
        colv = sb("colv", [128, NCOL])
        rowv = sb("rowv", [TT, NROW_BC])
        bias_p = sb("bias_p", [3, NROW - NROW_BC], BF16)
        ones3 = sb("ones3", [3, TT], BF16)
        gatew = sb("gatew", [128, 4, KD, E])
        stats = sb("stats", [TT, NT, 6])
        mv = sb("mv", [TT, NT, 2])
        rs = sb("rs", [TT, NT, 6])
        dev = sb("dev", [TT, NT])
        wrnn_s = sb("wrnn_s", [128, 3, KD, D])
        win_s = sb("win_s", [128, KD, 2 * D])
        wx_s = sb("wx_s", [128, KD, D + 2 * NS])
        wdt_s = sb("wdt_s", [128, KD, D])
        wout_s = sb("wout_s", [128, KD, D])
        wl1_s = sb("wl1_s", [128, 2, E1, KD, D])
        be2_s = sb("be2_s", [E, D])
        b20_s = sb("b20_s", [E, D])
        wlru_s = sb("wlru_s", [128, 4, D])
        wlruD_s = sb("wlruD_s", [128, KD, D])
        combT = sb("combT", [E, T])
        comb = sb("comb", [TT, NT, E])
        gl = sb("gl", [TT, NT, E])
        gm = sb("gm", [TT, NT, 8])
        gi = sb("gi", [TT, NT, 8], U32)
        gf = sb("gf", [TT, NT, 8])
        ge = sb("ge", [TT, NT, E])
        gk = sb("gk", [TT, NT, E])
        gs = sb("gs", [TT, NT])
        iota8 = sb("iota8", [TT, E], I32)
        iota8f = sb("iota8f", [TT, E])
        ARENA = 22500
        arena = sb("arena", [128, ARENA])
        o = 0

        def take(*shape):
            nonlocal o
            o += int(np.prod(shape))
            return part(o - int(np.prod(shape)), *shape)

        def part(at, *shape):
            n = int(np.prod(shape))
            assert at + n <= ARENA, (at + n, ARENA)
            names = "abc"[:len(shape)]
            if len(shape) == 1:
                return arena[:, at:at + n]
            return arena[:, at:at + n].rearrange(f"p ({' '.join(names)}) -> p {' '.join(names)}",
                                                 **dict(zip(names, shape)))

        wbuf = [take(WLEN) for _ in range(2)]
        xslot = [take(D) for _ in range(2)]
        xbT = [take(KD, SB) for _ in range(2)]
        sg_s = [take(512) for _ in range(2)]
        hid_b = [take(512) for _ in range(2)]
        y_s = [take(D) for _ in range(2)]
        sact = take(2, TH)
        shid = take(2, TH)
        Yg = take(2, NT * D)
        assert o <= ARENA, o
        wsh = sb("wsh", [128, sum(HLEN["ffn2"])])
        msk = sb("msk", [TT, 2, E, NT])
        mks = sb("mks", [TT, E, NT])
        cnt = sb("cnt", [TT, E, NT])
        pre = sb("pre", [TT, E, NT])
        posf = sb("posf", [TT, 2, E, NT])
        pos = sb("pos", [TT, 2, NT])
        posu = sb("posu", [TT, 2, NT], U32)
        nblk = sb("nblk", [TT, 3, E])
        wgt = sb("wgt", [TT, 2, NT])
        eid_f = sb("eid_f", [1, MAXB, E])
        eid_s = sb("eid_s", [1, MAXB])
        eid = sb("eid", [1, MAXB], I32)
        iob = sb("iob", [1, MAXB], I32)
        iobf = sb("iobf", [1, MAXB])
        zrow = sb("zrow", [128, D])
        patch_s = part(0, PATCH_K, T)
        wtok_s = part(PATCH_K * T, PATCH_K, D)
        HN = part(PATCH_K * (T + D), KD, T)
        o_ = PATCH_K * (T + D) + KD * T
        A_p = part(o_, 3 * KD * D // 2).bitcast(BF16).rearrange("p (i k d) -> p i k d", i=3, k=KD)
        A_rest = part(o_ + 3 * KD * D // 2, KD, D)
        h_p = part(o_ + 5 * KD * D // 2, 3 * KD * NB // 2).bitcast(BF16).rearrange("p (i k b l) -> p i k b l", i=3, k=KD, l=1)
        h_rest = part(o_ + 5 * KD * D // 2 + 3 * KD * NB // 2, KD, NB)
        bias_f = [part(PATCH_K * (T + D) + (KD + 4 + 4 * i) * T, NROW - NROW_BC)[0:3] for i in range(4)]
        U1 = KD * T
        xs, zs, dr, dl, dx, ys = (part(i * U1, KD, T) for i in range(6))
        dA = part(6 * U1, 2, KD, T)
        dBx = part(8 * U1, 2, KD, T)
        hs_ = part(10 * U1, 2, KD, T)
        hC = part(12 * U1, 2, KD, T)
        bcB = part(14 * U1, 4, T)
        bcC = part(16 * U1, 4, T)
        bc_s = part(18 * U1, T)
        A_s = part(18 * U1 + T, KD, NS)
        diagD = part(18 * U1 + T + KD * NS, KD, 128)
        n1 = part(0, NT, D)
        n1T = part(NT * D, KD, T)
        eu = part(NT * D + KD * T, 2, NT, D)
        r1, nmr1, r2, nmr2 = (sb(n, [TT, NT]) for n in ("r1", "nmr1", "r2", "nmr2"))
        U2 = KI * T
        wup_s = part(0, KD, 2 * INNER)
        wg_s = part(2 * 2 * INNER, 3, KI, 128)
        wdn_s = part(2 * 2 * INNER + 3 * KI * 128, KI, D)
        o2 = 2 * 2 * INNER + 3 * KI * 128 + KI * D
        xm = part(o2, KI, T)
        zz = part(o2 + U2, KI, T)
        ac = part(o2 + 2 * U2, KI, T)
        df = part(o2 + 3 * U2, KI, T)
        hsig = part(o2 + 4 * U2, KI, T)
        fi = part(o2 + 5 * U2, KI, 2, T)
        cosT, sinT, ncosg, cosg, sing = (sb(n, [128, L]) for n in ("cosT", "sinT", "nsinT", "cosg", "sing"))
        nsinT = ncosg
        lam = sb("lam", [128, T])
        lru_c = sb("lru_c", [128, 12])
        lt = [part(i * T, T) for i in range(10)]

        block = ctx.enter_context(nc.Block())

        STAGE = {"ffn0": 0, "ffn2": 1, "ffn3": 2}
        BLK0, USE0 = {}, {}
        n_, u_ = 0, [0, 0]
        for name in STAGE:
            BLK0[name], USE0[name] = n_, tuple(u_)
            n_ += NBLK[name]
            u_ = [u_[0] + (NBLK[name] + 1) // 2, u_[1] + NBLK[name] // 2]
        ALLB, ALLU = n_, u_
        SHN = {"ffn2": 0, "ffn3": 2 * CS}
        SCAT = [NT, 3 * NT, 5 * NT]

        def over_blocks(eng, nb, emit):
            emit(0, 0, 0)
            with eng.Fori(0, (nb - 1) // 2) as i:
                emit(2 * i + 1, i, 1)
                emit(2 * i + 2, i + 1, 0)
            if nb % 2 == 0:
                emit(nb - 1, (nb - 1) // 2, 1)

        def col(name, i=0):
            return colv[:, COL[name] + i:COL[name] + i + 1]

        def inner(x):
            return x.rearrange("p (b l) -> p b l", l=L)[:, :, 1:L]

        def row(name, w=D, i=0):
            return rowv[:, ROW[name] + i * w:ROW[name] + (i + 1) * w]

        @block.sync
        def _(sp):
            def load(dst, src, name):
                sp.dma_start(dst, src).then_inc(sem("ld_" + name), 16)

            for k in range(PATCH_K):
                load(patch_s[:, k], patches[:, k], f"patch{k}")
                load(wtok_s[:, k], w_tok[:, k], f"patch{k}")
            load(ident[:, :], ident_in, "const")
            load(tri[:, :, :], tri_in, "const")
            load(colv[:, :], cols, "const")
            load(rowv[:, :], rows[:, 0:NROW_BC].to_broadcast([TT, NROW_BC]), "const")
            load(bias_f[0], rows[:, NROW_BC:NROW].to_broadcast([3, NROW - NROW_BC]), "const")
            load(gatew[:, :, :, :], gate_w, "const")
            load(wrnn_s[:, :, :, :], w_rnn, "rnn")
            load(b20_s[:, :], b2_moe0, "rnn")
            load(win_s[:, :, :], w_in, "l1a")
            load(wx_s[:, :, :], w_x, "l1a")
            load(wdt_s[:, :, :], w_dt, "l1a")
            load(wout_s[:, :, :], w_out, "l1a")
            load(wl1_s[:, :, :, :, :], w_l1, "l1f")
            load(be2_s[:, :], be2_l1, "l1f")
            load(wsh[:, 0:SH2], w_sh2, "sh2")
            load(wlru_s[:, :, :], w_lru[:, 0:4], "lru")
            load(wlruD_s[:, :, :], w_lru[:, 4:6], "lru")

            sp.wait_ge(sem("pool_const"), 2)
            for b in range(MAXB):
                sp.dma_start(x_slots[SB * b:SB * (b + 1), :], zrow[:, :]).then_inc(sem("slots_zero"), 16)

            def expert_blocks(name, w):
                s = STAGE[name]
                nb, at = NBLK[name], BLK0[name]

                def expert_of(b):
                    return sp.value_load(eid[0:1, bass.ds(b, 1)], min_val=0, max_val=NEXP[name] - 1)

                def half(e, p, x):
                    o_ = sum(HLEN[name][:x])
                    n_ = HLEN[name][x]
                    src = w[bass.ds(e, 1), :, o_:o_ + n_].rearrange("e p n -> (e p) n")
                    sp.dma_start(wbuf[p][:, o_:o_ + n_], src).then_inc(sem(f"w{p}{x}"), 16)

                def rows_in(b, p):
                    sp.dma_start(xslot[p], x_slots[bass.ds(SB * b, SB), :]).then_inc(sem(f"x{p}"), 16)

                def rows_out(b, p):
                    sp.wait_ge(sem("y_sb"), b + (at + 1 + 2))
                    sp.dma_start(y_slots[bass.ds(SB * b, SB), :], y_s[p]).then_inc(sem(f"y{p}"), 16)

                def emit(b, hb, p, last=False):
                    if not last:
                        e = expert_of(b + 2)
                        sp.wait_ge(sem("downd"), 2 * b + (2 * at + 1))
                        rows_in(b + 2, p)
                        half(e, p, 0)
                        sp.wait_ge(sem("downd"), 2 * b + (2 * at + 2))
                        half(e, p, 1)
                    rows_out(b, p)

                sp.wait_ge(sem("eid_ready"), s + 1)
                for b in range(2):
                    e = expert_of(b)
                    for x in range(2):
                        half(e, b, x)
                sp.wait_ge(sem("scattered"), 16 * SCAT[s])
                for b in range(2):
                    rows_in(b, b)
                over_blocks(sp, nb - 2, emit)
                for b in range(nb - 2, nb):
                    emit(b, b // 2, b % 2, last=True)

            sp.wait_ge(sem("bias_ready"), 1)
            expert_blocks("ffn0", w_moe0)

            sp.wait_ge(sem("bc_rows"), 2)
            sp.dma_start(bc_scratch, bc_s[0:2 * NS, :]).then_inc(sem("bc_stored"), 16)
            sp.wait_ge(sem("bc_stored"), 16)
            for n in range(4):
                sp.dma_start(bcB[:, n], bc_scratch[n:n + 1, :].to_broadcast([128, T])).then_inc(sem(f"B{n}"), 16)
                sp.dma_start(bcC[:, n], bc_scratch[NS + n:NS + n + 1, :].to_broadcast([128, T]))\
                    .then_inc(sem(f"C{n}"), 16)
            with sp.Fori(1, NS // 4) as i:
                for n in range(4):
                    sp.wait_ge(sem("dbx_done"), 4 * i + (n - 3))
                    sp.dma_start(bcB[:, n], bc_scratch[bass.ds(4 * i + n, 1), :].to_broadcast([128, T]))\
                        .then_inc(sem(f"B{n}"), 16)
                    sp.wait_ge(sem("hc_done"), 4 * i + (n - 1))
                    sp.dma_start(bcC[:, n], bc_scratch[bass.ds(4 * i + (NS + n), 1), :].to_broadcast([128, T]))\
                        .then_inc(sem(f"C{n}"), 16)

            sp.wait_ge(sem("ffn1_out"), 1)
            load(wup_s, w_up, "l2a")
            load(wg_s, w_gates, "l2a")
            load(wdn_s, w_down, "l2a")

            expert_blocks("ffn2", w_moe2)
            load(wsh[:, :], w_sh3, "sh3")
            expert_blocks("ffn3", w_moe3)

            out_v = out.rearrange("b l d -> (b l) d").rearrange("(j p) d -> p j d", p=TT)
            for j in range(NT):
                sp.wait_ge(sem("out_tile"), j + 1)
                sp.dma_start(out_v[:, j], H[:, j]).then_inc(sem("stored"), 16)
            sp.wait_ge(sem("stored"), 16 * NT)

        @block.tensor
        def _(pe):
            def mm(out_, l, r, start=True, stop=True):
                return nc.tensor.matmul(out_, l, r, start=start, stop=stop, skip_group_check=True)

            def transpose_x(name):
                s = SUB[name]
                for j in range(NT):
                    pe.wait_ge(sem("xh_ready"), NT * s + j + 1)
                    for d in range(KD):
                        o_ = PS[:, 2 * (j // 3) + d, TT * (j % 3):TT * (j % 3 + 1)]
                        last = nc.tensor.transpose(o_, XH[:, j, 128 * d:128 * (d + 1)], ident[0:TT, 0:TT])
                    if j % 3 == 2:
                        last.then_inc(sem("xt_psum"), 1)

            def gate_logits(name):
                s = SUB[name]
                pe.wait_ge(sem("xt_ready"), 2 * s + 2)
                for j in range(NT):
                    for k in range(KD):
                        last = mm(PS[0:TT, 3, E * j:E * (j + 1)], XT[:, k, TT * j:TT * (j + 1)],
                                  gatew[:, GATES[name], k, :], k == 0, k == KD - 1)
                last.then_inc(sem("logits"), 1)

            def ranks(name):
                pe.wait_ge(sem("masks"), STAGE[name] + 1)
                mv_ = mks[:, :, :].rearrange("p e j -> p (e j)")
                mm(PS[0:TT, 3, 64:64 + E * NT], tri[:, 0, :], mv_)
                mm(PS[0:TT, 3, 128:128 + E * NT], tri[:, 1, :], mv_).then_inc(sem("ranks"), 1)

            def routed(name):
                at, nb = BLK0[name], NBLK[name]
                two_in = name != "ffn0"
                nv = 2 if two_in else 1

                def x_transposes(b, hb, p):
                    pe.wait_ge(sem(f"x{p}"), 16 * hb + 16 * (USE0[name][p] + 1))
                    for d in range(KD):
                        last = nc.tensor.transpose(PS[:, 6 + p, SB * d:SB * (d + 1)], xslot[p][:, 128 * d:128 * (d + 1)],
                                                   ident[:, :])
                    last.then_inc(sem("xt_t"), 1)

                def up(b, hb, p, x):
                    pe.wait_ge(sem(f"w{p}{x}"), 16 * hb + 16 * (USE0[name][p] + 1))
                    if x == 0:
                        pe.wait_ge(sem("xbT"), b + (at + 1))
                    w_, hu = wbuf[p][:, sum(HLEN[name][:x]):], HU[name][x]
                    full = hu // 128 * 128
                    parts_ = [(0, f, f) for f in range(0, full, 128)]
                    if full < hu:
                        parts_ += [(0, full, full)]
                    if two_in:
                        parts_ += [(1, f, 2 * hu - full + f) for f in range(0, full, 128)]
                    for v_, at_, f in parts_:
                        for k in range(KD):
                            o_ = k * nv * hu + f
                            last = mm(PS[:, 2 * x + v_, at_:at_ + SB], w_[:, o_:o_ + 128], xbT[p][:, k, :],
                                      k == 0, k == KD - 1)
                    last.then_inc(sem("upd"), 1)

                def down(b, p, x):
                    pe.wait_ge(sem("hid2"), 2 * b + (2 * at + x + 1))
                    if x == 0:
                        pe.wait_ge(sem("y_sb"), b + (at + 1))
                    o_ = sum(HLEN[name][:x]) + nv * KD * HU[name][x]
                    n_c = HC[name][x]
                    for c in range(n_c):
                        rows_ = min(128, HU[name][x] - 128 * c)
                        last = mm(PS[:, 4 + p, 0:D], hid_b[x][0:rows_, SB * c:SB * (c + 1)],
                                  wbuf[p][0:rows_, o_ + D * c:o_ + D * (c + 1)], x == 0 and c == 0, x == 1 and c == n_c - 1)
                    last.then_inc(sem("downd"), 1)

                def emit(b, hb, p, first=False, last=False):
                    up(b, hb, p, 0)
                    if not first:
                        down(b - 1, 1 - p, 1)
                    if not last:
                        x_transposes(b + 1, hb + p, 1 - p)
                    up(b, hb, p, 1)
                    down(b, p, 0)

                x_transposes(0, 0, 0)
                emit(0, 0, 0, first=True)
                with pe.Fori(0, (nb - 2) // 2) as i:
                    emit(2 * i + 1, i, 1)
                    emit(2 * i + 2, i + 1, 0)
                if nb % 2:
                    emit(nb - 2, (nb - 2) // 2, 1)
                emit(nb - 1, (nb - 1) // 2, (nb - 1) % 2, last=True)
                down(nb - 1, (nb - 1) % 2, 1)

            def residual_tiles(n_acc, halves):
                for j in range(3 * halves[0], 3 * halves[-1] + 3):
                    if j % 3 == 0:
                        pe.wait_ge(sem("yt_ready"), 2 * (n_acc - 1) + 1 + j // 3)
                    for d in range(KD):
                        last = nc.tensor.transpose(PS[0:TT, 4 + j // 2, (j % 2) * D + 128 * d:(j % 2) * D + 128 * (d + 1)],
                                                   YT[:, d, tsl(j)], ident[:, :])
                    last.then_inc(sem("tm_ready"), 1)

            def shared(name, widths, halves=(0, 1)):
                n = SHN[name]
                f = sum(widths)
                steps = len(widths)

                def up(h, c):
                    i = n + steps * h + c
                    if c >= 2 or h:
                        pe.wait_ge(sem("shid"), i - 1)
                    for v_ in range(2):
                        for k in range(KD):
                            o_ = (v_ * KD + k) * f + 128 * c
                            last = mm(PS[:, 4 + 2 * (i % 2) + v_, 0:TH], wsh[:, o_:o_ + 128], XT[:, k, hsl(h)],
                                      k == 0, k == KD - 1)
                    last.then_inc(sem("sup"), 1)

                def down(h, c):
                    i = n + steps * h + c
                    pe.wait_ge(sem("shid"), i + 1)
                    if h and c == 0:
                        pe.wait_ge(sem("yt_ready"), 2 * (STAGE[name] - 1) + 1)
                    for d in range(KD):
                        o_ = 2 * KD * f + D * c + 128 * d
                        last = mm(PS[:, d, 0:TH], wsh[0:widths[c], o_:o_ + 128], shid[0:widths[c], i % 2, :],
                                  c == 0, c == steps - 1)
                    last.then_inc(sem("sdown"), 1)

                order = [(h, c) for h in halves for c in range(steps)]
                up(*order[0])
                for a_, b_ in zip(order, order[1:] + [None]):
                    if b_:
                        up(*b_)
                    down(*a_)
                residual_tiles(STAGE[name], halves)

            def token_products(tiles_of, n_k, rhs):
                for j in range(NT):
                    for k in range(n_k):
                        last = mm(TM(j), tiles_of(k, j), rhs(k), k == 0, k == n_k - 1)
                    last.then_inc(sem("tm_ready"), 1)

            def products_by_block(n_k, wait_for, tiles_of, rhs):
                for k in range(n_k):
                    wait_for(k)
                    for j in range(NT):
                        last = mm(TM(j), tiles_of(k, j), rhs(k), k == 0 and j % 2 == 0, k == n_k - 1)
                        if k == n_k - 1:
                            last.then_inc(sem("tm_ready"), 1)

            def tsl(j):
                return slice(TT * j, TT * (j + 1))

            def hsl(h):
                return slice(TH * h, TH * (h + 1))

            products_by_block(PATCH_K, lambda k: pe.wait_ge(sem(f"ld_patch{k}"), 32),
                              lambda k, j: patch_s[:, k, tsl(j)], lambda k: wtok_s[:, k, :])

            pe.wait_ge(sem("ld_const"), 16 * 6)
            transpose_x("attn0")
            pe.wait_ge(sem("ld_rnn"), 32)
            pe.wait_ge(sem("xt_ready"), 2)
            for m in range(KD):
                for lh in range(2):
                    for k in range(KD):
                        xv = XT[:, k, :].rearrange("p (b l) -> p l b", l=L)[:, 18 * lh:18 * (lh + 1), :]
                        last = mm(PS[:, 4 + 2 * lh + m, 0:TH], wrnn_s[:, 1, k, 128 * m:128 * (m + 1)], xv, k == 0, False)
            last.then_inc(sem("rnn_x"), 1)
            HNv = HN[:, :, :].rearrange("p k (b l) -> p k b l", l=L)

            def rnn_step(lh, at, t):
                for i, (what, parts_of_a) in enumerate((("rnn_h", 3), ("rnn_h2", 2), ("rnn_h3", 1))):
                    pe.wait_ge(sem(what), t)
                    for a_ in range(parts_of_a):
                        for m in range(KD):
                            for k in range(KD):
                                last = mm(PS[:, 4 + 2 * lh + m, bass.ds(at, NB)], A_p[:, a_, k, 128 * m:128 * (m + 1)],
                                          h_p[:, i, k, :, 0], False, False)
                return last

            pe.wait_ge(sem("A_split"), 1)
            with pe.Fori(1, 18) as t:
                rnn_step(0, t * NB, t).then_inc(sem("rnn_z"), 1)
            with pe.Fori(18, 36) as t:
                rnn_step(1, t * NB - 18 * NB, t).then_inc(sem("rnn_z"), 1)
            pe.wait_ge(sem("rnn_h"), L)
            token_products(lambda k, j: HN[:, k, tsl(j)], KD, lambda k: wrnn_s[:, 2, k, :])

            transpose_x("ffn0")
            gate_logits("ffn0")
            ranks("ffn0")
            pe.wait_ge(sem("comb_ready"), 1)
            for j in range(NT):
                last = nc.tensor.transpose(PS[0:E, j // 3, TT * (j % 3):TT * (j % 3 + 1)], comb[:, j, :],
                                           ident[0:TT, 0:TT])
            last.then_inc(sem("combT_psum"), 1)
            pe.wait_ge(sem("combT_ready"), 1)
            for j in range(NT):
                mm(TM(j), combT[:, tsl(j)], b20_s[:, :]).then_inc(sem("tm_ready"), 1)
            pe.wait_ge(sem("side_added"), 1)
            routed("ffn0")

            transpose_x("attn1")
            pe.wait_ge(sem("ld_l1a"), 64)
            pe.wait_ge(sem("xt_ready"), 2 * SUB["attn1"] + 2)
            for m in range(2 * KD):
                for h in range(2):
                    for k in range(KD):
                        last = mm(PS[:, 4 + 2 * (m % 2) + h, 0:TH], win_s[:, k, 128 * m:128 * (m + 1)], XT[:, k, hsl(h)],
                                  k == 0, k == KD - 1)
                last.then_inc(sem("xz_psum"), 1)
                if m == 1:
                    pe.wait_ge(sem("xz_read"), 2)
            for h in range(2):
                for k in range(KD):
                    last = mm(PS[0:2 * NS, h, 0:TH], wx_s[:, k, D:D + 2 * NS], xs[:, k, hsl(h)], k == 0, k == KD - 1)
            last.then_inc(sem("bc_psum"), 1)
            pe.wait_ge(sem("xz_read"), 4)
            for m in range(KD):
                for h in range(2):
                    for k in range(KD):
                        last = mm(PS[:, 4 + 2 * h + m, 0:TH], wx_s[:, k, 128 * m:128 * (m + 1)], xs[:, k, hsl(h)],
                                  k == 0, k == KD - 1)
            last.then_inc(sem("dr_psum"), 1)
            pe.wait_ge(sem("dr_ready"), 2)
            for m in range(KD):
                for h in range(2):
                    for k in range(KD):
                        last = mm(PS[:, 4 + 2 * h + m, 0:TH], wdt_s[:, k, 128 * m:128 * (m + 1)], dr[:, k, hsl(h)],
                                  k == 0, k == KD - 1)
            last.then_inc(sem("dt_psum"), 1)
            pe.wait_ge(sem("bc_rows"), 2)
            pe.wait_ge(sem("diag_ready"), 1)
            for h in range(2):
                for d in range(KD):
                    mm(CM(d, h), diagD[:, d, :], xs[:, d, hsl(h)], True, False)
            pe.sem_inc(sem("hc_read"), 2)
            with pe.Fori(0, NS // 2) as i:
                for n in range(2):
                    pe.wait_ge(sem("hc_done"), 2 * i + (n + 3))
                    for h in range(2):
                        for d in range(KD):
                            last = mm(CM(d, h), ident[:, :], hC[:, n, d, hsl(h)], False, False)
                    last.then_inc(sem("hc_read"), 1)
            pe.wait_ge(sem("ys_ready"), 1)
            token_products(lambda k, j: ys[:, k, tsl(j)], KD, lambda k: wout_s[:, k, :])

            transpose_x("ffn1")
            gate_logits("ffn1")
            def first_products(e):
                for q in range(NT // 2):
                    if e:
                        pe.wait_ge(sem("e1_n1"), 3 * (e - 1) + q + 1)
                    for j in (2 * q, 2 * q + 1):
                        z = PS[0:TT, q, (j % 2) * D:(j % 2 + 1) * D]
                        mm(z, ones3[:, :], bias_p[:, e * D:(e + 1) * D], True, False)
                        for k in range(KD):
                            last = mm(z, XT[:, k, tsl(j)], wl1_s[:, 0, e, k, :], False, k == KD - 1)
                    last.then_inc(sem("e1_z1"), 1)

            def n1_transposes(e):
                for q in range(NT // 2):
                    i = 3 * e + q
                    pe.wait_ge(sem("e1_n1"), i + 1)
                    if i >= 2:
                        pe.wait_ge(sem("e1_h"), i - 1)
                    for d in range(KD):
                        for j in (2 * q, 2 * q + 1):
                            last = nc.tensor.transpose(PS[:, 3 + 4 * (i % 2), (2 * d + j % 2) * TT:(2 * d + j % 2 + 1) * TT],
                                                       n1[0:TT, j, 128 * d:128 * (d + 1)], ident[0:TT, 0:TT])
                    last.then_inc(sem("e1_t"), 1)

            def second_products(e):
                for q in range(NT // 2):
                    pe.wait_ge(sem("e1_h"), 3 * e + q + 1)
                    if e:
                        pe.wait_ge(sem("e1_u"), 3 * (e - 1) + q + 1)
                    for j in (2 * q, 2 * q + 1):
                        z = PS[0:TT, 4 + q, (j % 2) * D:(j % 2 + 1) * D]
                        mm(z, ones3[:, :], bias_p[:, (E1 + e) * D:(E1 + e + 1) * D], True, False)
                        for k in range(KD):
                            last = mm(z, n1T[:, k, tsl(j)], wl1_s[:, 1, e, k, :], False, k == KD - 1)
                    last.then_inc(sem("e1_z2"), 1)

            def second_shifts():
                pe.wait_ge(sem("comb_ready"), GATES["ffn1"] + 1)
                for j in range(NT):
                    last = nc.tensor.transpose(PS[0:E, 3 + 4 * (j // 3), TT * (j % 3):TT * (j % 3 + 1)], comb[:, j, :],
                                               ident[0:TT, 0:TT])
                last.then_inc(sem("combT_psum"), 1)
                pe.wait_ge(sem("combT_ready"), GATES["ffn1"] + 1)
                for j in range(NT):
                    mm(TM(j), combT[:, tsl(j)], be2_s[:, :]).then_inc(sem("tm_ready"), 1)

            pe.wait_ge(sem("ld_l1f"), 32)
            pe.wait_ge(sem("bias_ready"), 1)
            for e in range(E1 + 1):
                if e < E1:
                    first_products(e)
                if e == 0:
                    second_shifts()
                if e == 1:
                    pe.wait_ge(sem("be2_added"), 3)
                if e:
                    second_products(e - 1)
                if e < E1:
                    n1_transposes(e)

            transpose_x("attn2")
            pe.wait_ge(sem("ld_l2a"), 48)
            pe.wait_ge(sem("xt_ready"), 2 * SUB["attn2"] + 2)
            for m in range(2 * KI):
                if m >= 4:
                    pe.wait_ge(sem("up_read"), m - 3)
                for h in range(2):
                    for k in range(KD):
                        last = mm(PS[:, 2 * (m % 4) + h, 0:TH], wup_s[:, k, 128 * m:128 * (m + 1)], XT[:, k, hsl(h)],
                                  k == 0, k == KD - 1)
                last.then_inc(sem("up_psum"), 1)
            pe.wait_ge(sem("up_read"), 2 * KI)
            for m in range(KI):
                pe.wait_ge(sem("ac_ready"), m + 1)
                for g in (2, 0, 1):
                    if m >= 1:
                        pe.wait_ge(sem("hidden_read" if g == 2 else "gates_read"), m)
                    for h in range(2):
                        last = mm(PS[:, 2 * g + h, 0:TH], wg_s[:, g, m, :], ac[:, m, hsl(h)])
                last.then_inc(sem("gates_psum"), 1)
            products_by_block(KI, lambda k: pe.wait_ge(sem("h2_ready"), k + 1),
                              lambda k, j: xm[:, k, tsl(j)], lambda k: wdn_s[:, k, :])

            transpose_x("ffn2")
            gate_logits("ffn2")
            ranks("ffn2")
            pe.wait_ge(sem("ld_sh2"), 16)
            shared("ffn2", [128] * CS)
            pe.wait_ge(sem("side_added"), 2)
            routed("ffn2")

            transpose_x("attn3")
            pe.wait_ge(sem("ld_lru"), 32)
            pe.wait_ge(sem("xt_ready"), 2 * SUB["attn3"] + 2)
            for v in range(2):
                for h in range(2):
                    for k in range(KD):
                        last = mm(PS[:, 4 + 2 * v + h, 0:TH], wlru_s[:, v, 128 * k:128 * (k + 1)], XT[:, k, hsl(h)],
                                  k == 0, k == KD - 1)
            last.then_inc(sem("u_psum"), 1)
            pe.wait_ge(sem("s_ready"), 2)
            for j in range(NT):
                mm(TM(j), lt[8][:, tsl(j)], wlru_s[:, 2, :], True, False)
                mm(TM(j), lt[9][:, tsl(j)], wlru_s[:, 3, :], False, False)
                for k in range(KD):
                    last = mm(TM(j), XT[:, k, tsl(j)], wlruD_s[:, k, :], False, k == KD - 1)
                last.then_inc(sem("tm_ready"), 1)

            transpose_x("ffn3")
            gate_logits("ffn3")
            ranks("ffn3")
            pe.wait_ge(sem("ld_sh3"), 16)
            shared("ffn3", [128] * (CH2 - 1) + [64], (0,))
            pe.wait_ge(sem("side_added"), 3)
            routed("ffn3")
            pe.wait_ge(sem("y_sb"), ALLB + 2)
            shared("ffn3", [128] * (CH2 - 1) + [64], (1,))

        @block.scalar
        def _(act):
            roots = [0]

            def square_root(times=1):
                for _ in range(times):
                    roots[0] += 1
                    act.wait_ge(sem("var_ready"), roots[0])
                    nc.scalar.activation(dev[:, :], rs[:, :, 0], ACT.Sqrt).then_inc(sem("dev_ready"), 1)

            def xt_copy(name, scale=None, norms=1):
                square_root(norms)
                s = SUB[name]
                for h in range(2):
                    act.wait_ge(sem("xt_psum"), 2 * s + h + 1)
                    if scale is None:
                        nc.scalar.activation(XT[:, :, TH * h:TH * (h + 1)], PS[:, 2 * h:2 * h + 2, 0:TH], ACT.Copy)\
                            .then_inc(sem("xt_ready"), 1)
                    else:
                        for d in range(KD):
                            last = nc.scalar.activation(XT[:, d, TH * h:TH * (h + 1)], CM(d, h), ACT.Copy,
                                                        scale=col(scale, d))
                        last.then_inc(sem("xt_ready"), 1)

            def gate_exp(name, with_comb):
                g = GATES[name]
                act.wait_ge(sem("gate_shifted"), g + 1)
                nc.scalar.activation(ge[:, :, :], gl[:, :, :], ACT.Exp).then_inc(sem("gate_exp"), 1)
                if with_comb:
                    act.wait_ge(sem("combT_psum"), g + 1)
                    nc.scalar.activation(combT[:, :].rearrange("p (h t) -> p h t", h=2), PS[0:E, 0:2, 0:TH], ACT.Copy)\
                        .then_inc(sem("combT_ready"), 1)

            def routed(name):
                at, nb = BLK0[name], NBLK[name]
                two_in = name != "ffn0"

                def x_copy(b, p):
                    act.wait_ge(sem("xt_t"), b + (at + 1))
                    if two_in:
                        nc.scalar.activation(xbT[p], PS[:, 6 + p, 0:KD * SB].rearrange("p (k s) -> p k s", k=KD), ACT.Copy)\
                            .then_inc(sem("xbT"), 1)
                    else:
                        for d in range(KD):
                            last = nc.scalar.activation(xbT[p][:, d, :], PS[:, 6 + p, SB * d:SB * (d + 1)], ACT.Copy,
                                                        scale=col("rms_w", d))
                        last.then_inc(sem("xbT"), 1)

                def silu(b, p, x):
                    act.wait_ge(sem("upd"), 2 * b + (2 * at + x + 1))
                    if two_in:
                        nc.scalar.activation(sg_s[x][:, 0:3 * SB], PS[:, 2 * x, 0:3 * SB], ACT.Silu)\
                            .then_inc(sem("silu2"), 1)
                    else:
                        o_ = sum(HLEN[name][:x]) + HLEN[name][x] - HC[name][x]
                        for c in range(HC[name][x]):
                            last = nc.scalar.activation(hid_b[x][:, SB * c:SB * (c + 1)], PS[:, 2 * x, SB * c:SB * (c + 1)],
                                                        ACT.Silu, bias=wbuf[p][:, o_ + c:o_ + c + 1])
                        last.then_inc(sem("hid2"), 1)

                def y_copy(b, hb, p):
                    act.wait_ge(sem("downd"), 2 * b + (2 * at + 2))
                    act.wait_ge(sem(f"y{p}"), 16 * hb + 16 * (USE0[name][p] + 1))
                    nc.scalar.activation(y_s[p], PS[:, 4 + p, 0:D], ACT.Copy).then_inc(sem("y_sb"), 1)

                def emit(b, hb, p, first=False, last=False):
                    silu(b, p, 0)
                    if not first:
                        y_copy(b - 1, hb - 1 + p, 1 - p)
                    if not last:
                        x_copy(b + 1, 1 - p)
                    silu(b, p, 1)

                x_copy(0, 0)
                emit(0, 0, 0, first=True)
                with act.Fori(0, (nb - 2) // 2) as i:
                    emit(2 * i + 1, i, 1)
                    emit(2 * i + 2, i + 1, 0)
                if nb % 2:
                    emit(nb - 2, (nb - 2) // 2, 1)
                emit(nb - 1, (nb - 1) // 2, (nb - 1) % 2, last=True)
                y_copy(nb - 1, (nb - 1) // 2, (nb - 1) % 2)

            def shared(name, steps, halves=(0, 1)):
                for i in range(SHN[name] + steps * halves[0], SHN[name] + steps * (halves[-1] + 1)):
                    act.wait_ge(sem("sup"), i + 1)
                    if i >= 2:
                        act.wait_ge(sem("shid"), i - 1)
                    nc.scalar.activation(sact[:, i % 2, :], PS[:, 4 + 2 * (i % 2), 0:TH], ACT.Silu).then_inc(sem("ssilu"), 1)
                    if (i - SHN[name]) % steps == steps - 1:
                        h = (i - SHN[name]) // steps
                        act.wait_ge(sem("sdown"), i + 1)
                        nc.scalar.activation(YT[:, :, TH * h:TH * (h + 1)], PS[:, 0:2, 0:TH], ACT.Copy)\
                            .then_inc(sem("yt_ready"), 1)

            act.wait_ge(sem("ld_const"), 16 * 6)
            nc.scalar.activation(lru_c[:, 0:1], col("nu"), ACT.Exp).then_inc(sem("lru_a"), 1)
            nc.scalar.activation(lru_c[:, 2:3], col("theta"), ACT.Exp).then_inc(sem("lru_a"), 1)
            nc.scalar.activation(lru_c[:, 3:4], col("gamma"), ACT.Exp).then_inc(sem("lru_a"), 1)
            act.wait_ge(sem("lru_a"), 3)
            nc.scalar.activation(lru_c[:, 1:2], lru_c[:, 0:1], ACT.Exp, scale=-1.0).then_inc(sem("lru_b"), 1)

            xt_copy("attn0")
            HNv = HN[:, :, :].rearrange("p k (b l) -> p k b l", l=L)
            act.wait_ge(sem("rnn_x"), 1)
            nc.scalar.activation(h_p[:, 0], PS[:, 4:6, 0:NB], ACT.Tanh).then_inc(sem("rnn_h1"), 1)
            nc.scalar.activation(HNv[:, :, :, 0:1], PS[:, 4:6, 0:NB], ACT.Tanh).then_inc(sem("rnn_h"), 1)
            with act.Fori(1, 18) as t:
                act.wait_ge(sem("rnn_z"), t)
                act.wait_ge(sem("rnn_x"), 1)
                nc.scalar.activation(h_p[:, 0], PS[:, 4:6, bass.ds(t * NB, NB)], ACT.Tanh).then_inc(sem("rnn_h1"), 1)
                nc.scalar.activation(HNv[:, :, :, bass.ds(t, 1)], PS[:, 4:6, bass.ds(t * NB, NB)], ACT.Tanh)\
                    .then_inc(sem("rnn_h"), 1)
            with act.Fori(18, 36) as t:
                act.wait_ge(sem("rnn_z"), t)
                act.wait_ge(sem("rnn_x"), 1)
                nc.scalar.activation(h_p[:, 0], PS[:, 6:8, bass.ds(t * NB - 18 * NB, NB)], ACT.Tanh).then_inc(sem("rnn_h1"), 1)
                nc.scalar.activation(HNv[:, :, :, bass.ds(t, 1)], PS[:, 6:8, bass.ds(t * NB - 18 * NB, NB)], ACT.Tanh)\
                    .then_inc(sem("rnn_h"), 1)

            act.wait_ge(sem("lru_reduced"), 1)
            nc.scalar.activation(sinT[:, 1:2], lru_c[:, 6:7], ACT.Sin).then_inc(sem("lru_sc"), 1)
            nc.scalar.activation(cosT[:, 1:2], lru_c[:, 7:8], ACT.Sin).then_inc(sem("lru_sc"), 1)

            xt_copy("ffn0", "rms_w", norms=3)
            gate_exp("ffn0", True)
            act.sem_inc(sem("y_sb"), 2)
            act.sem_inc(sem("y0"), 16)
            act.sem_inc(sem("y1"), 16)
            routed("ffn0")

            xt_copy("attn1")
            for m in range(4):
                act.wait_ge(sem("xz_psum"), m + 1)
                b = 4 + 2 * (m % 2)
                dst = xs[:, m, :] if m < 2 else zs[:, m - 2, :]
                nc.scalar.activation(dst.rearrange("p (h t) -> p h t", h=2), PS[:, b:b + 2, 0:TH],
                                     ACT.Copy if m < 2 else ACT.Silu).then_inc(sem("xz_read"), 1)
            act.wait_ge(sem("bc_psum"), 1)
            for h in range(2):
                nc.scalar.activation(bc_s[0:2 * NS, TH * h:TH * (h + 1)], PS[0:2 * NS, h, 0:TH], ACT.Copy)\
                    .then_inc(sem("bc_rows"), 1)
            act.wait_ge(sem("dr_psum"), 1)
            for h in range(2):
                nc.scalar.activation(dr[:, :, TH * h:TH * (h + 1)], PS[:, 4 + 2 * h:6 + 2 * h, 0:TH], ACT.Copy)\
                    .then_inc(sem("dr_ready"), 1)
            act.wait_ge(sem("dt_psum"), 1)
            for m in range(KD):
                nc.scalar.activation(hs_[:, 1, m].rearrange("p (h t) -> p h t", h=2), PS[:, 4 + m:8:2, 0:TH], ACT.Abs,
                                     bias=col("b_dt", m)).then_inc(sem("dt_abs"), 1)
            act.wait_ge(sem("dt_abs"), KD)
            nc.scalar.activation(hs_[:, 0], hs_[:, 1], ACT.Exp, scale=-1.0).then_inc(sem("dt_e"), 1)
            act.wait_ge(sem("dt_u"), 1)
            nc.scalar.activation(dBx[:, 1], dBx[:, 0], ACT.Ln).then_inc(sem("dt_ln"), 1)
            nc.scalar.activation(A_s[:, :, :], colv[:, COL["A_log"]:COL["A_log"] + KD * NS]
                                 .rearrange("p (k n) -> p k n", k=KD), ACT.Exp).then_inc(sem("A_exp"), 1)
            act.wait_ge(sem("A_ready"), 1)
            act.wait_ge(sem("delta_ready"), 1)
            with act.Fori(0, NS // 2) as i:
                for n in range(2):
                    act.wait_ge(sem("scan_done"), 2 * i + (n + 1))
                    for d in range(KD):
                        act.wait_ge(sem("delta_ready"), 1)
                        last = nc.scalar.activation(inner(dA[:, n, d, :]), inner(dl[:, d, :]), ACT.Exp,
                                                    scale=A_s[:, d, bass.ds(2 * i + n, 1)])
                    last.then_inc(sem("dA_ready"), 1)

            xt_copy("ffn1", norms=2)
            gate_exp("ffn1", False)
            act.wait_ge(sem("combT_psum"), GATES["ffn1"] + 1)
            nc.scalar.activation(combT[:, :].rearrange("p (h t) -> p h t", h=2), PS[0:E, 3:8:4, 0:TH], ACT.Copy)\
                .then_inc(sem("combT_ready"), 1)
            for e in range(E1 + 1):
                if e < E1:
                    square_root()
                    act.wait_ge(sem("e1_r1"), e + 1)
                    for j in range(NT):
                        if e:
                            act.wait_ge(sem("e1_t"), 3 * e)
                        ins = nc.scalar.activation(n1[0:TT, j, :], PS[0:TT, j // 2, (j % 2) * D:(j % 2 + 1) * D],
                                                   ACT.Identity, bias=nmr1[:, j:j + 1], scale=r1[:, j:j + 1])
                        if j % 2:
                            ins.then_inc(sem("e1_n1"), 1)
                    for q in range(NT // 2):
                        i = 3 * e + q
                        act.wait_ge(sem("e1_t"), i + 1)
                        if e:
                            act.wait_ge(sem("e1_z2"), 3 * e)
                        for d in range(KD):
                            last = nc.scalar.activation(n1T[:, d, 2 * TT * q:2 * TT * (q + 1)],
                                                        PS[:, 3 + 4 * (i % 2), 2 * TT * d:2 * TT * (d + 1)], ACT.Relu,
                                                        bias=col("be1", e * KD + d), scale=col("g1", e * KD + d))
                        last.then_inc(sem("e1_h"), 1)
                if e:
                    f = e - 1
                    square_root()
                    act.wait_ge(sem("e1_r2"), f + 1)
                    for j in range(NT):
                        if f >= 2:
                            act.wait_ge(sem("e1_add"), 3 * (f - 2) + j // 2 + 1)
                        ins = nc.scalar.activation(eu[0:TT, f % 2, j, :], PS[0:TT, 4 + j // 2, (j % 2) * D:(j % 2 + 1) * D],
                                                   ACT.Identity, bias=nmr2[:, j:j + 1], scale=r2[:, j:j + 1])
                        if j % 2:
                            ins.then_inc(sem("e1_u"), 1)

            xt_copy("attn2")
            for m in range(2 * KI):
                act.wait_ge(sem("up_psum"), m + 1)
                b = 2 * (m % 4)
                dst = xm[:, m, :] if m < KI else zz[:, m - KI, :]
                nc.scalar.activation(dst.rearrange("p (h t) -> p h t", h=2), PS[:, b:b + 2, 0:TH],
                                     ACT.Identity if m < KI else ACT.Silu, bias=col("b_up", m)).then_inc(sem("up_read"), 1)
            for m in range(KI):
                act.wait_ge(sem("conv_ready"), m + 1)
                nc.scalar.activation(ac[:, m, :], df[:, m, :], ACT.Silu).then_inc(sem("ac_ready"), 1)

            def two(x):
                return x.rearrange("p (h t) -> p h t", h=2)

            for m in range(KI):
                act.wait_ge(sem("gates_psum"), m + 1)
                nc.scalar.activation(two(df[:, m, :]), PS[:, 4:6, 0:TH], ACT.Copy).then_inc(sem("hidden_read"), 1)
                for g in range(2):
                    nc.scalar.activation(two(fi[:, m, g]), PS[:, 2 * g:2 * g + 2, 0:TH], ACT.Abs)\
                        .then_inc(sem("g_abs"), 1)
                act.wait_ge(sem("g_abs"), 2 * m + 2)
                nc.scalar.activation(fi[:, m], fi[:, m], ACT.Exp, scale=-1.0).then_inc(sem("g_exp"), 1)
            for m in range(KI):
                act.wait_ge(sem("g_exp"), m + 1)
                nc.scalar.activation(fi[:, m], fi[:, m], ACT.Ln, bias=1.0).then_inc(sem("g_ln"), 1)
            for m in range(KI):
                act.wait_ge(sem("hidden_read"), m + 1)
                nc.scalar.activation(hsig[:, m, :], df[:, m, :], ACT.Sigmoid).then_inc(sem("sig"), 1)
                act.wait_ge(sem("diff_ready"), m + 1)
                for g, sign in ((0, 1.0), (1, -1.0)):
                    nc.scalar.activation(fi[:, m, g], xm[:, m, :], ACT.Sigmoid, scale=sign).then_inc(sem("sig"), 1)

            xt_copy("ffn2")
            gate_exp("ffn2", False)
            shared("ffn2", CS)
            routed("ffn2")
            xt_copy("attn3")
            xt_copy("ffn3")
            gate_exp("ffn3", False)
            shared("ffn3", CH2, (0,))
            routed("ffn3")
            shared("ffn3", CH2, (1,))

        @block.gpsimd
        def _(pool):
            nc.gpsimd.iota(iota8[:, :], pattern=[[1, E]], base=0, channel_multiplier=0).then_inc(sem("iota"), 1)
            nc.gpsimd.memset(ones3[:, :], 1.0).then_inc(sem("pool_const"), 1)
            nc.gpsimd.memset(zrow[:, :], 0.0).then_inc(sem("pool_const"), 1)
            nc.gpsimd.iota(iob[:, :], pattern=[[1, MAXB]], base=0, channel_multiplier=0).then_inc(sem("iota"), 1)

            pool.wait_ge(sem("ld_const"), 16 * 6)
            g = nc.gpsimd
            bf, rest, hi, mid = bias_f[0], bias_f[1], *(bias_f[i].bitcast(BF16)[:, 0:NROW - NROW_BC] for i in (2, 3))

            def step(ins, n):
                ins.then_inc(sem("bias_step"), 1)
                pool.wait_ge(sem("bias_step"), n)

            step(g.tensor_copy(hi, bf), 1)
            step(g.tensor_tensor(rest, bf, hi, ALU.subtract), 2)
            step(g.tensor_copy(mid, rest), 3)
            step(g.tensor_tensor(rest, rest, mid, ALU.subtract), 4)
            for i, src in enumerate((hi, mid, rest)):
                step(g.tensor_scalar(src, src, ident[0:3, i:i + 1], None, ALU.mult), 5 + i)
            step(g.tensor_tensor(rest, rest, mid, ALU.add), 8)
            g.tensor_tensor(bias_p[:, :], rest, hi, ALU.add).then_inc(sem("bias_ready"), 1)
            pool.wait_ge(sem("bias_ready"), 1)

            def dispatch(name, choices):
                s = STAGE[name]
                pool.wait_ge(sem("pos_ready"), s + 1)
                if s == 0:
                    pool.wait_ge(sem("slots_zero"), 16 * MAXB)
                for k in range(choices):
                    for j in range(NT):
                        pool.indirect_dma_start(x_slots, bass.IndirectOffsetOnAxis(ap=posu[:, k, j:j + 1], axis=0),
                                                XH[:, j, :], None).then_inc(sem("scattered"), 16)

            def collect(name, choices):
                s = STAGE[name]
                for p in range(2):
                    last = USE0[name][p] + (NBLK[name] + 1 - p) // 2
                    pool.wait_ge(sem(f"y{p}"), 16 * (last + 1))
                for j in range(NT):
                    for k in range(choices):
                        pool.indirect_dma_start(Yg[0:TT, k, j * D:(j + 1) * D], None, y_slots[0:SB * NBLK[name], :],
                                                bass.IndirectOffsetOnAxis(ap=posu[:, k, j:j + 1], axis=0))\
                            .then_inc(sem(f"row{k}{j}"), 16)

            dispatch("ffn0", 1)
            collect("ffn0", 1)
            pool.sem_inc(sem("hc_done"), 2)
            with pool.Fori(0, NS // 4) as i:
                for n in range(4):
                    pool.wait_ge(sem("scan_done"), 4 * i + (n + 3))
                    pool.wait_ge(sem("hc_read"), 4 * i + (n + 1))
                    pool.wait_ge(sem(f"C{n}"), 16 * i + 16)
                    nc.gpsimd.tensor_tensor(hC[:, n % 2, :, :], hs_[:, n % 2, :, :],
                                            bcC[:, n:n + 1, :].to_broadcast([128, KD, T]), ALU.mult)\
                        .then_inc(sem("hc_done"), 1)
            for e in range(E1):
                for q in range(NT // 2):
                    pool.wait_ge(sem("e1_u"), 3 * e + q + 1)
                    u = eu[0:TT, e % 2, 2 * q:2 * q + 2, :]
                    nc.gpsimd.tensor_tensor(u, u, row("g2", D, e)[:, None, :].to_broadcast([TT, 2, D]), ALU.mult)\
                        .then_inc(sem("e1_ug"), 1)
            for m in range(KI):
                pool.wait_ge(sem("g_ln"), m + 1)
                nc.gpsimd.tensor_tensor(fi[:, m, 0], fi[:, m, 0], fi[:, m, 1], ALU.subtract).then_inc(sem("ln_diff"), 1)
            for m in range(KI):
                pool.wait_ge(sem("h2_gate"), m + 1)
                nc.gpsimd.tensor_tensor(xm[:, m, :], df[:, m, :], zz[:, m, :], ALU.mult).then_inc(sem("h2_ready"), 1)
            dispatch("ffn2", 2)
            collect("ffn2", 2)
            dispatch("ffn3", 2)
            collect("ffn3", 2)

        @block.vector
        def _(dve):
            v = nc.vector
            chain = [0]

            def link(ins):
                chain[0] += 1
                ins.then_inc(sem("dve_step"), 1)
                dve.wait_ge(sem("dve_step"), chain[0])

            def mark(ins):
                chain[0] += 1
                ins.then_inc(sem("dve_step"), 1)

            def join():
                dve.wait_ge(sem("dve_step"), chain[0])

            def tile_in(before, j):
                dve.wait_ge(sem("tm_ready"), before + 2 * (j // 2) + 2)

            roots = [0]

            def rsqrt(dst, var, eps):
                x, y, a = rs[:, :, 0], rs[:, :, 1], rs[:, :, 2]
                roots[0] += 1
                v.tensor_scalar(x, var, eps, None, ALU.add).then_inc(sem("var_ready"), 1)
                dve.wait_ge(sem("dev_ready"), roots[0])
                link(v.reciprocal(y, dev[:, :]))
                link(v.tensor_tensor(a, y, y, ALU.mult))
                link(v.scalar_tensor_tensor(a, a, -0.5, x, ALU.mult, ALU.mult))
                link(v.scalar_tensor_tensor(dst, a, 1.5, y, ALU.add, ALU.mult))

            def tile_stats(src, j):
                v_in = src
                link(v.bn_stats(stats[:, j, :], v_in))
                mark(v.bn_aggr(mv[:, j, :], stats[:, j, :]))

            def all_stats(x):
                join()
                for j in range(NT):
                    mark(v.bn_stats(stats[:, j, :], x[:, j, :]))
                join()
                for j in range(NT):
                    mark(v.bn_aggr(mv[:, j, :], stats[:, j, :]))

            RSTD = rs[:, :, 3]

            def norm_to_xh():
                for j in range(NT):
                    v.tensor_scalar(XH[:, j, :], H[:, j, :], mv[:, j, 0:1], rs[:, j, 3:4], ALU.subtract, ALU.mult)\
                        .then_inc(sem("xh_ready"), 1)

            def layer_norm_h():
                join()
                rsqrt(RSTD, mv[:, :, 1], LN_EPS)
                norm_to_xh()

            def gates(name, second, over_chosen, bias=None):
                g = GATES[name]
                if g == 0:
                    dve.wait_ge(sem("iota"), 2)
                    mark(v.tensor_copy(iota8f[:, :], iota8[:, :]))
                    mark(v.tensor_copy(iobf[:, :], iob[:, :]))
                dve.wait_ge(sem("logits"), g + 1)
                lp = PS[0:TT, 3, 0:NT * E].rearrange("p (j e) -> p j e", e=E)
                if bias is None:
                    mark(v.tensor_copy(gl[:, :, :], lp))
                else:
                    mark(v.tensor_tensor(gl[:, :, :], lp, row(bias, E)[:, None, :].to_broadcast([TT, NT, E]), ALU.add))
                join()
                for j in range(NT):
                    mark(v.max(gm[:, j, :], gl[:, j, :]))
                join()
                for j in range(NT):
                    mark(v.max_index(gi[:, j, :], gm[:, j, :], gl[:, j, :]))
                join()
                v.tensor_tensor(gl[:, :, :], gl[:, :, :], gm[:, :, 0:1].to_broadcast([TT, NT, E]), ALU.subtract)\
                    .then_inc(sem("gate_shifted"), 1)
                link(v.tensor_copy(gf[:, :, :], gi[:, :, :]))
                io = iota8f[:, :, None].to_broadcast([TT, E, NT])
                for k in range(2 if second else 1):
                    mark(v.tensor_tensor(msk[:, k], io, gf[:, None, :, k].to_broadcast([TT, E, NT]), ALU.is_equal))
                join()
                if second:
                    ins = v.tensor_tensor(mks[:, :, :], msk[:, 0], msk[:, 1], ALU.add)
                else:
                    ins = v.tensor_copy(mks[:, :, :], msk[:, 0])
                if name in STAGE:
                    ins.then_inc(sem("masks"), 1)
                else:
                    link(ins)

            def weights(name, second, over_chosen, with_comb):
                g = GATES[name]
                dve.wait_ge(sem("gate_exp"), g + 1)
                if name in STAGE:
                    dve.wait_ge(sem("masks"), STAGE[name] + 1)
                mkt = mks[:, :, :].rearrange("p e j -> p j e")
                link(v.tensor_tensor(gk[:, :, :], mkt, ge[:, :, :], ALU.mult))
                link(v.tensor_reduce(gs[:, :], (gk if over_chosen else ge)[:, :, :], AX.X, ALU.add))
                link(v.reciprocal(gs[:, :], gs[:, :]))
                if with_comb:
                    v.tensor_tensor(comb[:, :, :], gk[:, :, :], gs[:, :, None].to_broadcast([TT, NT, E]), ALU.mult)\
                        .then_inc(sem("comb_ready"), 1)
                if name in STAGE:
                    if with_comb:
                        dve.wait_ge(sem("comb_ready"), g + 1)
                    for k in range(2 if second else 1):
                        link(v.tensor_tensor(gk[:, :, :], msk[:, k].rearrange("p e j -> p j e"), ge[:, :, :], ALU.mult))
                        link(v.tensor_reduce(wgt[:, k, :], gk[:, :, :], AX.X, ALU.add))
                        link(v.tensor_tensor(wgt[:, k, :], wgt[:, k, :], gs[:, :], ALU.mult))

            def places(name, second):
                s = STAGE[name]
                nk = 2 if second else 1
                dve.wait_ge(sem("ranks"), s + 1)
                ej = lambda x: x.rearrange("p (e j) -> p e j", j=NT)
                link(v.tensor_copy(cnt[:, :, :], ej(PS[0:TT, 3, 128:128 + E * NT])))
                flat = lambda x: x.rearrange("p e j -> p (e j)")
                link(v.tensor_tensor_scan(flat(pre[:, :, :]), tri[:, 2, 0:E * NT], flat(cnt[:, :, :]), 0.0, ALU.mult,
                                          ALU.add))
                n_, incl, excl = nblk[:, 0, :], nblk[:, 1, :], nblk[:, 2, :]
                link(v.tensor_scalar(n_, pre[:, :, NT - 1], 1.0 / SB, (SB - 1) / SB - 0.5 + 0.5 / SB, ALU.mult, ALU.add))
                link(v.tensor_scalar(n_, n_, ROUND_MAGIC, None, ALU.add))
                link(v.tensor_scalar(n_, n_, -ROUND_MAGIC, None, ALU.add))
                link(v.tensor_tensor_scan(incl, tri[:, 1, 0:E], n_, 0.0, ALU.mult, ALU.add))
                mark(v.tensor_tensor(eid_f[:, :, :], iobf[:, :, None].to_broadcast([1, MAXB, E]),
                                     nblk[0:1, 1:2, :].to_broadcast([1, MAXB, E]), ALU.is_ge))
                mark(v.tensor_tensor(excl, incl, n_, ALU.subtract))
                mark(v.tensor_tensor(pre[:, :, :], pre[:, :, :], cnt[:, :, :], ALU.subtract))
                join()
                mark(v.tensor_reduce(eid_s[:, :], eid_f[:, :, :], AX.X, ALU.add))
                mark(v.tensor_tensor(pre[:, :, :], pre[:, :, :], ej(PS[0:TT, 3, 64:64 + E * NT]), ALU.add))
                join()
                v.tensor_scalar(eid[:, :], eid_s[:, :], float(NEXP[name] - 1), None, ALU.min).then_inc(sem("eid_ready"), 1)
                link(v.scalar_tensor_tensor(pre[:, :, :], excl[:, :, None].to_broadcast([TT, E, NT]), float(SB),
                                            pre[:, :, :], ALU.mult, ALU.add))
                for k in range(nk):
                    mark(v.tensor_tensor(posf[:, k], msk[:, k], pre[:, :, :], ALU.mult))
                join()
                for k in range(nk):
                    mark(v.tensor_reduce(pos[:, k, :], posf[:, k].rearrange("p e j -> p j e"), AX.X, ALU.add))
                join()
                v.tensor_copy(posu[:, 0:nk, :], pos[:, 0:nk, :]).then_inc(sem("pos_ready"), 1)

            def side_tiles(tm0, n, tiles=range(NT)):
                for j in tiles:
                    if len(tiles) == NT:
                        tile_in(tm0, j)
                    else:
                        dve.wait_ge(sem("tm_ready"), tm0 + tiles[-1] + 1)
                    ins = v.tensor_tensor(H[:, j, :], H[:, j, :], TM(j), ALU.add)
                    if j < tiles[-1]:
                        mark(ins)
                    else:
                        ins.then_inc(sem("side_added"), 1)
                join()
                dve.wait_ge(sem("side_added"), n)

            def shared(name, steps, halves=(0, 1)):
                for i in range(SHN[name] + steps * halves[0], SHN[name] + steps * (halves[-1] + 1)):
                    if halves == (1,) and i > SHN[name] + steps + 1:
                        collect_tile(name, i - SHN[name] - steps - 2, 2, (3, 2))
                    dve.wait_ge(sem("sup"), i + 1)
                    dve.wait_ge(sem("ssilu"), i + 1)
                    if i >= 2:
                        dve.wait_ge(sem("sdown"), i - 1)
                    v.tensor_tensor(shid[:, i % 2, :], sact[:, i % 2, :], PS[:, 5 + 2 * (i % 2), 0:TH], ALU.mult)\
                        .then_inc(sem("shid"), 1)

            def routed(name):
                at, nb = BLK0[name], NBLK[name]

                def emit(b, hb, p):
                    for x in range(2):
                        dve.wait_ge(sem("silu2"), 2 * b + (2 * at + x + 1 - 2 * NBLK["ffn0"]))
                        full = HU[name][x] // 128 * SB
                        ins = v.tensor_tensor(hid_b[x][:, 0:full], sg_s[x][:, 0:full], PS[:, 2 * x + 1, 0:full], ALU.mult)
                        if full < 3 * SB:
                            ins = v.tensor_tensor(hid_b[x][0:64, full:3 * SB], sg_s[x][0:64, full:3 * SB],
                                                  PS[64:128, 2 * x, full:3 * SB], ALU.mult)
                        ins.then_inc(sem("hid2"), 1)

                over_blocks(dve, nb, emit)

            def collect_tile(name, j, choices, uses):
                for k in range(choices):
                    dve.wait_ge(sem(f"row{k}{j}"), 16 * uses[k])
                    link(v.scalar_tensor_tensor(H[:, j, :], Yg[0:TT, k, j * D:(j + 1) * D], wgt[:, k, j:j + 1],
                                                H[:, j, :], ALU.mult, ALU.add))

            def collect(name, choices, uses):
                for j in range(NT):
                    collect_tile(name, j, choices, uses)
                    tile_stats(H[:, j, :], j)

            dve.wait_ge(sem("ld_const"), 16 * 6)
            for j in range(NT):
                tile_in(0, j)
                mark(v.tensor_tensor(H[:, j, :], TM(j), row("tok_b"), ALU.add))
            all_stats(H)
            layer_norm_h()

            def normed_residual(tm0, scale_row, shift_row):
                for j in range(NT):
                    mark(v.tensor_tensor(H[:, j, :], H[:, j, :], row(shift_row), ALU.add))
                for q in range(NT // 2):
                    dve.wait_ge(sem("tm_ready"), tm0 + 2 * q + 2)
                    mark(v.tensor_tensor(TMP[:, 2 * q:2 * q + 2, :], TM(2 * q, 2).rearrange("p (j d) -> p j d", d=D),
                                         XH[:, 2 * q:2 * q + 2, :], ALU.add))
                all_stats(TMP)
                join()
                rsqrt(RSTD, mv[:, :, 1], LN_EPS)
                for j in range(NT):
                    mark(v.scalar_tensor_tensor(TMP[:, j, :], TMP[:, j, :], mv[:, j, 0:1], row(scale_row), ALU.subtract,
                                                ALU.mult))
                join()
                for j in range(NT):
                    mark(v.scalar_tensor_tensor(H[:, j, :], TMP[:, j, :], rs[:, j, 3:4], H[:, j, :], ALU.mult, ALU.add))
                all_stats(H)

            dve.wait_ge(sem("ld_rnn"), 32)
            link(v.tensor_copy(A_p[:, 0], wrnn_s[:, 0]))
            link(v.tensor_tensor(A_rest[:, :, :], wrnn_s[:, 0], A_p[:, 0], ALU.subtract))
            link(v.tensor_copy(A_p[:, 1], A_rest[:, :, :]))
            v.tensor_tensor(A_p[:, 2], A_rest[:, :, :], A_p[:, 1], ALU.subtract).then_inc(sem("A_split"), 1)
            HNv = HN[:, :, :].rearrange("p k (b l) -> p k b l", l=L)
            with dve.Fori(0, L - 1) as t:
                dve.wait_ge(sem("rnn_h"), t + 1)
                v.tensor_tensor(h_p[:, 1], HNv[:, :, :, bass.ds(t, 1)], h_p[:, 0], ALU.subtract).then_inc(sem("rnn_h2"), 1)
                v.tensor_tensor(h_rest[:, :, :, None], HNv[:, :, :, bass.ds(t, 1)], h_p[:, 0], ALU.subtract)\
                    .then_inc(sem("rnn_rest"), 1)
                dve.wait_ge(sem("rnn_h2"), t + 1)
                dve.wait_ge(sem("rnn_rest"), t + 1)
                v.tensor_tensor(h_p[:, 2], h_rest[:, :, :, None], h_p[:, 1], ALU.subtract).then_inc(sem("rnn_h3"), 1)

            dve.wait_ge(sem("lru_b"), 1)
            c_ = lambda i: lru_c[:, i:i + 1]
            link(v.tensor_scalar(c_(5), c_(2), float(np.pi / 2), None, ALU.add))
            link(v.tensor_copy(c_(4), c_(2)))
            link(v.tensor_scalar(lru_c[:, 8:10], lru_c[:, 4:6], float(1 / (2 * np.pi)), ROUND_MAGIC, ALU.mult, ALU.add))
            link(v.tensor_scalar(lru_c[:, 8:10], lru_c[:, 8:10], -ROUND_MAGIC, None, ALU.add))
            link(v.scalar_tensor_tensor(lru_c[:, 4:6], lru_c[:, 8:10], -TWO_PI_HI, lru_c[:, 4:6], ALU.mult, ALU.add))
            link(v.scalar_tensor_tensor(lru_c[:, 4:6], lru_c[:, 8:10], -TWO_PI_LO, lru_c[:, 4:6], ALU.mult, ALU.add))
            v.tensor_scalar(lru_c[:, 6:8], lru_c[:, 4:6], -3.1415925, 3.1415925, ALU.max, ALU.min)\
                .then_inc(sem("lru_reduced"), 1)
            normed_residual(NT, "gamma", "beta")
            join()
            rsqrt(RSTD, mv[:, :, 1], LN_EPS)
            link(v.tensor_tensor(rs[:, :, 4], RSTD, RSTD, ALU.mult))
            link(v.tensor_tensor(rs[:, :, 4], rs[:, :, 4], mv[:, :, 1], ALU.mult))
            rsqrt(rs[:, :, 5], rs[:, :, 4], RMS_EPS)
            link(v.tensor_tensor(RSTD, RSTD, rs[:, :, 5], ALU.mult))
            norm_to_xh()
            gates("ffn0", False, False)
            places("ffn0", False)
            weights("ffn0", False, False, True)
            side_tiles(2 * NT, 1)
            mark(v.memset(cosT[:, 0:1], 1.0))
            mark(v.memset(sinT[:, 0:1], 0.0))
            join()
            dve.wait_ge(sem("lru_sc"), 2)
            n = 1
            while n < L - 1:
                w = min(n, L - 1 - n)
                cr, si = cosT[:, n:n + 1], sinT[:, n:n + 1]
                C1, S1 = cosT[:, 1:1 + w], sinT[:, 1:1 + w]
                C2, S2 = cosT[:, n + 1:n + 1 + w], sinT[:, n + 1:n + 1 + w]
                mark(v.tensor_scalar(cosg[:, 0:w], S1, si, None, ALU.mult))
                mark(v.tensor_scalar(sing[:, 0:w], S1, cr, None, ALU.mult))
                join()
                mark(v.scalar_tensor_tensor(C2, C1, cr, cosg[:, 0:w], ALU.mult, ALU.subtract))
                mark(v.scalar_tensor_tensor(S2, C1, si, sing[:, 0:w], ALU.mult, ALU.add))
                join()
                n += w
            mark(v.tensor_scalar(cosg[:, :], cosT[:, :], c_(3), None, ALU.mult))
            mark(v.tensor_scalar(sing[:, :], sinT[:, :], c_(3), None, ALU.mult))
            mark(v.tensor_scalar(nsinT[:, :], sinT[:, :], -1.0, None, ALU.mult))
            link(v.memset(lam[:, :], 1.0))
            link(v.memset(lam[:, :].rearrange("p (b l) -> p b l", l=L)[:, :, 0:1], 0.0))
            link(v.tensor_scalar(lam[:, :], lam[:, :], c_(1), None, ALU.mult))

            collect("ffn0", 1, (1, 0))

            def residual(tm0):
                for q in range(NT // 2):
                    dve.wait_ge(sem("tm_ready"), tm0 + 2 * q + 2)
                    hp = H[:, 2 * q:2 * q + 2, :]
                    mark(v.tensor_tensor(hp, hp, TM(2 * q, 2).rearrange("p (j d) -> p j d", d=D), ALU.add))
                all_stats(H)

            layer_norm_h()
            for d in range(KD):
                last = v.tensor_scalar(diagD[:, d, :], ident[:, :], col("D_param", d), None, ALU.mult)
                mark(last)
            join()
            dve.sem_inc(sem("diag_ready"), 1)
            mark(v.memset(dA[:, :, :, :].rearrange("p n k (b l) -> p (n k b) l", l=L)[:, :, 0:1], 0.0))
            dve.wait_ge(sem("dt_abs"), KD)
            for m in range(KD):
                mark(v.tensor_scalar(dr[:, m, :].rearrange("p (h t) -> p h t", h=2), PS[:, 4 + m:8:2, 0:TH],
                                     col("b_dt", m), None, ALU.add))
            ee, u, ln_u = hs_[:, 0], dBx[:, 0], dBx[:, 1]
            dve.wait_ge(sem("dt_e"), 1)
            v.tensor_scalar(u, ee, 1.0, None, ALU.add).then_inc(sem("dt_u"), 1)
            dve.wait_ge(sem("dt_u"), 1)
            link(v.scalar_tensor_tensor(ee, u, 1.0, ee, ALU.subtract, ALU.subtract))
            link(v.scalar_tensor_tensor(dl[:, :, :], dr[:, :, :], 0.0, ee, ALU.max, ALU.subtract))
            dve.wait_ge(sem("dt_ln"), 1)
            link(v.scalar_tensor_tensor(ln_u, u, 1.0, ln_u, ALU.is_gt, ALU.mult))
            v.tensor_tensor(dl[:, :, :], dl[:, :, :], ln_u, ALU.add).then_inc(sem("delta_ready"), 1)
            dve.wait_ge(sem("A_exp"), 1)
            v.tensor_scalar(A_s[:, :, :], A_s[:, :, :], -1.0, None, ALU.mult).then_inc(sem("A_ready"), 1)
            dve.wait_ge(sem("delta_ready"), 1)
            link(v.tensor_tensor(dx[:, :, :], dl[:, :, :], xs[:, :, :], ALU.mult))
            dve.sem_inc(sem("scan_done"), 2)

            def input_of(i, n):
                dve.wait_ge(sem(f"B{n}"), 16 * i + 16)
                dve.wait_ge(sem("scan_done"), 4 * i + (n + 1))
                v.tensor_tensor(dBx[:, n % 2, :, :], dx[:, :, :], bcB[:, n:n + 1, :].to_broadcast([128, KD, T]), ALU.mult)\
                    .then_inc(sem("dbx_done"), 1)

            def scan(i, n):
                dve.wait_ge(sem("dA_ready"), 4 * i + (n + 1))
                dve.wait_ge(sem("dbx_done"), 4 * i + (n + 1))
                dve.wait_ge(sem("hc_done"), 4 * i + (n + 1))
                v.tensor_tensor_scan(hs_[:, n % 2].rearrange("p k t -> p (k t)"),
                                     dA[:, n % 2].rearrange("p k t -> p (k t)"),
                                     dBx[:, n % 2].rearrange("p k t -> p (k t)"), 0.0, ALU.mult, ALU.add)\
                    .then_inc(sem("scan_done"), 1)

            input_of(0, 0)
            with dve.Fori(0, NS // 4 - 1) as i:
                for n in range(4):
                    input_of(i + (n + 1) // 4, (n + 1) % 4)
                    scan(i, n)
            for n in range(4):
                if n < 3:
                    input_of(NS // 4 - 1, n + 1)
                scan(NS // 4 - 1, n)
            dve.wait_ge(sem("hc_read"), NS + 2)
            link(v.tensor_tensor(ys[:, :, 0:TH], PS[:, 0:2, 0:TH], zs[:, :, 0:TH], ALU.mult))
            v.tensor_tensor(ys[:, :, TH:T], PS[:, 2:4, 0:TH], zs[:, :, TH:T], ALU.mult).then_inc(sem("ys_ready"), 1)
            normed_residual(3 * NT, "ln_g", "ln_b")

            layer_norm_h()
            gates("ffn1", True, True, "gate_b1")
            def add_pairs(e, stats_too=False):
                for q in range(NT // 2):
                    dve.wait_ge(sem("e1_ug"), 3 * e + q + 1)
                    if e:
                        dve.wait_ge(sem("e1_add"), 3 * (e - 1) + q + 1)
                    hp = H[:, 2 * q:2 * q + 2, :]
                    v.tensor_tensor(hp, hp, eu[0:TT, e % 2, 2 * q:2 * q + 2, :], ALU.add).then_inc(sem("e1_add"), 1)
                    if stats_too:
                        dve.wait_ge(sem("e1_add"), 3 * e + q + 1)
                        for j in (2 * q, 2 * q + 1):
                            tile_stats(H[:, j, :], j)

            def product_norm(ready, e, bank, scale, shift, done, weight=None):
                for j in range(NT):
                    dve.wait_ge(sem(ready), 3 * e + j // 2 + 1)
                    mark(v.bn_stats(stats[:, j, :], PS[0:TT, bank + j // 2, (j % 2) * D:(j % 2 + 1) * D]))
                join()
                for j in range(NT):
                    mark(v.bn_aggr(mv[:, j, :], stats[:, j, :]))
                join()
                rsqrt(scale[:, :], mv[:, :, 1], LN_EPS)
                if weight is not None:
                    link(v.tensor_tensor(scale[:, :], scale[:, :], weight, ALU.mult))
                v.scalar_tensor_tensor(shift[:, :], mv[:, :, 0], -1.0, scale[:, :], ALU.mult, ALU.mult)\
                    .then_inc(sem(done), 1)
                dve.wait_ge(sem(done), e + 1)

            weights("ffn1", True, True, True)
            for e in range(E1 + 1):
                if e < E1:
                    product_norm("e1_z1", e, 0, r1, nmr1, "e1_r1")
                if e == 0:
                    for q in range(NT // 2):
                        hp = H[:, 2 * q:2 * q + 2, :]
                        mark(v.tensor_tensor(hp, hp, XH[:, 2 * q:2 * q + 2, :], ALU.add))
                    join()
                    for q in range(NT // 2):
                        dve.wait_ge(sem("tm_ready"), 4 * NT + 2 * q + 2)
                        hp = H[:, 2 * q:2 * q + 2, :]
                        v.tensor_tensor(hp, hp, TM(2 * q, 2).rearrange("p (j d) -> p j d", d=D), ALU.add)\
                            .then_inc(sem("be2_added"), 1)
                    dve.wait_ge(sem("be2_added"), 3)
                if e >= 2:
                    add_pairs(e - 2)
                if e:
                    product_norm("e1_z2", e - 1, 4, r2, nmr2, "e1_r2", comb[:, :, e - 1])
            add_pairs(E1 - 1, True)
            dve.sem_inc(sem("ffn1_out"), 1)

            layer_norm_h()
            for j in range(NT):
                mark(v.tensor_tensor(H[:, j, :], H[:, j, :], row("b_down"), ALU.add))
            for m in range(KI):
                dve.wait_ge(sem("up_read"), m + 1)
                link(v.tensor_scalar(df[:, m, :], xm[:, m, :], col("conv_w", 4 * m + 3), col("conv_b", m), ALU.mult, ALU.add))
                for back in range(1, 4):
                    xv = xm[:, m, :].rearrange("p (b l) -> p b l", l=L)[:, :, 0:L - back]
                    dv = df[:, m, :].rearrange("p (b l) -> p b l", l=L)[:, :, back:L]
                    ins = v.scalar_tensor_tensor(dv, xv, col("conv_w", 4 * m + 3 - back), dv, ALU.mult, ALU.add)
                    if back < 3:
                        link(ins)
                    else:
                        ins.then_inc(sem("conv_ready"), 1)

            def two(x):
                return x.rearrange("p (h t) -> p h t", h=2)

            for m in range(KI):
                dve.wait_ge(sem("g_abs"), 2 * m + 2)
                link(v.tensor_scalar(two(xm[:, m, :]), PS[:, 2:4, 0:TH], 0.0, None, ALU.min))
                v.scalar_tensor_tensor(two(xm[:, m, :]), PS[:, 0:2, 0:TH], 0.0, two(xm[:, m, :]), ALU.min,
                                       ALU.subtract).then_inc(sem("gates_read"), 1)
            for m in range(KI):
                dve.wait_ge(sem("ln_diff"), m + 1)
                dve.wait_ge(sem("gates_read"), m + 1)
                v.tensor_tensor(xm[:, m, :], xm[:, m, :], fi[:, m, 0], ALU.subtract).then_inc(sem("diff_ready"), 1)
            for m in range(KI):
                dve.wait_ge(sem("sig"), 3 * m + 1)
                link(v.scalar_tensor_tensor(df[:, m, :], df[:, m, :], 0.5, hsig[:, m, :], ALU.add, ALU.max))
                dve.wait_ge(sem("sig"), 3 * m + 3)
                mark(v.tensor_tensor(df[:, m, :], df[:, m, :], fi[:, m, 1], ALU.mult))
                mark(v.memset(fi[:, m, 0].rearrange("p (b l) -> p b l", l=L)[:, :, 0:1], 0.0))
                join()
                link(v.tensor_tensor_scan(xm[:, m, :], fi[:, m, 0], df[:, m, :], 0.0, ALU.mult, ALU.add))
                xv = xm[:, m, :].rearrange("p (b l) -> p b l", l=L)
                v.scalar_tensor_tensor(df[:, m, :].rearrange("p (b l) -> p b l", l=L),
                                            ac[:, m, :].rearrange("p (b l) -> p b l", l=L), col("skip", m),
                                            xv[:, :, L - 1:L].to_broadcast([128, NB, L]), ALU.mult, ALU.add)\
                    .then_inc(sem("h2_gate"), 1)
            residual(5 * NT)
            join()

            layer_norm_h()
            gates("ffn2", True, False)
            places("ffn2", True)
            weights("ffn2", True, False, False)
            shared("ffn2", CS)
            side_tiles(6 * NT, 2)
            routed("ffn2")
            collect("ffn2", 2, (2, 1))

            layer_norm_h()
            dve.wait_ge(sem("u_psum"), 1)
            ur = PS[:, 4:6, 0:TH].rearrange("p h (b l) -> p h b l", l=L)
            ui = PS[:, 6:8, 0:TH].rearrange("p h (b l) -> p h b l", l=L)

            def tab(t):
                return t[:, None, None, :].to_broadcast([128, 2, NB // 2, L])

            def tab3(t):
                return t[:, None, :].to_broadcast([128, NB, L])

            def hb(x):
                return x.rearrange("p (h b l) -> p h b l", h=2, l=L)

            def bl(x):
                return x.rearrange("p (b l) -> p b l", l=L)

            mark(v.tensor_tensor(hb(lt[0]), ur, tab(cosg), ALU.mult))
            mark(v.tensor_tensor(hb(lt[1]), ui, tab(sing), ALU.mult))
            mark(v.tensor_tensor(hb(lt[2]), ui, tab(cosg), ALU.mult))
            mark(v.tensor_tensor(hb(lt[3]), ur, tab(sing), ALU.mult))
            join()
            mark(v.tensor_tensor(lt[4], lt[0], lt[1], ALU.add))
            mark(v.tensor_tensor(lt[5], lt[2], lt[3], ALU.subtract))
            join()
            mark(v.tensor_tensor_scan(lt[6], lam[:, :], lt[4], 0.0, ALU.mult, ALU.add))
            mark(v.tensor_tensor_scan(lt[7], lam[:, :], lt[5], 0.0, ALU.mult, ALU.add))
            join()
            mark(v.tensor_tensor(bl(lt[0]), bl(lt[6]), tab3(cosT), ALU.mult))
            mark(v.tensor_tensor(bl(lt[1]), bl(lt[7]), tab3(sinT), ALU.mult))
            mark(v.tensor_tensor(bl(lt[2]), bl(lt[6]), tab3(nsinT), ALU.mult))
            mark(v.tensor_tensor(bl(lt[3]), bl(lt[7]), tab3(cosT), ALU.mult))
            join()
            v.tensor_tensor(lt[8], lt[0], lt[1], ALU.subtract).then_inc(sem("s_ready"), 1)
            v.tensor_tensor(lt[9], lt[2], lt[3], ALU.subtract).then_inc(sem("s_ready"), 1)
            residual(7 * NT)

            layer_norm_h()
            gates("ffn3", True, True, "gate_b3")
            places("ffn3", True)
            weights("ffn3", True, True, False)
            shared("ffn3", CH2, (0,))
            side_tiles(8 * NT, 3, range(0, 3))
            routed("ffn3")
            shared("ffn3", CH2, (1,))
            for j in range(CH2 - 2, NT):
                collect_tile("ffn3", j, 2, (3, 2))
            dve.sem_inc(sem("out_tile"), 3)
            for j in range(3, NT):
                dve.wait_ge(sem("tm_ready"), 9 * NT)
                v.tensor_tensor(H[:, j, :], H[:, j, :], TM(j), ALU.add).then_inc(sem("out_tile"), 1)


def kernel(**inputs):
    import concourse.bacc as bacc
    from concourse.bass_utils import run_bass_kernel_spmd

    x = {k: np.asarray(v) for k, v in inputs.items()}

    def km(w):
        k, n = w.shape
        return w.reshape(k // 128, 128, n).transpose(1, 0, 2)

    def cv(w):
        w = w.reshape(-1, 128)
        return w.T

    a = {}
    xx = x["x"]
    B_, C_, H_, W_ = xx.shape
    p = xx.reshape(B_, C_, H_ // 16, 16, W_ // 16, 16).transpose(0, 1, 2, 4, 3, 5).reshape(T, 768)
    a["patches"] = km(p.T)
    a["w_tok"] = km(x["L0_tok_W"].T)
    a["w_rnn"] = np.stack([km(x["L0_attn_" + n].T) for n in "ABC"], 1)

    def records(name, up, wd, b1=None):
        n, parts, f0 = len(wd), [], 0
        for hu, hc in zip(HU[name], HC[name]):
            w = [u[:, :, f0:f0 + hu].reshape(n, KD, 128, hu).transpose(0, 2, 1, 3) for u in up]
            full = hu // 128 * 128
            w = [w[0]] + [np.concatenate([u[..., full:], u[..., :full]], -1) for u in w[1:]]
            parts.append(np.concatenate(w, -1).reshape(n, 128, -1))
            d_ = np.concatenate([wd[:, f0:f0 + hu], np.zeros((n, hc * 128 - hu, D), np.float32)], 1)
            parts.append(d_.reshape(n, hc, 128, D).transpose(0, 2, 1, 3).reshape(n, 128, -1))
            if b1 is not None:
                parts.append(b1[:, f0:f0 + hu].reshape(n, hc, 128).transpose(0, 2, 1))
            f0 += hu
        return np.concatenate(parts, -1)

    def flat_record(ups, wd):
        f = wd.shape[0]
        d_ = np.concatenate([wd, np.zeros((-f % 128, D), np.float32)])
        return np.concatenate([km(w).reshape(128, -1) for w in ups] + [km(d_).reshape(128, -1)], 1)

    a["w_moe0"] = records("ffn0", [x["L0_ffn_W1"]], x["L0_ffn_W2"], x["L0_ffn_b1"])
    a["b2_moe0"] = x["L0_ffn_b2"]
    a["w_in"] = km(x["L1_attn_W_in"])
    a["w_x"] = km(x["L1_attn_W_x"])
    a["w_dt"] = km(x["L1_attn_W_dt"])
    a["w_out"] = km(x["L1_attn_W_out"])
    a["w_l1"] = np.stack([np.stack([km(x["L1_ffn_" + n][e]) for e in range(E1)], 1) for n in ("W1", "W2")], 1)
    a["be2_l1"] = np.concatenate([x["L1_ffn_be2"], np.zeros((E - E1, D), np.float32)])
    a["w_up"] = km(x["L2_attn_w_up"].T)
    g = np.zeros((3, KI, 32, 4, 32, 4), np.float32)
    for n, name in enumerate(("w_f", "w_i", "w_h")):
        w = x["L2_attn_" + name].reshape(KI, 32, 4, 4)
        for r in range(32):
            g[n, :, r, :, r, :] = w[:, r].transpose(0, 2, 1)
    a["w_gates"] = g.reshape(3, KI, 128, 128).transpose(2, 0, 1, 3)
    a["w_down"] = km(x["L2_attn_w_down"].T)

    a["w_moe2"] = records("ffn2", [x["L2_ffn_w1"], x["L2_ffn_w3"]], x["L2_ffn_w2"])
    a["w_sh2"] = flat_record([x["L2_ffn_sw1"], x["L2_ffn_sw3"]], x["L2_ffn_sw2"])
    a["w_lru"] = np.stack([km(x["L3_attn_B_re"].T).reshape(128, D), km(x["L3_attn_B_im"].T).reshape(128, D),
                           x["L3_attn_C_re"].T, x["L3_attn_C_im"].T, *km(x["L3_attn_D"].T).transpose(1, 0, 2)], 1)
    tr = lambda w: w.transpose(0, 2, 1)
    a["w_moe3"] = records("ffn3", [tr(x["L3_ffn_rg"]), tr(x["L3_ffn_ru"])], tr(x["L3_ffn_rd"]))
    a["w_sh3"] = flat_record([x["L3_ffn_sg"].T, x["L3_ffn_su"].T], x["L3_ffn_sd"].T)
    zpad = lambda w: np.concatenate([w, np.zeros((D, E - w.shape[1]), np.float32)], 1)
    a["gate_w"] = np.stack([km(zpad(w)) for w in (x["L0_ffn_gate_w"].T, x["L1_ffn_gate_W"], x["L2_ffn_gate_w"].T,
                                                  x["L3_ffn_wr"].T)], 1)
    al = x["L1_attn_A_log"].reshape(KD, 128, NS).transpose(1, 0, 2).reshape(128, KD * NS)
    cw = x["L2_attn_conv_w"].reshape(KI, 128, 4).transpose(1, 0, 2).reshape(128, 4 * KI)
    a["cols"] = np.concatenate([cv(x["L0_ffn_rms_w"]), cv(x["L1_attn_b_dt"]), cv(x["L1_attn_D_param"]),
                                al, cv(x["L1_ffn_g1"]), cv(x["L1_ffn_be1"]), cw, cv(x["L2_attn_conv_b"]),
                                cv(x["L2_attn_skip"]), cv(x["L2_attn_b_up"]), cv(x["L3_attn_nu_log"]),
                                cv(x["L3_attn_theta_log"]), cv(x["L3_attn_gamma_log"])], 1)
    pad = lambda w: np.concatenate([w, np.full(E - len(w), NEG, np.float32)])
    a["rows"] = np.concatenate([x["L0_tok_b"], x["L0_attn_gamma"], x["L0_attn_beta"], x["L1_attn_ln_g"], x["L1_attn_ln_b"],
                                x["L2_attn_b_down"], x["L1_ffn_g2"].ravel(), pad(x["L1_ffn_gate_b"]),
                                pad(x["L3_ffn_rb"]), x["L1_ffn_b1"].ravel(), x["L1_ffn_b2"].ravel()])[None]
    a["ident_in"] = np.eye(128, dtype=np.float32)
    s = np.zeros((TT, 3, TT), np.float32)
    s[:, 0] = np.triu(np.ones((TT, TT)), 1)
    s[:, 1] = 1
    s[:, 2, :E * NT] = np.arange(E * NT) % NT != 0
    a["tri_in"] = s
    a = {k: np.ascontiguousarray(w, dtype=np.float32) for k, w in a.items()}

    nc = bacc.Bacc("TRN2", target_bir_lowering=False, num_devices=1)
    args = {k: nc.dram_tensor(k, w.shape, F32, kind="ExternalInput").ap() for k, w in a.items()}
    out = nc.dram_tensor("out", (NB, L, D), F32, kind="ExternalOutput").ap()
    bc_scratch = nc.dram_tensor("bc_scratch", (2 * NS, T), F32, kind="Internal").ap()
    x_slots = nc.dram_tensor("x_slots", (MAXB * SB, D), F32, kind="Internal").ap()
    y_slots = nc.dram_tensor("y_slots", (MAXB * SB, D), F32, kind="Internal").ap()
    tower(nc, **args, out=out, bc_scratch=bc_scratch, x_slots=x_slots, y_slots=y_slots)
    r = run_bass_kernel_spmd(nc, [a], core_ids=[0])
    return r.results[0]["out"]
```
